# Optimizing a Trainium2 kernel written in Bass

```python
import numpy as np
import jax
import jax.numpy as jnp

def _softmax(x, axis=-1):
    return jax.nn.softmax(x, axis=axis)

def _gelu(x):
    return jax.nn.gelu(x, approximate=True)

def _silu(x):
    return jax.nn.silu(x)

def _sigmoid(x):
    return jax.nn.sigmoid(x)

def _layernorm(x, axis=-1, eps=1e-05):
    m = jnp.mean(x, axis=axis, keepdims=True)
    v = jnp.var(x, axis=axis, keepdims=True)
    return (x - m) / jnp.sqrt(v + eps)

def _scatter_add(tgt, idx, src, axis=0):
    return tgt.at[idx].add(src)

def _segment_sum(src, seg, n):
    return jax.ops.segment_sum(src, seg, n)
kernel_name = 'mk_perceiver_d2_seqx_r4_f2189a'

def setup_inputs(seed: int=0):
    np.random.seed(seed)
    _w = jnp.asarray

    def _rec_inputs():
        import jax
        import jax.numpy as jnp
        _rk = jax.random.key(seed)
        x = 7.22e-05 + 1 * jax.random.normal(jax.random.fold_in(_rk, 1), (1, 256, 256), jnp.float32)
        _lenS = 256 - jax.random.randint(jax.random.fold_in(_rk, 7), (1,), 0, max(1, 256 // 4) + 1, jnp.int32)
        _lenS2 = 4096 - jax.random.randint(jax.random.fold_in(_rk, 8), (1,), 0, max(1, 4096 // 4) + 1, jnp.int32)
        _ctx_768P = jax.random.normal(jax.random.fold_in(_rk, 11), (1, 16, 192), jnp.float32)
        _ctx_768c = jax.random.dirichlet(jax.random.fold_in(_rk, 511), 0.3 * jnp.ones((16,), jnp.float32), (1, 4096))
        _ctx_768t = jnp.einsum('bsk,bkd->bsd', _ctx_768c, _ctx_768P)
        _ctx_768t = _ctx_768t * jax.lax.rsqrt(jnp.mean(jnp.square(_ctx_768t)) + 1e-12) * 0.953939
        ctx_768 = -0.000191848 + 0.999787 * (_ctx_768t + 0.3 * jax.random.normal(jax.random.fold_in(_rk, 611), (1, 4096, 192), jnp.float32))
        _validS = jnp.arange(256)[None, :] < _lenS[:, None]
        _validS2 = jnp.arange(4096)[None, :] < _lenS2[:, None]
        _causal = jnp.tril(jnp.ones((256, 256), dtype=bool))
        mask_1x1xSxS2_bk0 = jnp.logical_not(jnp.broadcast_to(_validS2[0:1, None, None, :], (1, 1, 256, 4096)))
        return (x, ctx_768, mask_1x1xSxS2_bk0)
    x, ctx_768, mask_1x1xSxS2_bk0 = _rec_inputs()

    def _L0_xattn_setup():
        import jax, jax.numpy as jnp
        import numpy as np
        B, T, Q_DIM, KV_DIM = (4, 512, 256, 192)
        HEADS, DIM_HEAD = (16, 64)
        INNER = HEADS * DIM_HEAD
        NUM_FRAMES, NUM_PATCHES = (8, 64)
        LN_EPS = 1e-05

        def diagonal_frame_mask(num_patches, num_frames):
            fid = np.repeat(np.arange(num_frames), num_patches)
            m = fid[:, None] == fid[None, :]
            return jnp.asarray(m[None, None])
        key = jax.random.key(seed)
        ks = jax.random.split(key, 6)
        s = lambda d: 1.0 / np.sqrt(d)
        return {'x': jax.random.normal(ks[0], (B, T, Q_DIM), jnp.float32), 'context': jax.random.normal(ks[1], (B, T, KV_DIM), jnp.float32), 'ln_gamma': jnp.ones((Q_DIM,), jnp.float32), 'ln_beta': jnp.zeros((Q_DIM,), jnp.float32), 'Wq': jax.random.normal(ks[2], (Q_DIM, INNER), jnp.float32) * s(Q_DIM), 'Wkv': jax.random.normal(ks[3], (KV_DIM, 2 * INNER), jnp.float32) * s(KV_DIM), 'Wo': jax.random.normal(ks[4], (INNER, Q_DIM), jnp.float32) * s(INNER), 'bo': jnp.zeros((Q_DIM,), jnp.float32), 'mask': diagonal_frame_mask(NUM_PATCHES, NUM_FRAMES)}
    _L0_xattn_all = _L0_xattn_setup()
    _L0_xattn_in = {k: v for k, v in _L0_xattn_all.items() if k in ('ln_gamma', 'ln_beta', 'Wq', 'Wkv', 'Wo', 'bo')}
    del _L0_xattn_all

    def _L0_attn_setup():
        import math
        import jax, jax.numpy as jnp
        import numpy as np
        from jax.scipy.special import logsumexp
        B, L, D_MODEL = (2, 256, 256)
        H = 16
        DH = D_MODEL // H
        M = 24
        WINDOW = 128
        MASK_VAL = -10000.0
        EPS = 0.0001
        SCALE = 1.0 / math.sqrt(DH)

        def _sb_features(x, proj, is_query):
            xh = x * math.sqrt(SCALE)
            x_dash = jnp.einsum('bhld,md->bhlm', xh, proj)
            diag = 0.5 * jnp.sum(xh * xh, axis=-1, keepdims=True)
            log_feat = x_dash - diag
            if is_query:
                stab = jax.lax.stop_gradient(jnp.max(log_feat, axis=-1, keepdims=True))
            else:
                stab = jax.lax.stop_gradient(jnp.max(log_feat, axis=(-2, -1), keepdims=True))
            prime = jnp.exp(log_feat - stab) + EPS
            return (prime, stab)

        def _local_mask(L):
            i = jnp.arange(L)[:, None]
            j = jnp.arange(L)[None, :]
            keep = (j <= i) & (j >= i - WINDOW)
            return jnp.where(keep, 0.0, MASK_VAL).astype(jnp.float32)
        if __name__ == '__main__':
            o = reference(**setup_inputs())
            print(o.shape, o.dtype)
        key = jax.random.key(seed)
        ks = jax.random.split(key, 4)
        x = jax.random.normal(ks[0], (B, L, D_MODEL), dtype=jnp.float32)
        Wqkv_w = jax.random.normal(ks[1], (3 * D_MODEL, D_MODEL), dtype=jnp.float32) * D_MODEL ** (-0.5)
        Wqkv_b = jnp.zeros((3 * D_MODEL,), dtype=jnp.float32)
        proj = jax.random.normal(ks[2], (M, DH), dtype=jnp.float32)
        out_w = jax.random.normal(ks[3], (D_MODEL, D_MODEL), dtype=jnp.float32) * D_MODEL ** (-0.5)
        out_b = jnp.zeros((D_MODEL,), dtype=jnp.float32)
        return {'x': x, 'Wqkv_w': Wqkv_w, 'Wqkv_b': Wqkv_b, 'proj': proj, 'out_w': out_w, 'out_b': out_b}
    _L0_attn_all = _L0_attn_setup()
    _L0_attn_in = {k: v for k, v in _L0_attn_all.items() if k in ('Wqkv_w', 'Wqkv_b', 'proj', 'out_w', 'out_b')}
    del _L0_attn_all

    def _L0_ffn_setup():
        import jax, jax.numpy as jnp
        import numpy as np
        B, T, D = (2, 256, 256)
        H, DK, K = (8, 128, 8)
        NKEYS = 64
        NEXP = NKEYS * NKEYS

        def _rmsnorm(x, w, eps=1e-06):
            inv = jax.lax.rsqrt(jnp.mean(x * x, axis=-1, keepdims=True) + eps)
            return x * inv * w
        key = jax.random.key(seed)
        ks = jax.random.split(key, 5)
        return {'x': jax.random.normal(ks[0], (B, T, D), jnp.float32), 'w_q': jax.random.normal(ks[1], (H * 2 * DK, D), jnp.float32) * 0.02, 'keys': jax.random.normal(ks[2], (H, NKEYS, 2, DK), jnp.float32) * 0.02, 'expert_down': jax.random.normal(ks[3], (NEXP, D), jnp.float32) * 0.02, 'expert_up': jax.random.normal(ks[4], (NEXP, D), jnp.float32) * 0.02, 'norm_w': jnp.ones((D,), jnp.float32)}
    _L0_ffn_all = _L0_ffn_setup()
    _L0_ffn_in = {k: v for k, v in _L0_ffn_all.items() if k in ('w_q', 'keys', 'expert_down', 'expert_up', 'norm_w')}
    del _L0_ffn_all

    def _L1_xattn_setup():
        import jax, jax.numpy as jnp
        import numpy as np
        B, LQ, LK = (4, 512, 512)
        D1, D2, H = (256, 192, 256)
        key = jax.random.key(seed)
        ks = jax.random.split(key, 9)
        s1, s2, sh = (1.0 / np.sqrt(D1), 1.0 / np.sqrt(D2), 1.0 / np.sqrt(H))
        return {'query': jax.random.normal(ks[0], (B, LQ, D1), jnp.float32), 'key': jax.random.normal(ks[1], (B, LK, D2), jnp.float32), 'value': jax.random.normal(ks[2], (B, LK, D2), jnp.float32), 'Wq': jax.random.normal(ks[3], (D1, H), jnp.float32) * s1, 'bq': jax.random.normal(ks[4], (H,), jnp.float32) * s1, 'Wk': jax.random.normal(ks[5], (D2, H), jnp.float32) * s2, 'bk': jax.random.normal(ks[6], (H,), jnp.float32) * s2, 'Wv': jax.random.normal(ks[7], (D2, H), jnp.float32) * s2, 'bv': jax.random.normal(ks[8], (H,), jnp.float32) * s2}
    _L1_xattn_all = _L1_xattn_setup()
    _L1_xattn_in = {k: v for k, v in _L1_xattn_all.items() if k in ('Wq', 'bq', 'Wk', 'bk', 'Wv', 'bv')}
    del _L1_xattn_all

    def _L1_attn_setup():
        import jax, jax.numpy as jnp
        import numpy as np
        EMBED_DIM = 256
        K_DIM = 256
        MAX_SEQ_LEN = 512
        key = jax.random.key(seed)
        ks = jax.random.split(key, 9)
        s = 0.02
        x = jax.random.normal(ks[0], (4, 512, EMBED_DIM), dtype=jnp.float32)
        wq = jax.random.normal(ks[1], (EMBED_DIM, K_DIM), dtype=jnp.float32) * s
        bq = jnp.zeros((K_DIM,), dtype=jnp.float32)
        wk = jax.random.normal(ks[2], (EMBED_DIM, K_DIM), dtype=jnp.float32) * s
        bk = jnp.zeros((K_DIM,), dtype=jnp.float32)
        wv = jax.random.normal(ks[3], (EMBED_DIM, K_DIM), dtype=jnp.float32) * s
        bv = jnp.zeros((K_DIM,), dtype=jnp.float32)
        wo = jax.random.normal(ks[4], (K_DIM, EMBED_DIM), dtype=jnp.float32) * s
        bo = jnp.zeros((EMBED_DIM,), dtype=jnp.float32)
        return {'x': x, 'wq': wq, 'bq': bq, 'wk': wk, 'bk': bk, 'wv': wv, 'bv': bv, 'wo': wo, 'bo': bo}
    _L1_attn_all = _L1_attn_setup()
    _L1_attn_in = {k: v for k, v in _L1_attn_all.items() if k in ('wq', 'bq', 'wk', 'bk', 'wv', 'bv', 'wo', 'bo')}
    del _L1_attn_all

    def _L1_ffn_setup():
        import jax, jax.numpy as jnp
        import numpy as np
        TOP_K = 2
        ROUTE_SCALE = 1.0
        EPS = 1e-20
        B, S, D = (2, 128, 256)
        E = 8
        F = 192
        FS = 192 * 1
        key = jax.random.key(seed)
        ks = jax.random.split(key, 9)
        s = 0.02
        return {'hidden_states': jax.random.normal(ks[0], (B, S, D), dtype=jnp.float32), 'W_gate_router': jax.random.normal(ks[1], (D, E), dtype=jnp.float32) * s, 'expert_bias': jnp.zeros((E,), dtype=jnp.float32), 'Wg': jax.random.normal(ks[2], (E, D, F), dtype=jnp.float32) * s, 'Wu': jax.random.normal(ks[3], (E, D, F), dtype=jnp.float32) * s, 'Wd': jax.random.normal(ks[4], (E, F, D), dtype=jnp.float32) * s, 'Wg_s': jax.random.normal(ks[5], (D, FS), dtype=jnp.float32) * s, 'Wu_s': jax.random.normal(ks[6], (D, FS), dtype=jnp.float32) * s, 'Wd_s': jax.random.normal(ks[7], (FS, D), dtype=jnp.float32) * s}
    _L1_ffn_all = _L1_ffn_setup()
    _L1_ffn_in = {k: v for k, v in _L1_ffn_all.items() if k in ('W_gate_router', 'expert_bias', 'Wg', 'Wu', 'Wd', 'Wg_s', 'Wu_s', 'Wd_s')}
    del _L1_ffn_all
    return {'x': x, 'ctx_768': ctx_768, 'mask_1x1xSxS2_bk0': mask_1x1xSxS2_bk0, 'L0_xattn_ln_gamma': _L0_xattn_in['ln_gamma'], 'L0_xattn_ln_beta': _L0_xattn_in['ln_beta'], 'L0_xattn_Wq': _L0_xattn_in['Wq'], 'L0_xattn_Wkv': _L0_xattn_in['Wkv'], 'L0_xattn_Wo': _L0_xattn_in['Wo'], 'L0_xattn_bo': _L0_xattn_in['bo'], 'L0_attn_Wqkv_w': _L0_attn_in['Wqkv_w'], 'L0_attn_Wqkv_b': _L0_attn_in['Wqkv_b'], 'L0_attn_proj': _L0_attn_in['proj'], 'L0_attn_out_w': _L0_attn_in['out_w'], 'L0_attn_out_b': _L0_attn_in['out_b'], 'L0_ffn_w_q': _L0_ffn_in['w_q'], 'L0_ffn_keys': _L0_ffn_in['keys'], 'L0_ffn_expert_down': _L0_ffn_in['expert_down'], 'L0_ffn_expert_up': _L0_ffn_in['expert_up'], 'L0_ffn_norm_w': _L0_ffn_in['norm_w'], 'L1_xattn_Wq': _L1_xattn_in['Wq'], 'L1_xattn_bq': _L1_xattn_in['bq'], 'L1_xattn_Wk': _L1_xattn_in['Wk'], 'L1_xattn_bk': _L1_xattn_in['bk'], 'L1_xattn_Wv': _L1_xattn_in['Wv'], 'L1_xattn_bv': _L1_xattn_in['bv'], 'L1_attn_wq': _L1_attn_in['wq'], 'L1_attn_bq': _L1_attn_in['bq'], 'L1_attn_wk': _L1_attn_in['wk'], 'L1_attn_bk': _L1_attn_in['bk'], 'L1_attn_wv': _L1_attn_in['wv'], 'L1_attn_bv': _L1_attn_in['bv'], 'L1_attn_wo': _L1_attn_in['wo'], 'L1_attn_bo': _L1_attn_in['bo'], 'L1_ffn_W_gate_router': _L1_ffn_in['W_gate_router'], 'L1_ffn_expert_bias': _L1_ffn_in['expert_bias'], 'L1_ffn_Wg': _L1_ffn_in['Wg'], 'L1_ffn_Wu': _L1_ffn_in['Wu'], 'L1_ffn_Wd': _L1_ffn_in['Wd'], 'L1_ffn_Wg_s': _L1_ffn_in['Wg_s'], 'L1_ffn_Wu_s': _L1_ffn_in['Wu_s'], 'L1_ffn_Wd_s': _L1_ffn_in['Wd_s']}

def reference(x, ctx_768, mask_1x1xSxS2_bk0, L0_xattn_ln_gamma, L0_xattn_ln_beta, L0_xattn_Wq, L0_xattn_Wkv, L0_xattn_Wo, L0_xattn_bo, L0_attn_Wqkv_w, L0_attn_Wqkv_b, L0_attn_proj, L0_attn_out_w, L0_attn_out_b, L0_ffn_w_q, L0_ffn_keys, L0_ffn_expert_down, L0_ffn_expert_up, L0_ffn_norm_w, L1_xattn_Wq, L1_xattn_bq, L1_xattn_Wk, L1_xattn_bk, L1_xattn_Wv, L1_xattn_bv, L1_attn_wq, L1_attn_bq, L1_attn_wk, L1_attn_bk, L1_attn_wv, L1_attn_bv, L1_attn_wo, L1_attn_bo, L1_ffn_W_gate_router, L1_ffn_expert_bias, L1_ffn_Wg, L1_ffn_Wu, L1_ffn_Wd, L1_ffn_Wg_s, L1_ffn_Wu_s, L1_ffn_Wd_s):
    import jax
    import jax.numpy as jnp

    def _L0_xattn_ref(x, context, ln_gamma, ln_beta, Wq, Wkv, Wo, bo, mask):
        import jax, jax.numpy as jnp
        import numpy as np
        B, T, Q_DIM, KV_DIM = (4, 512, 256, 192)
        HEADS, DIM_HEAD = (16, 64)
        INNER = HEADS * DIM_HEAD
        NUM_FRAMES, NUM_PATCHES = (8, 64)
        LN_EPS = 1e-05

        def diagonal_frame_mask(num_patches, num_frames):
            fid = np.repeat(np.arange(num_frames), num_patches)
            m = fid[:, None] == fid[None, :]
            return jnp.asarray(m[None, None])
        mu = jnp.mean(x, axis=-1, keepdims=True)
        var = jnp.mean(jnp.square(x - mu), axis=-1, keepdims=True)
        xn = (x - mu) * jax.lax.rsqrt(var + LN_EPS) * ln_gamma + ln_beta
        scale = DIM_HEAD ** (-0.5)
        q = xn @ Wq
        kv = context @ Wkv
        k, v = jnp.split(kv, 2, axis=-1)
        split_heads = lambda t: t.reshape(t.shape[0], t.shape[1], HEADS, DIM_HEAD).transpose(0, 2, 1, 3)
        q, k, v = (split_heads(q), split_heads(k), split_heads(v))
        dots = jnp.einsum('bhnd,bhmd->bhnm', q, k) * scale
        dots = jnp.where(mask, dots, -jnp.inf)
        attn = jax.nn.softmax(dots, axis=-1)
        out = jnp.einsum('bhnm,bhmd->bhnd', attn, v)
        out = out.transpose(0, 2, 1, 3).reshape(x.shape[0], x.shape[1], INNER)
        return out @ Wo + bo

    def _L0_attn_ref(x, Wqkv_w, Wqkv_b, proj, out_w, out_b):
        import math
        import jax, jax.numpy as jnp
        import numpy as np
        from jax.scipy.special import logsumexp
        B, L, D_MODEL = (2, 256, 256)
        H = 16
        DH = D_MODEL // H
        M = 24
        WINDOW = 128
        MASK_VAL = -10000.0
        EPS = 0.0001
        SCALE = 1.0 / math.sqrt(DH)

        def _sb_features(x, proj, is_query):
            xh = x * math.sqrt(SCALE)
            x_dash = jnp.einsum('bhld,md->bhlm', xh, proj)
            diag = 0.5 * jnp.sum(xh * xh, axis=-1, keepdims=True)
            log_feat = x_dash - diag
            if is_query:
                stab = jax.lax.stop_gradient(jnp.max(log_feat, axis=-1, keepdims=True))
            else:
                stab = jax.lax.stop_gradient(jnp.max(log_feat, axis=(-2, -1), keepdims=True))
            prime = jnp.exp(log_feat - stab) + EPS
            return (prime, stab)

        def _local_mask(L):
            i = jnp.arange(L)[:, None]
            j = jnp.arange(L)[None, :]
            keep = (j <= i) & (j >= i - WINDOW)
            return jnp.where(keep, 0.0, MASK_VAL).astype(jnp.float32)
        if __name__ == '__main__':
            o = reference(**setup_inputs())
            print(o.shape, o.dtype)
        b, l, dm = x.shape
        qkv = (x @ Wqkv_w.T + Wqkv_b).reshape(b, l, 3, H, DH)
        q = jnp.transpose(qkv[:, :, 0], (0, 2, 1, 3))
        k = jnp.transpose(qkv[:, :, 1], (0, 2, 1, 3))
        v = jnp.transpose(qkv[:, :, 2], (0, 2, 1, 3))
        q_prime, q_ls = _sb_features(q, proj, is_query=True)
        k_prime, k_ls = _sb_features(k, proj, is_query=False)
        global_scale = q_ls + k_ls
        global_out_cumsum = jnp.einsum('bhnm,bhnm->bhn', q_prime, jnp.cumsum(k_prime, axis=-2))
        kv = jnp.cumsum(k_prime[..., :, :, None] * v[..., :, None, :], axis=-3)
        global_out = jnp.einsum('bhlm,bhlmd->bhld', q_prime, kv)
        mask = _local_mask(l)
        g_scores = jnp.einsum('bhmd,bhnd->bhmn', q_prime, k_prime) * SCALE + mask
        global_qk = jnp.where(g_scores <= 0, 0.0, g_scores)
        l_scores = jnp.einsum('bhmd,bhnd->bhmn', q, k) * SCALE + mask
        QK_lse = logsumexp(l_scores, axis=-1, keepdims=True)
        gqk_sum = jnp.sum(global_qk, axis=-1, keepdims=True)
        g_log_norm = jnp.log(jnp.clip(global_out_cumsum[..., None] - gqk_sum, 1e-24)) + global_scale
        log_norm = jnp.logaddexp(QK_lse, g_log_norm)
        g_prime_scale = jnp.exp(global_scale - log_norm)
        local_score = jax.nn.softmax(l_scores - log_norm, axis=-1) - global_qk * g_prime_scale
        out = jnp.einsum('bhmn,bhnd->bhmd', local_score, v) + global_out * g_prime_scale
        ctx = jnp.transpose(out, (0, 2, 1, 3)).reshape(b, l, dm)
        return ctx @ out_w.T + out_b

    def _L0_ffn_ref(x, w_q, keys, expert_down, expert_up, norm_w):
        import jax, jax.numpy as jnp
        import numpy as np
        B, T, D = (2, 256, 256)
        H, DK, K = (8, 128, 8)
        NKEYS = 64
        NEXP = NKEYS * NKEYS

        def _rmsnorm(x, w, eps=1e-06):
            inv = jax.lax.rsqrt(jnp.mean(x * x, axis=-1, keepdims=True) + eps)
            return x * inv * w
        b, t, d = x.shape
        xn = _rmsnorm(x, norm_w)
        q = (xn @ w_q.T).reshape(b, t, H, 2, DK)
        sim1 = jnp.einsum('bthd,hkd->bthk', q[..., 0, :], keys[:, :, 0, :])
        sim2 = jnp.einsum('bthd,hkd->bthk', q[..., 1, :], keys[:, :, 1, :])
        s1, i1 = jax.lax.top_k(sim1, K)
        s2, i2 = jax.lax.top_k(sim2, K)
        all_idx = (i1[..., :, None] * NKEYS + i2[..., None, :]).reshape(b, t, H, K * K)
        all_sc = (s1[..., :, None] + s2[..., None, :]).reshape(b, t, H, K * K)
        fs, pk = jax.lax.top_k(all_sc, K)
        fi = jnp.take_along_axis(all_idx, pk, axis=-1)
        wd = expert_down[fi]
        wu = expert_up[fi]
        hidden = jax.nn.gelu(jnp.einsum('btd,bthkd->bthk', xn, wd), approximate=False)
        hidden = hidden * jax.nn.relu(fs)
        return jnp.einsum('bthk,bthkd->btd', hidden, wu)

    def _L1_xattn_ref(query, key, value, Wq, bq, Wk, bk, Wv, bv):
        import jax, jax.numpy as jnp
        import numpy as np
        B, LQ, LK = (4, 512, 512)
        D1, D2, H = (256, 192, 256)
        q = jnp.einsum('bqd,dh->bqh', query, Wq) + bq
        k = jnp.einsum('bkd,dh->bkh', key, Wk) + bk
        v = jnp.einsum('bkd,dh->bkh', value, Wv) + bv
        scores = jnp.einsum('bqh,bkh->bqk', q, k)
        weights = jax.nn.softmax(scores, axis=-1)
        return jnp.einsum('bqk,bkh->bqh', weights, v)

    def _L1_attn_ref(x, wq, bq, wk, bk, wv, bv, wo, bo):
        import jax, jax.numpy as jnp
        import numpy as np
        EMBED_DIM = 256
        K_DIM = 256
        MAX_SEQ_LEN = 512
        B, S, D = x.shape
        scale = jnp.asarray(K_DIM ** 0.5, x.dtype)
        Q = x @ wq + bq
        K = x @ wk + bk
        V = x @ wv + bv
        scores = jnp.einsum('bqk,bsk->bqs', Q, K) / scale
        row = jnp.arange(S)[:, None]
        col = jnp.arange(S)[None, :]
        mask = col <= row + 1
        scores = jnp.where(mask, jnp.asarray(-1000000000.0, scores.dtype), scores)
        attn = jax.nn.softmax(scores, axis=-1)
        out = jnp.einsum('bqs,bsk->bqk', attn, V)
        return out @ wo + bo

    def _L1_ffn_ref(hidden_states, W_gate_router, expert_bias, Wg, Wu, Wd, Wg_s, Wu_s, Wd_s):
        import jax, jax.numpy as jnp
        import numpy as np
        TOP_K = 2
        ROUTE_SCALE = 1.0
        EPS = 1e-20
        B, S, D = (2, 128, 256)
        E = 8
        F = 192
        FS = 192 * 1
        b, s, d = hidden_states.shape
        x = hidden_states.reshape(-1, d)
        T = x.shape[0]
        logits = x @ W_gate_router
        scores = jax.nn.sigmoid(logits.astype(jnp.float32))
        _, sel = jax.lax.top_k(scores + expert_bias, TOP_K)
        top_scores = jnp.take_along_axis(scores, sel, axis=1)
        top_scores = top_scores / (top_scores.sum(-1, keepdims=True) + EPS)
        top_scores = top_scores * ROUTE_SCALE
        shared = jax.nn.silu(x @ Wg_s) * (x @ Wu_s) @ Wd_s
        tok = jnp.repeat(jnp.arange(T), TOP_K)
        exp = sel.reshape(-1)
        w = top_scores.reshape(-1)
        xr = x[tok]
        h = jax.nn.silu(jnp.einsum('nd,edf->enf', xr, Wg)) * jnp.einsum('nd,edf->enf', xr, Wu)
        out_all = jnp.einsum('enf,efd->end', h, Wd)
        routed = out_all[exp, jnp.arange(exp.shape[0])]
        routed = (routed.astype(jnp.float32) * w[:, None]).astype(hidden_states.dtype)
        out = shared.at[tok].add(routed)
        return out.reshape(b, s, d)
    x = x + _L0_xattn_ref(_layernorm(x, axis=-1), ctx_768, L0_xattn_ln_gamma, L0_xattn_ln_beta, L0_xattn_Wq, L0_xattn_Wkv, L0_xattn_Wo, L0_xattn_bo, mask_1x1xSxS2_bk0)
    x = x + _L0_attn_ref(_layernorm(x, axis=-1), L0_attn_Wqkv_w, L0_attn_Wqkv_b, L0_attn_proj, L0_attn_out_w, L0_attn_out_b)
    x = x + _L0_ffn_ref(_layernorm(x, axis=-1), L0_ffn_w_q, L0_ffn_keys, L0_ffn_expert_down, L0_ffn_expert_up, L0_ffn_norm_w)
    x = x + _L1_xattn_ref(_layernorm(x, axis=-1), ctx_768, ctx_768, L1_xattn_Wq, L1_xattn_bq, L1_xattn_Wk, L1_xattn_bk, L1_xattn_Wv, L1_xattn_bv)
    x = x + _L1_attn_ref(_layernorm(x, axis=-1), L1_attn_wq, L1_attn_bq, L1_attn_wk, L1_attn_bk, L1_attn_wv, L1_attn_bv, L1_attn_wo, L1_attn_bo)
    x = x + _L1_ffn_ref(_layernorm(x, axis=-1), L1_ffn_W_gate_router, L1_ffn_expert_bias, L1_ffn_Wg, L1_ffn_Wu, L1_ffn_Wd, L1_ffn_Wg_s, L1_ffn_Wu_s, L1_ffn_Wd_s)
    return x

_drawn_inputs = setup_inputs


def setup_inputs(seed=0):
    import zlib

    import numpy as np

    out = dict(_drawn_inputs(seed))
    spreads = {'L0_xattn_ln_gamma': (1.0, 0.2),
     'L0_xattn_ln_beta': (0.0, 0.1),
     'L0_xattn_bo': (0.0, 0.1),
     'L0_attn_Wqkv_b': (0.0, 0.1),
     'L0_attn_out_b': (0.0, 0.1),
     'L0_ffn_norm_w': (1.0, 0.6),
     'L1_attn_bq': (0.0, 2.0),
     'L1_attn_bk': (0.0, 2.0),
     'L1_attn_bv': (0.0, 1.831),
     'L1_attn_bo': (0.0, 0.42),
     'L1_ffn_expert_bias': (0.0, 0.8)}
    factors = {'L0_ffn_w_q': 4.946,
     'L0_ffn_keys': 5.944,
     'L0_ffn_expert_down': 5.68,
     'L0_ffn_expert_up': 4.948,
     'L1_xattn_bk': 64.0,
     'L1_attn_wq': 42.059,
     'L1_attn_wk': 42.189,
     'L1_ffn_W_gate_router': 8.0,
     'L1_ffn_Wg': 8.0,
     'L1_ffn_Wu': 8.0,
     'L1_ffn_Wd': 8.0,
     'L1_ffn_Wg_s': 8.0,
     'L1_ffn_Wu_s': 8.0,
     'L1_ffn_Wd_s': 8.0,
     'L1_xattn_bq': 2.73,
     'L1_xattn_bv': 8.0,
     'L1_attn_wv': 8.0}
    for name, (base, spread) in spreads.items():
        noise = np.random.default_rng([zlib.crc32(name.encode()), seed]).standard_normal(out[name].shape)
        drawn = base * np.exp(spread * noise) if base else spread * noise
        out[name] = jnp.asarray(drawn.astype(out[name].dtype))
    for name, factor in factors.items():
        out[name] = (out[name] * factor).astype(out[name].dtype)
    return out
```

```python
from contextlib import ExitStack

import numpy as np

import concourse.bass as bass
from concourse import mybir

ACT = mybir.ActivationFunctionType
ALU = mybir.AluOpType
AX = mybir.AxisListType
F32 = mybir.dt.float32
BF16 = mybir.dt.bfloat16
U32 = mybir.dt.uint32
I32 = mybir.dt.int32
U8 = mybir.dt.uint8

P = 128
T = 256
TT = T // P
D = 256
DC = D // P
CD = 192
S2 = 4096
BLK = 512
NBLK = S2 // BLK
KT_PER = BLK // P
XH, XD = 16, 64
MASKED = -1e30
LH, LM = 16, 24
EXPERTS = 4096
ET = EXPERTS // P
EH, NK = 8, 64
GS = 16
FF, MOE = 192, 8
FALL = (MOE + 1) * FF
FT = (FALL + P - 1) // P
UNITS = 2 * S2 // 1024


COLUMNS = ["L0_xattn_ln_gamma", "L0_xattn_ln_beta", "L0_ffn_norm_w", "L1_xattn_bq", "L1_attn_bq", "L1_attn_bk"]
EPS_OF_NORM = [1e-5] * 4 + [1e-6] + [1e-5] * 3
ROWS = ["L0_xattn_bo", "L0_attn_v_b", "L0_attn_out_b", "L1_attn_bv", "L1_attn_bo"]


class Chain:

    def __init__(self, eng, sem):
        self.eng, self.sem, self.n = eng, sem, 0

    def __call__(self, ins):
        self.n += 1
        ins.then_inc(self.sem, 1)
        self.eng.wait_ge(self.sem, self.n)


def build(nc, a, out):
    with ExitStack() as ctx:
        def sb(name, shape, dt=F32):
            return ctx.enter_context(nc.sbuf_tensor(name, shape, dt))

        def sem(name):
            return ctx.enter_context(nc.semaphore(name))

        bank = [ctx.enter_context(nc.psum_tensor(f"bank{i}", [P, 512], F32)) for i in range(8)]

        ident = sb("ident", [P, P])
        ident_h = sb("ident_h", [P, P], BF16)
        ones = sb("ones", [P, P])
        x_res = sb("x_res", [P, TT, D])
        xn = sb("xn", [P, TT, D])
        xnT = sb("xnT", [P, DC, T])
        bn = sb("bn", [P, TT, 6])
        mv = sb("mv", [P, TT, 2])
        rstd = sb("rstd", [P, TT])
        var = sb("var", [P, TT])
        log_var = sb("log_var", [P, TT])
        newton = sb("newton", [P, TT])
        columns = sb("columns", [P, len(COLUMNS) * DC])
        rows = sb("rows", [1, len(ROWS) * D])

        def column(name, c):
            k = COLUMNS.index(name) * DC + c
            return columns[:, k:k + 1]

        def row(name):
            k = ROWS.index(name) * D
            return rows[0:1, k:k + D]

        region_a = sb("region_a", [P, 14336])
        region_g = sb("region_g", [P, 8192])
        kT = region_a[:, 0:4096].rearrange("p (m k) -> p m k", m=8)
        v_blk = region_a[:, 4096:8192].rearrange("p (t n) -> p t n", t=KT_PER)
        wkv = region_a[:, 8192:12288].rearrange("p (c n) -> p c n", c=2)
        wq = region_a[:, 12288:14336].rearrange("p (c n) -> p c n", c=2)
        o_acc = region_g[:, 0:2048].rearrange("p (t n) -> p t n", t=TT)
        prob = region_g[:, 2048:4096].rearrange("p (b t k) -> p b t k", b=2, t=TT)
        probT = region_g[:, 4096:6144].rearrange("p (b t k) -> p b t k", b=2, t=TT)
        mask_w = region_g[:, 6144:8192]
        oT = region_g[:, 2048:4096].rearrange("p (c n) -> p c n", c=8)
        wo = sb("wo", [P, 8, D])
        qT = sb("qT", [P, 8, T])
        region_u = sb("region_u", [P, 8192])
        region_d = sb("region_d", [P, 8192])
        wqk2 = region_u[:, 0:2048].rearrange("p (c n) -> p c n", c=DC)
        wv2 = region_u[:, 2048:2560].rearrange("p (c n) -> p c n", c=DC)
        wo2 = region_u[:, 2560:3072].rearrange("p (c n) -> p c n", c=DC)
        proj = region_u[:, 3072:3200]
        minus_half = region_u[:, 3200:3328]
        band = region_u[:, 3328:3840].rearrange("p (t k) -> p t k", t=TT)
        mixT = region_u[:, 3840:4224]

        def part(region, at, size):
            return region[:, at:at + size]

        q2T = part(region_a, 0, 1024).rearrange("p (c n) -> p c n", c=4)
        k2T = part(region_a, 1024, 1024).rearrange("p (c n) -> p c n", c=4)
        q2sq = part(region_a, 2048, 1024).rearrange("p (c n) -> p c n", c=4)
        k2sq = part(region_a, 3072, 1024).rearrange("p (c n) -> p c n", c=4)
        fq = part(region_a, 4096, 1024).rearrange("p (t h m) -> p t h m", t=TT, h=LH)
        fk = part(region_a, 5120, 1024).rearrange("p (t h m) -> p t h m", t=TT, h=LH)
        fqT = part(region_a, 6144, 1024).rearrange("p (c n) -> p c n", c=4)
        fkT = part(region_a, 7168, 1024).rearrange("p (c n) -> p c n", c=4)
        mixed0 = part(region_a, 8192, 4096).rearrange("p (h i) -> p h i", h=LH)
        mixed1 = part(region_a, 12288, 2048).rearrange("p (h i) -> p h i", h=LH)
        s2 = part(region_g, 0, 1024).rearrange("p (b t k) -> p b t k", b=2, t=TT)
        p2 = part(region_g, 1024, 1024).rearrange("p (b t k) -> p b t k", b=2, t=TT)
        p2T = part(region_g, 2048, 1024).rearrange("p (b k) -> p b k", b=2)
        v2 = part(region_g, 3072, TT * LH * 17).rearrange("p (t h d) -> p t h d", t=TT, h=LH)
        lin = part(region_g, 3616, TT * LH * 17).rearrange("p (t h d) -> p t h d", t=TT, h=LH)
        att = part(region_g, 4160, TT * D).rearrange("p (t h d) -> p t h d", t=TT, h=LH)
        att_flat = part(region_g, 4160, TT * D).rearrange("p (t n) -> p t n", t=TT)
        attT = sb("attT", [P, DC, T])
        w_q3 = part(region_d, 0, 4096).rearrange("p (g d) -> p g d", g=2 * EH)
        keysT = part(region_d, 4096, 1024)
        downT = region_d[:, :].rearrange("p (c e) -> p c e", c=DC)
        up = region_u[:, :].rearrange("p (h d) -> p h d", h=ET)
        w_sim = sb("w_sim", [P, DC, 2 * EH * NK])
        hidden = region_g[:, :].rearrange("p (h t) -> p h t", h=ET)
        hot_lo = part(region_a, 0, GS * P).bitcast(BF16).rearrange("p (b l s) -> p b l s", b=2, s=GS)
        hot_hi = part(region_a, 2048, 3 * GS * ET).bitcast(BF16).rearrange("p (b w h s) -> p b w h s", b=2, w=3, s=GS)
        hit_hi = part(region_a, 4096, GS * ET).bitcast(BF16).rearrange("p (b h s) -> p b h s", b=2, s=GS)
        iota_h = part(region_a, 6400, GS * P // 2).bitcast(BF16).rearrange("p (l s) -> p l s", s=GS)
        chosen_h = part(region_a, 7424, 5 * P // 2).bitcast(BF16).rearrange("p (k n) -> p k n", k=5)
        rest_w = part(region_a, 7744, P)
        iota = part(region_a, 5120, P)
        chosenT = part(region_a, 5248, 3 * P).rearrange("p (s n) -> p s n", s=3)
        top = part(region_a, 5632, TT * 2 * EH * 8).rearrange("p (t g k) -> p t g k", t=TT, g=2 * EH)
        top_i = part(region_a, 5888, TT * 2 * EH * 8).bitcast(U32).rearrange("p (t g k) -> p t g k", t=TT, g=2 * EH)
        top_f = part(region_a, 6144, TT * 2 * EH * 8).rearrange("p (t g k) -> p t g k", t=TT, g=2 * EH)
        pairs = part(region_a, 0, TT * EH * 64).rearrange("p (t h k) -> p t h k", t=TT, h=EH)
        pick = part(region_a, 1024, 512).rearrange("p (k j) -> p k j", j=8)
        squares = part(region_a, 1536, TT * D).rearrange("p (t d) -> p t d", t=TT)
        best = part(region_a, 2048, P).rearrange("p (t k) -> p t k", t=TT)
        best_i = part(region_a, 2176, P).bitcast(U32).rearrange("p (t k) -> p t k", t=TT)
        rank_i = part(region_a, 2304, 2 * P).bitcast(U32).rearrange("p (s t k) -> p s t k", s=2, t=TT)
        rank = part(region_a, 2560, 2 * P).rearrange("p (s t k) -> p s t k", s=2, t=TT)
        side = part(region_a, 2816, 2 * P).rearrange("p (s t k) -> p s t k", s=2, t=TT)
        expert = part(region_a, 3072, P).rearrange("p (t k) -> p t k", t=TT)
        expert_i = part(region_a, 3200, P).bitcast(U32).rearrange("p (t k) -> p t k", t=TT)
        split_i = part(region_a, 3328, 2 * P).bitcast(U32).rearrange("p (s t k) -> p s t k", s=2, t=TT)
        chosen = part(region_a, 3584, 3 * P).rearrange("p (s n) -> p s n", s=3)
        qT_flat = qT[:, :, :].rearrange("p m q -> p (m q)")
        wq4 = part(qT_flat, 0, 512).rearrange("p (c n) -> p c n", c=DC)
        wk4T = part(qT_flat, 512, 2 * (CD + 1)).rearrange("p (c n) -> p c n", c=DC)
        wv4a = part(qT_flat, 898, D)
        wv4b = part(qT_flat, 1154, D)[0:CD - P + 1]
        ctxT_a = region_d[:, 0:S2]
        ctxT_b = region_d[0:CD - P + 1, S2:2 * S2]
        ctx_rows = part(region_a, 8192, S2 // P * CD).rearrange("p (k d) -> p k d", k=S2 // P)
        q4T = part(region_g, 0, 512).rearrange("p (c n) -> p c n", c=DC)
        qk_a = part(region_g, 512, T)
        qk_b = part(region_g, 768, T)[0:CD - P + 1]
        p4 = part(region_g, 1024, 2048).rearrange("p (b k) -> p b k", b=2)
        p4T = part(region_g, 3072, 2048).rearrange("p (b k) -> p b k", b=2)
        o4 = part(region_g, 5120, TT * CD).rearrange("p (t d) -> p t d", t=TT)
        o4T_a = part(region_g, 5504, T)
        o4T_b = part(region_g, 5760, T)[0:CD - P + 1]
        nm4_half = sb("nm4_half", [P, TT, 2])
        nm4_run = sb("nm4_run", [P, TT])
        nm4_new = sb("nm4_new", [P, TT])
        diff4 = sb("diff4", [P, UNITS])
        alpha4 = sb("alpha4", [P, UNITS])
        sum4 = sb("sum4", [P, UNITS, 2])
        l4 = sb("l4", [P, TT])
        w5 = wo[:, :, :].rearrange("p c n -> p (c n)").rearrange("p (w c n) -> p w c n", w=4, c=DC)
        q5T = part(region_g, 0, 512).rearrange("p (c n) -> p c n", c=DC)
        k5T = part(region_g, 512, 512).rearrange("p (c n) -> p c n", c=DC)
        v5 = part(region_g, 1024, 512).rearrange("p (t n) -> p t n", t=TT)
        s5 = part(region_g, 1536, 512).rearrange("p (t n) -> p t n", t=TT)
        p5 = part(region_g, 2048, 512).rearrange("p (t n) -> p t n", t=TT)
        p5T = part(region_g, 2560, 512)
        keep5 = part(region_g, 6016, 512).rearrange("p (t n) -> p t n", t=TT)
        fill5 = part(region_g, 6528, 512).rearrange("p (t n) -> p t n", t=TT)
        wg6 = part(region_u, 0, DC * FALL).rearrange("p (c n) -> p c n", c=DC)
        wu6 = part(region_u, DC * FALL, DC * FALL).rearrange("p (c n) -> p c n", c=DC)
        wd6 = part(region_a, 0, FT * D).rearrange("p (m n) -> p m n", m=FT)
        owner6 = part(region_a, FT * D, FALL)[0:MOE + 1]
        wr6 = part(region_a, FT * D + FALL, DC * MOE).rearrange("p (c n) -> p c n", c=DC)
        ebias6 = part(region_a, FT * D + FALL + 16, MOE)
        iota6 = part(region_a, FT * D + FALL + 24, MOE)
        silu6 = part(region_g, 0, 2 * T).rearrange("p (b n) -> p b n", b=2)
        h6 = part(region_g, 512, FT * T).rearrange("p (m n) -> p m n", m=FT)
        w6T = part(region_g, 512 + FT * T, T)[0:MOE + 1]
        r6 = sb("r6", [P, 6, TT, MOE + 1])
        r6_i = sb("r6_i", [P, TT, 8], U32)
        r6_s = sb("r6_s", [P, TT])
        qk_bias = sb("qk_bias", [P, 8])
        q_ls = sb("q_ls", [P, TT, LH])
        k_ls = sb("k_ls", [P, TT, LH])
        k_max = sb("k_max", [P, LH])
        k_stab = sb("k_stab", [P, LH])
        nm2 = sb("nm2", [P, TT, LH])
        sum2 = sb("sum2", [P, TT, LH])
        stat = sb("stat", [P, 4, TT, LH])
        ctx_a = sb("ctx_a", [P, BLK])
        ctx_b = sb("ctx_b", [CD - P, BLK])
        bias_h = sb("bias_h", [P, TT, BLK], BF16)
        seen = sb("seen", [P, TT, NBLK])
        is_row = sb("is_row", [P, TT])
        any_q = sb("any_q", [P, TT])
        rng = sb("rng", [1, 8 * NBLK])
        rng_i = sb("rng_i", [1, 2], I32)
        blk_lo = sb("blk_lo", [1, NBLK])
        blk_hi = sb("blk_hi", [1, NBLK])
        nm_run = sb("nm_run", [P, XH, TT])
        nm_blk = sb("nm_blk", [P, XH, TT])
        nm_new = sb("nm_new", [P, XH, TT])
        m_diff = sb("m_diff", [P, XH, TT])
        alpha = sb("alpha", [P, XH, TT])
        l_blk = sb("l_blk", [P, XH, TT])
        l_run = sb("l_run", [P, XH, TT])

        x_in, weights_in, mask_in, small_in, wkv_in, wo_in = (
            sem(n) for n in ("x_in", "weights_in", "mask_in", "small_in", "wkv_in", "wo_in"))
        ctx_landed, ctx_free = sem("ctx_landed"), sem("ctx_free")
        dve_step, act_step = sem("dve_step"), sem("act_step")
        consts_set = sem("consts_set")
        blocks_seen, blocks_counted, range_set = sem("blocks_seen"), sem("blocks_counted"), sem("range_set")
        xn_ready, xnT_psum, xnT_ready = sem("xn_ready"), sem("xnT_psum"), sem("xnT_ready")
        q_psum, q_ready = sem("q_psum"), sem("q_ready")
        bias_ready, k_psum, v_psum, k_ready, v_ready = (
            sem(n) for n in ("bias_ready", "k_psum", "v_psum", "k_ready", "v_ready"))
        s_ready, nm_blk_ready, nm_ready, diff_ready, prob_ready, alpha_ready = (
            sem(n) for n in ("s_ready", "nm_blk_ready", "nm_ready", "diff_ready", "prob_ready", "alpha_ready"))
        pT_psum, pT_ready0, pT_ready1, o_psum, o_added = (
            sem(n) for n in ("pT_psum", "pT_ready0", "pT_ready1", "o_psum", "o_added"))
        l_scaled, run_kept = sem("l_scaled"), sem("run_kept")
        o_normed, oT_psum, oT_ready, y_psum, x_ready = (
            sem(n) for n in ("o_normed", "oT_psum", "oT_ready", "y_psum", "x_ready"))
        var_ready, rstd_ready = sem("var_ready"), sem("rstd_ready")
        stored = sem("stored")
        late_w_in, ctxT_in, ctx_rows_in, masks5_in, moe_in, moe_small_in = (
            sem(n) for n in ("late_w_in", "ctxT_in", "ctx_rows_in", "masks5_in", "moe_in", "moe_small_in"))
        q4_psum, q4_ready, qk4_psum, qk4_ready = (
            sem(n) for n in ("q4_psum", "q4_ready", "qk4_psum", "qk4_ready"))
        s4_psum, nm4_ready, diff4_ready, p4_ready, alpha4_ready, p4T_psum, p4T_ready0, p4T_ready1, o4_psum, o4_added = (
            sem(n) for n in ("s4_psum", "nm4_ready", "diff4_ready", "p4_ready", "alpha4_ready", "p4T_psum",
                             "p4T_ready0", "p4T_ready1", "o4_psum", "o4_added"))
        v5_ready = sem("v5_ready")
        o4_normed, o4T_psum, o4T_ready, ones4_set = (
            sem(n) for n in ("o4_normed", "o4T_psum", "o4T_ready", "ones4_set"))
        qkv5_psum, qkv5_ready, s5_psum, s5_ready, p5_ready, p5T_psum, p5T_ready, o5_psum = (
            sem(n) for n in ("qkv5_psum", "qkv5_ready", "s5_psum", "s5_ready", "p5_ready", "p5T_psum", "p5T_ready",
                             "o5_psum"))
        router_psum, router_exp, w6_ready, w6T_psum, w6T_ready, gate_psum, up6_psum, silu_ready, h6_ready = (
            sem(n) for n in ("router_psum", "router_exp", "w6_ready", "w6T_psum", "w6T_ready", "gate_psum", "up6_psum",
                             "silu_ready", "h6_ready"))
        up_in = sem("up_in")
        sim_in, experts_in, wsim_psum, wsim_ready, iota_in = (
            sem(n) for n in ("sim_in", "experts_in", "wsim_psum", "wsim_ready", "iota_in"))
        sim_psum, down_psum, gelu_ready, chosen_ready, chosenT_psum = (
            sem(n) for n in ("sim_psum", "down_psum", "gelu_ready", "chosen_ready", "chosenT_psum"))
        hit_ready, hot_ready, mixw_psum, hidden_ready = (
            sem(n) for n in ("hit_ready", "hot_ready", "mixw_psum", "hidden_ready"))
        lin_in, norm_done = sem("lin_in"), sem("norm_done")
        qk2_psum, q2_ready, k2_ready, v2_psum, v2_ready = (
            sem(n) for n in ("qk2_psum", "q2_ready", "k2_ready", "v2_psum", "v2_ready"))
        fq_psum, fk_psum, k_maxed, k_stab_ready, fq_arg, fk_arg, fq_ready, fk_ready = (
            sem(n) for n in ("fq_psum", "fk_psum", "k_maxed", "k_stab_ready", "fq_arg", "fk_arg", "fq_ready", "fk_ready"))
        s2_psum, s2_ready, p2_ready, p2T_psum, p2T_ready, pv2_psum = (
            sem(n) for n in ("s2_psum", "s2_ready", "p2_ready", "p2T_psum", "p2T_ready", "pv2_psum"))
        fT_psum, fqT_ready, fkT_ready, mix_psum, mix_ready, hv_psum = (
            sem(n) for n in ("fT_psum", "fqT_ready", "fkT_ready", "mix_psum", "mix_ready", "hv_psum"))
        gap_ready, gap_exp, att_ready, attT_psum, attT_ready = (
            sem(n) for n in ("gap_ready", "gap_exp", "att_ready", "attT_psum", "attT_ready"))

        norms = [0]

        def refine_rstd(dve, step):
            step(nc.vector.tensor_tensor(newton[:, :], var[:, :], rstd[:, :], ALU.mult))
            step(nc.vector.tensor_tensor(newton[:, :], newton[:, :], rstd[:, :], ALU.mult))
            step(nc.vector.tensor_scalar(newton[:, :], newton[:, :], -0.5, 1.5, ALU.mult, ALU.add))
            step(nc.vector.tensor_tensor(rstd[:, :], rstd[:, :], newton[:, :], ALU.mult))

        def rstd_by_exp(act, nth):
            act.wait_ge(var_ready, nth)
            nc.scalar.activation(log_var[:, :], var[:, :], ACT.Ln).then_inc(act_step, 1)
            act.wait_ge(act_step, nth)
            nc.scalar.activation(rstd[:, :], log_var[:, :], ACT.Exp, scale=-0.5).then_inc(rstd_ready, 1)

        def layer_norm(dve, step, src, dst, after=None):
            for t in range(TT):
                ins = nc.vector.bn_stats(bn[:, t], src[:, t])
            step(ins)
            for t in range(TT):
                ins = nc.vector.bn_aggr(mv[:, t], bn[:, t])
            step(ins)
            nc.vector.tensor_scalar(var[:, :], mv[:, :, 1], EPS_OF_NORM[norms[0]], None, ALU.add).then_inc(var_ready, 1)
            norms[0] += 1
            dve.wait_ge(rstd_ready, norms[0])
            refine_rstd(dve, step)
            for t in range(TT):
                ins = nc.vector.tensor_scalar(dst[:, t], src[:, t], mv[:, t, 0:1], rstd[:, t:t + 1],
                                              ALU.subtract, ALU.mult)
                if after is not None:
                    ins.then_inc(after, 1)
            if after is None:
                step(ins)

        def within(eng, b):
            return nc.s_assert_within(b, 0, NBLK - 1)

        def turn_xn(pe, nth, into):
            pe.wait_ge(xn_ready, TT * nth)
            for c in range(DC):
                for t in range(TT):
                    mm = nc.tensor.transpose(into[c][:, t * P:(t + 1) * P],
                                             xn[:, t, c * P:(c + 1) * P], ident[:, :])
            mm.then_inc(xnT_psum, 1)

        def turn_and_project(pe, nth, src, banks, w, bias, dst):
            pe.wait_ge(att_ready, nth)
            for c in range(DC):
                for t in range(TT):
                    mm = nc.tensor.transpose(banks[c][:, t * P:(t + 1) * P], src[:, t, c * P:(c + 1) * P], ident[:, :])
                mm.then_inc(attT_psum, 1)
            pe.wait_ge(attT_ready, 2 * nth)
            for t in range(TT):
                into = dst[:, t * D:(t + 1) * D]
                nc.tensor.matmul(into, lhsT=ones[0:1, :], rhs=bias, start=True, stop=False)
                for c in range(DC):
                    mm = nc.tensor.matmul(into, lhsT=attT[:, c, t * P:(t + 1) * P], rhs=w[:, c, :],
                                          start=False, stop=c == DC - 1)
            mm.then_inc(y_psum, 1)

        block = ctx.enter_context(nc.Block())

        @block.sync
        def _(sp):
            sp.dma_start(x_res[:, :, :], a["x"].rearrange("(t p) d -> p t d", p=P)).then_inc(x_in, 16)
            sp.dma_start(mask_w.bitcast(U32).rearrange("p (t w) -> p t w", t=TT),
                         a["mask"].rearrange("(t p) w -> p t w", p=P)).then_inc(mask_in, 16)
            sp.dma_start(ident[:, :], a["ident"]).then_inc(small_in, 16)
            sp.dma_start(columns[:, :], a["columns"]).then_inc(small_in, 16)
            sp.dma_start(blk_lo[:, :], a["block_numbers"][0:1]).then_inc(small_in, 16)
            sp.dma_start(blk_hi[:, :], a["block_numbers"][1:2]).then_inc(small_in, 16)
            sp.dma_start(rows[:, :], a["rows"]).then_inc(small_in, 16)
            sp.dma_start(wq, a["Wq"].rearrange("(c p) n -> p c n", p=P)).then_inc(weights_in, 16)
            sp.dma_start(w_q3, a["w_q"].rearrange("(g p) d -> p g d", p=P)).then_inc(sim_in, 16)
            sp.dma_start(keysT, a["keysT"]).then_inc(sim_in, 16)
            sp.dma_start(wkv[:, 0, :], a["Wkv"][0:P]).then_inc(wkv_in, 16)
            sp.dma_start(wkv[0:CD - P, 1, :], a["Wkv"][P:CD]).then_inc(wkv_in, 16)
            sp.dma_start(wo[:, :, :], a["Wo"].rearrange("(c p) n -> p c n", p=P)).then_inc(wo_in, 16)
            for dst, name in ((wqk2, "wqk2"), (wv2, "wv2"), (wo2, "wo2")):
                sp.dma_start(dst, a[name].rearrange("(c p) n -> p c n", p=P)).then_inc(lin_in, 16)
            for dst, name in ((proj, "proj"), (minus_half, "minus_half"), (mixT, "mixT"), (qk_bias[:, :], "qk_bias")):
                sp.dma_start(dst, a[name]).then_inc(lin_in, 16)
            sp.dma_start(band, a["band"].rearrange("p (t k) -> p t k", t=TT)).then_inc(lin_in, 16)
            sp.wait_ge(range_set, 1)
            first = sp.value_load(rng_i[0:1, 0:1], min_val=0, max_val=NBLK - 1)
            n_blocks = sp.value_load(rng_i[0:1, 1:2], min_val=1, max_val=NBLK)

            def load_block(b):
                sp.dma_start(ctx_a[:, :], a["ctxT"][0:P, bass.ds(b * BLK, BLK)]).then_inc(ctx_landed, 16)
                sp.dma_start(ctx_b[:, :], a["ctxT"][P:CD, bass.ds(b * BLK, BLK)]).then_inc(ctx_landed, 16)

            with sp.Fori(0, n_blocks) as i:
                sp.wait_ge(ctx_free, i + 1)
                load_block(within(sp, first + i))
            sp.wait_ge(wsim_psum, 4)
            for c in range(DC):
                sp.dma_start(downT[:, c], a["downT"][c * P:(c + 1) * P]).then_inc(experts_in, 16)
            sp.wait_ge(x_ready, 2)
            sp.dma_start(iota, a["iota"]).then_inc(iota_in, 16)
            for c in range(2):
                sp.dma_start(up[:, c * 16:(c + 1) * 16], a["up"].rearrange("(h l) d -> l h d", l=P)[:, c * 16:(c + 1) * 16]
                             ).then_inc(up_in, 16)
            sp.dma_start(wq4, a["wq4"].rearrange("(c p) n -> p c n", p=P)).then_inc(late_w_in, 16)
            sp.dma_start(wk4T, a["wk4T"].rearrange("(c p) n -> p c n", p=P)).then_inc(late_w_in, 16)
            sp.dma_start(wv4a, a["wv4"][0:P]).then_inc(late_w_in, 16)
            sp.dma_start(wv4b, a["wv4"][P:CD + 1]).then_inc(late_w_in, 16)
            sp.dma_start(ctx_rows, a["ctx"].rearrange("(k p) d -> p k d", p=P)).then_inc(ctx_rows_in, 16)
            sp.wait_ge(down_psum, ET // 2)
            sp.dma_start(ctxT_a, a["ctxT"][0:P]).then_inc(ctxT_in, 16)
            sp.dma_start(ctxT_b[0:CD - P], a["ctxT"][P:CD]).then_inc(ctxT_in, 16)
            for w, name in enumerate(("wq5", "wk5", "wv5", "wo5")):
                sp.dma_start(w5[:, w], a[name].rearrange("(c p) n -> p c n", p=P)).then_inc(late_w_in, 16)
            sp.wait_ge(x_ready, 3)
            sp.dma_start(keep5, a["keep5"].rearrange("p (t n) -> p t n", t=TT)).then_inc(masks5_in, 16)
            sp.dma_start(fill5, a["fill5"].rearrange("p (t n) -> p t n", t=TT)).then_inc(masks5_in, 16)
            sp.dma_start(wr6, a["wr6"].rearrange("(c p) n -> p c n", p=P)).then_inc(moe_small_in, 16)
            sp.dma_start(ebias6, a["ebias6"].partition_broadcast(P)).then_inc(moe_small_in, 16)
            sp.dma_start(iota6, a["iota"][:, 0:MOE]).then_inc(moe_small_in, 16)
            sp.dma_start(owner6, a["owner6"]).then_inc(moe_small_in, 16)
            sp.dma_start(wg6, a["wg6"].rearrange("(c p) n -> p c n", p=P)).then_inc(moe_in, 16)
            sp.dma_start(wu6, a["wu6"].rearrange("(c p) n -> p c n", p=P)).then_inc(moe_in, 16)
            full = FALL // P
            sp.dma_start(wd6[:, 0:full], a["wd6"][0:full * P].rearrange("(m p) n -> p m n", p=P)).then_inc(moe_in, 16)
            sp.dma_start(wd6[0:FALL - full * P, full], a["wd6"][full * P:FALL]).then_inc(moe_in, 16)
            sp.wait_ge(x_ready, 6)
            sp.dma_start(out.rearrange("(t p) d -> p t d", p=P), x_res[:, :, :]).then_inc(stored, 16)
            sp.wait_ge(stored, 16)

        @block.tensor
        def _(pe):
            pe.wait_ge(small_in, 80)
            pe.wait_ge(consts_set, 3)
            pe.wait_ge(blocks_seen, 1)
            nc.tensor.matmul(bank[0][0:1, 0:TT * NBLK], lhsT=ones[:, 0:1],
                             rhs=seen[:, :, :].rearrange("p t b -> p (t b)"),
                             start=True, stop=True).then_inc(blocks_counted, 1)
            turn_xn(pe, 1, (bank[1], bank[7]))
            pe.wait_ge(weights_in, 16)
            pe.wait_ge(xnT_ready, 2)
            for m in range(8):
                dst = bank[2 + m // 2][:, (m % 2) * T:(m % 2 + 1) * T]
                for c in range(DC):
                    mm = nc.tensor.matmul(dst, lhsT=wq[:, c, m * P:(m + 1) * P], rhs=xnT[:, c, :],
                                          start=c == 0, stop=c == DC - 1)
                if m % 2:
                    mm.then_inc(q_psum, 1)
            pe.wait_ge(sim_in, 32)
            for c in range(DC):
                for g in range(2 * EH):
                    if g == 0 and c == 0:
                        pe.wait_ge(range_set, 1)
                    mm = nc.tensor.matmul(bank[(0, 1, 6, 7)[2 * c + g // EH]][:, (g % EH) * NK:(g % EH + 1) * NK],
                                          lhsT=w_q3[:, g, c * P:(c + 1) * P], rhs=keysT[:, g * NK:(g + 1) * NK],
                                          start=True, stop=True)
                    if g % EH == EH - 1:
                        mm.then_inc(wsim_psum, 1)
            pe.wait_ge(wkv_in, 32)
            pe.wait_ge(range_set, 1)
            n_blocks = pe.value_load(rng_i[0:1, 1:2], min_val=1, max_val=NBLK)
            pe.wait_ge(wsim_ready, 4)
            pe.wait_ge(q_ready, 4)
            with pe.Fori(0, n_blocks) as i:
                base = pe.snap(i * XH)
                base8 = pe.snap(i * 8)
                pe.wait_ge(ctx_landed, i * 32 + 32)
                for j in range(16):
                    if j in (4, 5, 6, 7, 8, 9, 10, 11):
                        pe.wait_ge(k_ready, base8 + (j - 3))
                    elif j >= 12:
                        pe.wait_ge(v_ready, base8 + (j - 11))
                    for c, rows in ((0, P), (1, CD - P)):
                        src = (ctx_a, ctx_b)[c]
                        if j < 8:
                            lhsT, rhs = wkv[0:rows, c, j * P:(j + 1) * P], src[:, :]
                        else:
                            t, half = (j - 8) // 2, j % 2
                            lhsT = src[:, t * P:(t + 1) * P]
                            rhs = wkv[0:rows, c, 1024 + half * 512:1024 + (half + 1) * 512]
                        mm = nc.tensor.matmul(bank[j % 4][:, :], lhsT=lhsT, rhs=rhs, start=c == 0, stop=c == 1)
                    mm.then_inc(k_psum if j < 8 else v_psum, 1)
                pe.wait_ge(bias_ready, i + 1)
                pe.wait_ge(k_ready, base8 + 8)
                pe.wait_ge(v_ready, base8 + 8)

                def scores(h):
                    if h >= 2:
                        pe.wait_ge(prob_ready, 2 * base + 2 * (h - 1))
                    for t in range(TT):
                        dst = bank[2 * (h % 2) + t][:, :]
                        rows = slice(XD * (h % 2), XD * (h % 2) + XD)
                        mm = nc.tensor.matmul(dst, lhsT=qT[rows, h // 2, t * P:(t + 1) * P], rhs=kT[rows, h // 2, :],
                                              start=True, stop=False)
                        if h == 0 and t == 0:
                            mm.then_inc(ctx_free, 1)
                        mm = nc.tensor.matmul(dst, lhsT=ident_h[:, :], rhs=bias_h[:, t, :], start=False, stop=True)
                    mm.then_inc(s_ready, 1)

                def turn(h):
                    for t in range(TT):
                        pe.wait_ge(prob_ready, 2 * base + (2 * h + t + 1))
                        if h >= 1:
                            pe.wait_ge((pT_ready0, pT_ready1)[t], base + h)
                        for k in range(KT_PER):
                            mm = nc.tensor.transpose(bank[4 + t][:, k * P:(k + 1) * P],
                                                     prob[:, h % 2, t, k * P:(k + 1) * P], ident[:, :])
                        mm.then_inc(pT_psum, 1)

                def values(h):
                    if h >= 2:
                        pe.wait_ge(o_added, base + (h - 1))
                    for t in range(TT):
                        pe.wait_ge((pT_ready0, pT_ready1)[t], base + (h + 1))
                        for k in range(KT_PER):
                            mm = nc.tensor.matmul(bank[6 + h % 2][:, t * XD:(t + 1) * XD],
                                                  lhsT=probT[:, h % 2, t, k * P:(k + 1) * P],
                                                  rhs=v_blk[:, k, h * XD:(h + 1) * XD],
                                                  start=k == 0, stop=k == KT_PER - 1)
                    mm.then_inc(o_psum, 1)

                for h in range(XH + 2):
                    if h < XH:
                        scores(h)
                    if 1 <= h <= XH:
                        turn(h - 1)
                    if h >= 2:
                        values(h - 2)
            pe.wait_ge(o_normed, 1)
            for c in range(8):
                for t in range(TT):
                    mm = nc.tensor.transpose(bank[c // 2][:, (c % 2) * T + t * P:(c % 2) * T + (t + 1) * P],
                                             o_acc[:, t, c * P:(c + 1) * P], ident[:, :])
                if c % 2:
                    mm.then_inc(oT_psum, 1)
            pe.wait_ge(wo_in, 16)
            pe.wait_ge(oT_ready, 4)
            for t in range(TT):
                dst = bank[4][:, t * D:(t + 1) * D]
                nc.tensor.matmul(dst, lhsT=ones[0:1, :], rhs=row("L0_xattn_bo"), start=True, stop=False)
                for c in range(8):
                    mm = nc.tensor.matmul(dst, lhsT=oT[:, c, t * P:(t + 1) * P], rhs=wo[:, c, :],
                                          start=False, stop=c == 7)
            mm.then_inc(y_psum, 1)

            turn_xn(pe, 2, (bank[0], bank[1]))
            pe.wait_ge(lin_in, 128)
            pe.wait_ge(xnT_ready, 4)
            for m in range(8):
                for c in range(DC):
                    mm = nc.tensor.matmul(bank[2 + m // 2][:, (m % 2) * T:(m % 2 + 1) * T],
                                          lhsT=wqk2[:, c, m * P:(m + 1) * P], rhs=xnT[:, c, :],
                                          start=c == 0, stop=c == DC - 1)
                if m % 2:
                    mm.then_inc(qk2_psum, 1)
            for t in range(TT):
                dst = bank[6][:, t * D:(t + 1) * D]
                nc.tensor.matmul(dst, lhsT=ones[0:1, :], rhs=row("L0_attn_v_b"), start=True, stop=False)
                for c in range(DC):
                    mm = nc.tensor.matmul(dst, lhsT=xnT[:, c, t * P:(t + 1) * P], rhs=wv2[:, c, :],
                                          start=False, stop=c == DC - 1)
            mm.then_inc(v2_psum, 1)
            for x2, sq, ready, psum, first in ((q2T, q2sq, q2_ready, fq_psum, 0), (k2T, k2sq, k2_ready, fk_psum, 2)):
                pe.wait_ge(ready, 5)
                if first:
                    pe.wait_ge(q2_ready, 5)
                for t in range(TT):
                    for c in range(4):
                        dst = bank[first + t][:, c * P:(c + 1) * P]
                        nc.tensor.matmul(dst, lhsT=x2[:, c, t * P:(t + 1) * P], rhs=proj, start=True, stop=False)
                        mm = nc.tensor.matmul(dst, lhsT=sq[:, c, t * P:(t + 1) * P], rhs=minus_half,
                                              start=False, stop=True)
                    mm.then_inc(psum, 1)

            def scores2(n):
                g, c = n // 4, n % 4
                if n >= 2:
                    pe.wait_ge(s2_ready, n - 1)
                for t in range(TT):
                    mm = nc.tensor.matmul(bank[4 + n % 2][:, t * T:(t + 1) * T],
                                          lhsT=q2T[32 * g:32 * g + 16, c, t * P:(t + 1) * P],
                                          rhs=k2T[32 * g:32 * g + 16, c, :], start=True, stop=True)
                mm.then_inc(s2_psum, 1)

            def turn2(n):
                pe.wait_ge(p2_ready, 2 * n + 2)
                if n >= 2:
                    pe.wait_ge(p2T_ready, n - 1)
                for j in range(TT):
                    for t in range(TT):
                        mm = nc.tensor.transpose(bank[6 + n % 2][:, (2 * j + t) * P:(2 * j + t + 1) * P],
                                                 p2[:, n % 2, t, j * P:(j + 1) * P], ident[:, :])
                mm.then_inc(p2T_psum, 1)

            def values2(n):
                h = 4 * (n % 4) + n // 4
                pe.wait_ge(p2T_ready, n + 1)
                for t in range(TT):
                    for j in range(TT):
                        mm = nc.tensor.matmul(bank[3][:, t * D + h * 16:t * D + h * 16 + 16],
                                              lhsT=p2T[:, n % 2, (2 * j + t) * P:(2 * j + t + 1) * P],
                                              rhs=v2[:, j, h, 0:16], start=j == 0, stop=j == TT - 1)
                mm.then_inc(pv2_psum, 1)

            pe.wait_ge(v2_ready, 1)
            pe.wait_ge(fk_arg, 2)
            for n in range(LH + 2):
                if n < LH:
                    scores2(n)
                if 1 <= n <= LH:
                    turn2(n - 1)
                if n >= 2:
                    values2(n - 2)
            for f, ready, banks in ((fq, fq_ready, (0, 1)), (fk, fk_ready, (2, 4))):
                pe.wait_ge(ready, 2)
                for c in range(4):
                    for t in range(TT):
                        mm = nc.tensor.transpose(bank[banks[c // 2]][:, (c % 2) * T + t * P:(c % 2) * T + (t + 1) * P],
                                                 f[:, t, 4 * c:4 * c + 4, :].rearrange("p h m -> p (h m)"), ident[:, :])
                    if c % 2:
                        mm.then_inc(fT_psum, 1)
            pe.wait_ge(fqT_ready, 2)
            pe.wait_ge(fkT_ready, 2)
            for g in range(4):
                own = (5, 6, 7) if g % 2 == 0 else (0, 1, 2)
                if g >= 2:
                    pe.wait_ge(mix_ready, 3 * (g - 1))
                rows32 = slice(32 * g, 32 * g + LM)
                for c in range(4):
                    mm = nc.tensor.matmul(bank[own[c // 2]][:, (c % 2) * T:(c % 2 + 1) * T],
                                          lhsT=fkT[rows32, c, 0:P], rhs=fqT[rows32, c, :], start=True, stop=True)
                    if c % 2:
                        mm.then_inc(mix_psum, 1)
                for c in range(4):
                    mm = nc.tensor.matmul(bank[own[2]][:, c * P:(c + 1) * P],
                                          lhsT=fkT[rows32, c, P:T], rhs=fqT[rows32, c, P:T], start=True, stop=True)
                mm.then_inc(mix_psum, 1)
            pe.wait_ge(mix_ready, 12)
            for h in range(LH):
                slot = 4 * (h % 4) + h // 4
                nc.tensor.matmul(bank[4][:, h * 17:(h + 1) * 17], lhsT=mixed0[:, slot, 0:P], rhs=v2[:, 0, h, :],
                                 start=True, stop=True)
                nc.tensor.matmul(bank[5][:, h * 17:(h + 1) * 17], lhsT=mixed0[:, slot, P:T], rhs=v2[:, 0, h, :],
                                 start=True, stop=False)
                mm = nc.tensor.matmul(bank[5][:, h * 17:(h + 1) * 17], lhsT=mixed1[:, slot, :], rhs=v2[:, 1, h, :],
                                      start=False, stop=True)
            mm.then_inc(hv_psum, 1)
            turn_and_project(pe, 1, att_flat, (bank[0], bank[1]), wo2, row("L0_attn_out_b"), bank[2])

            turn_xn(pe, 3, (bank[0], bank[1]))
            pe.wait_ge(xnT_ready, 6)
            for t in range(TT):
                for half in range(2):
                    for c in range(DC):
                        mm = nc.tensor.matmul(bank[2 + 2 * t + half][:, :], lhsT=xnT[:, c, t * P:(t + 1) * P],
                                              rhs=w_sim[:, c, half * 512:(half + 1) * 512],
                                              start=c == 0, stop=c == DC - 1)
                    mm.then_inc(sim_psum, 1)
            pe.wait_ge(experts_in, 32)
            for e in range(ET):
                b = e // 2
                if e % 2 == 0 and b >= 4:
                    pe.wait_ge(gelu_ready, b - 3)
                for c in range(DC):
                    mm = nc.tensor.matmul(bank[(6, 7, 0, 1)[b % 4]][:, (e % 2) * T:(e % 2 + 1) * T],
                                          lhsT=downT[:, c, e * P:(e + 1) * P], rhs=xnT[:, c, :],
                                          start=c == 0, stop=c == DC - 1)
                if e % 2:
                    mm.then_inc(down_psum, 1)
                if e == ET - 7:
                    pe.wait_ge(chosen_ready, 3)
                    for k in range(3):
                        mm = nc.tensor.transpose(bank[2][:, k * P:(k + 1) * P], chosen[:, k, :], ident[:, :])
                    mm.then_inc(chosenT_psum, 1)
            with pe.Fori(0, P // GS // 2) as i:
                two = pe.snap(i * 2)
                for g in range(2):
                    pe.wait_ge(hot_ready, two + (g + 1))
                    pe.wait_ge(hidden_ready, two + (g + 1))
                    for t in range(TT):
                        own = slice(64 * t, 64 * t + 64)
                        for s in range(GS):
                            for w in range(3):
                                mm = nc.tensor.matmul(
                                    bank[2 + 2 * g + t][:, :].rearrange("p (h s) -> p h s", h=ET)[:, :, s],
                                    lhsT=hot_lo[own, g, :, s], rhs=hot_hi[own, g, w, :, s], start=w == 0, stop=w == 2)
                    mm.then_inc(mixw_psum, 1)
            pe.wait_ge(gelu_ready, ET // 2)
            pe.wait_ge(hidden_ready, 2 + P // GS)
            pe.wait_ge(up_in, 32)
            for t in range(TT):
                for e in range(ET):
                    mm = nc.tensor.matmul(bank[6][:, t * D:(t + 1) * D], lhsT=hidden[:, e, t * P:(t + 1) * P],
                                          rhs=up[:, e, :], start=e == 0, stop=e == ET - 1)
            mm.then_inc(y_psum, 1)

            turn_xn(pe, 4, (bank[0], bank[1]))
            pe.wait_ge(late_w_in, 128)
            pe.wait_ge(xnT_ready, 8)
            for m in range(DC):
                for c in range(DC):
                    mm = nc.tensor.matmul(bank[2][:, m * T:(m + 1) * T], lhsT=wq4[:, c, m * P:(m + 1) * P],
                                          rhs=xnT[:, c, :], start=c == 0, stop=c == DC - 1)
            mm.then_inc(q4_psum, 1)
            pe.wait_ge(q4_ready, 2)
            for m, rows_m in ((0, P), (1, CD - P + 1)):
                for c in range(DC):
                    mm = nc.tensor.matmul(bank[3 + m][0:rows_m, 0:T], lhsT=wk4T[:, c, m * P:m * P + rows_m],
                                          rhs=q4T[:, c, :], start=c == 0, stop=c == DC - 1)
                mm.then_inc(qk4_psum, 1)
            pe.wait_ge(ctxT_in, 32)
            pe.wait_ge(ctx_rows_in, 16)
            pe.wait_ge(ones4_set, 2)
            pe.wait_ge(qk4_ready, 2)

            def scores4(u):
                i, t = u // TT, u % TT
                if u >= 2:
                    pe.wait_ge(p4_ready, 2 * (u - 1))
                for half in range(2):
                    dst = bank[2 * (u % 2) + half][:, :]
                    keys = slice(i * 1024 + half * 512, i * 1024 + half * 512 + 512)
                    nc.tensor.matmul(dst, lhsT=qk_a[:, t * P:(t + 1) * P], rhs=ctxT_a[:, keys], start=True, stop=False)
                    mm = nc.tensor.matmul(dst, lhsT=qk_b[:, t * P:(t + 1) * P], rhs=ctxT_b[:, keys],
                                          start=False, stop=True)
                mm.then_inc(s4_psum, 1)

            def turn4(u):
                for half in range(2):
                    pe.wait_ge(p4_ready, 2 * u + half + 1)
                    if u >= 1:
                        pe.wait_ge((p4T_ready0, p4T_ready1)[half], u)
                    for k in range(4):
                        mm = nc.tensor.transpose(bank[4 + half][:, k * P:(k + 1) * P],
                                                 p4[:, u % 2, half * 512 + k * P:half * 512 + (k + 1) * P], ident[:, :])
                    mm.then_inc(p4T_psum, 1)

            def values4(u):
                i = u // TT
                if u >= 2:
                    pe.wait_ge(o4_added, u - 1)
                for k in range(8):
                    if k % 4 == 0:
                        pe.wait_ge((p4T_ready0, p4T_ready1)[k // 4], u + 1)
                    mm = nc.tensor.matmul(bank[6 + u % 2][:, 0:CD], lhsT=p4T[:, u % 2, k * P:(k + 1) * P],
                                          rhs=ctx_rows[:, i * 8 + k, :], start=k == 0, stop=k == 7)
                mm.then_inc(o4_psum, 1)

            for u in range(UNITS + 2):
                if u < UNITS:
                    scores4(u)
                if 1 <= u <= UNITS:
                    turn4(u - 1)
                if u >= 2:
                    values4(u - 2)
            pe.wait_ge(o4_normed, 2)
            for t in range(TT):
                mm = nc.tensor.transpose(bank[0][:, t * P:(t + 1) * P], o4[:, t, 0:P], ident[:, :])
            mm.then_inc(o4T_psum, 1)
            for t in range(TT):
                mm = nc.tensor.transpose(bank[1][0:CD - P, t * P:(t + 1) * P], o4[:, t, P:CD], ident[:, :])
            mm.then_inc(o4T_psum, 1)
            pe.wait_ge(o4T_ready, 2)
            for t in range(TT):
                nc.tensor.matmul(bank[2][:, t * D:(t + 1) * D], lhsT=o4T_a[:, t * P:(t + 1) * P], rhs=wv4a,
                                 start=True, stop=False)
                mm = nc.tensor.matmul(bank[2][:, t * D:(t + 1) * D], lhsT=o4T_b[:, t * P:(t + 1) * P], rhs=wv4b,
                                      start=False, stop=True)
            mm.then_inc(y_psum, 1)
            turn_xn(pe, 5, (bank[0], bank[1]))
            pe.wait_ge(xnT_ready, 10)
            for w in range(2):
                for m in range(DC):
                    for c in range(DC):
                        mm = nc.tensor.matmul(bank[3 + w][:, m * T:(m + 1) * T], lhsT=w5[:, w, c, m * P:(m + 1) * P],
                                              rhs=xnT[:, c, :], start=c == 0, stop=c == DC - 1)
                mm.then_inc(qkv5_psum, 1)
            for t in range(TT):
                dst = bank[5][:, t * D:(t + 1) * D]
                nc.tensor.matmul(dst, lhsT=ones[0:1, :], rhs=row("L1_attn_bv"), start=True, stop=False)
                for c in range(DC):
                    mm = nc.tensor.matmul(dst, lhsT=xnT[:, c, t * P:(t + 1) * P], rhs=w5[:, 2, c, :],
                                          start=False, stop=c == DC - 1)
            mm.then_inc(qkv5_psum, 1)
            pe.wait_ge(qkv5_ready, 4)
            for t in range(TT):
                for c in range(DC):
                    mm = nc.tensor.matmul(bank[6 + t][:, 0:T], lhsT=q5T[:, c, t * P:(t + 1) * P], rhs=k5T[:, c, :],
                                          start=c == 0, stop=c == DC - 1)
                mm.then_inc(s5_psum, 1)
            for t in range(TT):
                pe.wait_ge(p5_ready, t + 1)
                for j in range(TT):
                    mm = nc.tensor.transpose(bank[0][:, (2 * t + j) * P:(2 * t + j + 1) * P], p5[:, t, j * P:(j + 1) * P],
                                             ident[:, :])
            mm.then_inc(p5T_psum, 1)
            pe.wait_ge(p5T_ready, 1)
            pe.wait_ge(v5_ready, 1)
            for t in range(TT):
                for j in range(TT):
                    mm = nc.tensor.matmul(bank[1][:, t * D:(t + 1) * D],
                                          lhsT=p5T[:, (2 * t + j) * P:(2 * t + j + 1) * P], rhs=v5[:, j, :],
                                          start=j == 0, stop=j == TT - 1)
            mm.then_inc(o5_psum, 1)
            turn_and_project(pe, 2, att_flat, (bank[2], bank[3]), w5[:, 3], row("L1_attn_bo"), bank[4])
            turn_xn(pe, 6, (bank[0], bank[1]))
            pe.wait_ge(xnT_ready, 12)
            pe.wait_ge(moe_small_in, 64)
            for t in range(TT):
                for c in range(DC):
                    mm = nc.tensor.matmul(bank[2][:, t * MOE:(t + 1) * MOE], lhsT=xnT[:, c, t * P:(t + 1) * P],
                                          rhs=wr6[:, c, :], start=c == 0, stop=c == DC - 1)
            mm.then_inc(router_psum, 1)
            pe.wait_ge(moe_in, 64)

            def rows_of(m):
                return min(P, FALL - m * P)

            def gate_and_up(m):
                n = rows_of(m)
                if m >= 2:
                    pe.wait_ge(silu_ready, m - 1)
                    pe.wait_ge(h6_ready, m - 1)
                for w, b, psum in ((wg6, 3, gate_psum), (wu6, 5, None)):
                    for c in range(DC):
                        mm = nc.tensor.matmul(bank[b + m % 2][0:n, 0:T], lhsT=w[:, c, m * P:m * P + n],
                                              rhs=xnT[:, c, :], start=c == 0, stop=c == DC - 1)
                    if psum:
                        mm.then_inc(psum, 1)
                if m == 0:
                    pe.wait_ge(w6_ready, 1)
                    for t in range(TT):
                        mm = nc.tensor.transpose(bank[2][0:MOE + 1, t * P:(t + 1) * P], r6[:, 5, t, :], ident[:, :])
                    mm.then_inc(w6T_psum, 1)
                    pe.wait_ge(w6T_ready, 1)
                mm = nc.tensor.matmul(bank[5 + m % 2][0:n, T:2 * T], lhsT=owner6[:, m * P:m * P + n], rhs=w6T,
                                      start=True, stop=True)
                mm.then_inc(up6_psum, 1)

            def down(m):
                n = rows_of(m)
                pe.wait_ge(h6_ready, m + 1)
                for t in range(TT):
                    mm = nc.tensor.matmul(bank[(7, 0)[t]][:, 0:D], lhsT=h6[0:n, m, t * P:(t + 1) * P],
                                          rhs=wd6[0:n, m, :], start=m == 0, stop=m == FT - 1)
                if m == FT - 1:
                    mm.then_inc(y_psum, 1)

            for m in range(FT + 1):
                if m < FT:
                    gate_and_up(m)
                if m >= 1:
                    down(m - 1)

        @block.scalar
        def _(act):
            rstd_by_exp(act, 1)
            rstd_by_exp(act, 2)
            act.wait_ge(small_in, 80)
            act.wait_ge(xnT_psum, 1)
            nc.scalar.activation(xnT[:, 0, :], bank[1][:, 0:T], ACT.Identity, bias=column("L0_xattn_ln_beta", 0),
                                 scale=column("L0_xattn_ln_gamma", 0)).then_inc(xnT_ready, 1)
            for j in range(4):
                act.wait_ge(q_psum, j + 1)
                nc.scalar.activation(qT[:, 2 * j:2 * j + 2, :], bank[2 + j][:, :].rearrange("p (m q) -> p m q", m=2),
                                     ACT.Copy, scale=XD ** -0.5).then_inc(q_ready, 1)
            act.wait_ge(range_set, 1)
            n_blocks = act.value_load(rng_i[0:1, 1:2], min_val=1, max_val=NBLK)
            with act.Fori(0, n_blocks) as i:
                base = act.snap(i * XH)
                base8 = act.snap(i * 8)
                for j in range(8):
                    act.wait_ge(k_psum, base8 + (j + 1))
                    nc.scalar.copy(kT[:, j, :], bank[j % 4][:, :]).then_inc(k_ready, 1)

                def exps(h):
                    act.wait_ge(nm_ready, base + (h + 1))
                    if h >= 2:
                        act.wait_ge(pT_psum, 2 * base + 2 * (h - 1))
                    for t in range(TT):
                        nc.scalar.activation(prob[:, h % 2, t, :], bank[2 * (h % 2) + t][:, :], ACT.Exp,
                                             bias=nm_new[:, h, t:t + 1],
                                             accum_out=l_blk[:, h, t:t + 1]).then_inc(prob_ready, 1)
                    act.wait_ge(diff_ready, base + (h + 1))
                    nc.scalar.activation(alpha[:, h, :], m_diff[:, h, :], ACT.Exp).then_inc(alpha_ready, 1)

                def copy_pT(h):
                    act.wait_ge(pT_psum, 2 * base + (2 * h + 2))
                    if h >= 2:
                        act.wait_ge(o_psum, base + (h - 1))
                    nc.scalar.copy(probT[:, h % 2, 1, :], bank[5][:, :]).then_inc(pT_ready1, 1)

                for h in range(XH + 1):
                    if h < XH:
                        exps(h)
                    if h >= 1:
                        copy_pT(h - 1)
            for j in range(0, 4, 2):
                act.wait_ge(oT_psum, j + 1)
                nc.scalar.copy(oT[:, 2 * j:2 * j + 2, :],
                               bank[j][:, :].rearrange("p (m q) -> p m q", m=2)).then_inc(oT_ready, 1)

            rstd_by_exp(act, 3)
            act.wait_ge(xnT_psum, 2)
            nc.scalar.copy(xnT[:, 0, :], bank[0][:, 0:T]).then_inc(xnT_ready, 1)
            for m in range(4):
                act.wait_ge(qk2_psum, 3 + m // 2)
                ins = nc.scalar.activation(k2T[:, m, :], bank[4 + m // 2][:, (m % 2) * T:(m % 2 + 1) * T], ACT.Identity,
                                           bias=qk_bias[:, 4 + m:5 + m], scale=0.5).then_inc(k2_ready, 1)
            act.wait_ge(k2_ready, 4)
            nc.scalar.activation(k2sq, k2T, ACT.Square).then_inc(k2_ready, 1)
            for arg, ready, f in ((fq_arg, fq_ready, fq), (fk_arg, fk_ready, fk)):
                for t in range(TT):
                    act.wait_ge(arg, t + 1)
                    nc.scalar.activation(f[:, t, :, 0:LM], f[:, t, :, 0:LM], ACT.Exp).then_inc(ready, 1)

            def exps2(n):
                h = 4 * (n % 4) + n // 4
                act.wait_ge(s2_ready, n + 1)
                if n >= 2:
                    act.wait_ge(p2T_psum, n - 1)
                for t in range(TT):
                    nc.scalar.activation(p2[:, n % 2, t, :], s2[:, n % 2, t, :], ACT.Exp, scale=-1.0,
                                         bias=nm2[:, t, h:h + 1], accum_out=sum2[:, t, h:h + 1]).then_inc(p2_ready, 1)

            def copy_p2T(n):
                act.wait_ge(p2T_psum, n + 1)
                if n >= 2:
                    act.wait_ge(pv2_psum, n - 1)
                nc.scalar.copy(p2T[:, n % 2, :], bank[6 + n % 2][:, :]).then_inc(p2T_ready, 1)

            for n in range(LH + 1):
                if n < LH:
                    exps2(n)
                if n >= 1:
                    copy_p2T(n - 1)
            for k, into in ((0, 2), (1, 4)):
                act.wait_ge(fT_psum, 3 + k)
                nc.scalar.activation(fkT[:, 2 * k:2 * k + 2, :], bank[into][:, :].rearrange("p (c n) -> p c n", c=2),
                                     ACT.Copy, bias=1e-4).then_inc(fkT_ready, 1)
            act.wait_ge(gap_ready, 1)
            nc.scalar.activation(stat[:, 1], stat[:, 0], ACT.Exp, scale=-1.0).then_inc(gap_exp, 1)
            act.wait_ge(attT_psum, 1)
            nc.scalar.copy(attT[:, 0, :], bank[0][:, 0:T]).then_inc(attT_ready, 1)

            rstd_by_exp(act, 4)
            rstd_by_exp(act, 5)
            act.wait_ge(xnT_psum, 3)
            nc.scalar.activation(xnT[:, 0, :], bank[0][:, 0:T], ACT.Copy, scale=column("L0_ffn_norm_w", 0)
                                 ).then_inc(xnT_ready, 1)
            for b in range(ET // 2):
                act.wait_ge(down_psum, b + 1)
                nc.scalar.activation(hidden[:, 2 * b:2 * b + 2, :],
                                     bank[(6, 7, 0, 1)[b % 4]][:, :].rearrange("p (e t) -> p e t", e=2), ACT.Gelu
                                     ).then_inc(gelu_ready, 1)

            rstd_by_exp(act, 6)
            act.wait_ge(xnT_psum, 4)
            nc.scalar.copy(xnT[:, 0, :], bank[0][:, 0:T]).then_inc(xnT_ready, 1)
            act.wait_ge(qk4_psum, 1)
            nc.scalar.copy(qk_a, bank[3][:, 0:T]).then_inc(qk4_ready, 1)

            def exps4(u):
                t = u % TT
                act.wait_ge(nm4_ready, u + 1)
                if u >= 2:
                    act.wait_ge(p4T_psum, 2 * (u - 1))
                for half in range(2):
                    nc.scalar.activation(p4[:, u % 2, half * 512:(half + 1) * 512], bank[2 * (u % 2) + half][:, :],
                                         ACT.Exp, bias=nm4_new[:, t:t + 1], accum_out=sum4[:, u, half:half + 1]
                                         ).then_inc(p4_ready, 1)
                act.wait_ge(diff4_ready, u + 1)
                nc.scalar.activation(alpha4[:, u:u + 1], diff4[:, u:u + 1], ACT.Exp).then_inc(alpha4_ready, 1)

            def copy_p4T(u):
                act.wait_ge(p4T_psum, 2 * u + 1)
                if u >= 2:
                    act.wait_ge(o4_psum, u - 1)
                nc.scalar.copy(p4T[:, u % 2, 0:512], bank[4][:, :]).then_inc(p4T_ready0, 1)

            for u in range(UNITS + 1):
                if u < UNITS:
                    exps4(u)
                if u >= 1:
                    copy_p4T(u - 1)
            act.wait_ge(o4T_psum, 1)
            nc.scalar.copy(o4T_a, bank[0][:, 0:T]).then_inc(o4T_ready, 1)
            rstd_by_exp(act, 7)
            act.wait_ge(xnT_psum, 5)
            nc.scalar.copy(xnT[:, 0, :], bank[0][:, 0:T]).then_inc(xnT_ready, 1)
            act.wait_ge(qkv5_psum, 2)
            for m in range(DC):
                nc.scalar.activation(k5T[:, m, :], bank[4][:, m * T:(m + 1) * T], ACT.Identity,
                                     bias=column("L1_attn_bk", m)).then_inc(qkv5_ready, 1)
            for t in range(TT):
                act.wait_ge(s5_ready, t + 1)
                nc.scalar.activation(p5[:, t, :], s5[:, t, :], ACT.Exp, scale=-1.0, bias=nm4_new[:, t:t + 1],
                                     accum_out=l4[:, t:t + 1]).then_inc(p5_ready, 1)
            act.wait_ge(attT_psum, 3)
            nc.scalar.copy(attT[:, 0, :], bank[2][:, 0:T]).then_inc(attT_ready, 1)
            rstd_by_exp(act, 8)
            act.wait_ge(xnT_psum, 6)
            nc.scalar.copy(xnT[:, 0, :], bank[0][:, 0:T]).then_inc(xnT_ready, 1)
            act.wait_ge(router_psum, 1)
            nc.scalar.activation(r6[:, 0, :, 0:MOE], bank[2][:, 0:TT * MOE].rearrange("p (t e) -> p t e", t=TT),
                                 ACT.Exp, scale=-1.0).then_inc(router_exp, 1)
            for m in range(FT):
                n = min(P, FALL - m * P)
                act.wait_ge(gate_psum, m + 1)
                if m >= 2:
                    act.wait_ge(h6_ready, m - 1)
                nc.scalar.activation(silu6[0:n, m % 2, :], bank[3 + m % 2][0:n, 0:T], ACT.Silu).then_inc(silu_ready, 1)

        @block.vector
        def _(dve):
            step = Chain(dve, dve_step)
            nc.vector.memset(ones[:, :], 1.0).then_inc(consts_set, 1)
            nc.vector.memset(nm_run[:, :, :], -2 * MASKED).then_inc(consts_set, 1)
            nc.vector.memset(l_run[:, :, :], 0.0).then_inc(ctx_free, 1)
            step(nc.vector.memset(o_acc, 0.0))
            dve.wait_ge(small_in, 80)
            nc.vector.tensor_copy(ident_h[:, :], ident[:, :]).then_inc(consts_set, 1)
            dve.wait_ge(x_in, 16)
            layer_norm(dve, step, x_res, xn)
            layer_norm(dve, step, xn, xn, after=xn_ready)
            dve.wait_ge(mask_in, 16)
            step(nc.vector.tensor_reduce(seen[:, :, :],
                                         mask_w.bitcast(U32).rearrange("p (t b w) -> p t b w", t=TT, b=NBLK),
                                         AX.X, ALU.max))
            step(nc.vector.tensor_scalar(seen[:, :, :], seen[:, :, :], 1.0, None, ALU.min))
            nc.vector.tensor_reduce(any_q[:, :], seen[:, :, :], AX.X, ALU.max).then_inc(blocks_seen, 1)
            dve.wait_ge(xnT_psum, 1)
            nc.vector.tensor_scalar(xnT[:, 1, :], bank[7][:, 0:T], column("L0_xattn_ln_gamma", 1), column("L0_xattn_ln_beta", 1),
                                    ALU.mult, ALU.add).then_inc(xnT_ready, 1)
            dve.wait_ge(blocks_counted, 1)
            r = [rng[:, k * NBLK:(k + 1) * NBLK] for k in range(8)]
            nc.vector.tensor_copy(rng[:, 0:2 * NBLK], bank[0][0:1, 0:2 * NBLK]).then_inc(dve_step, 1)
            step.n += 1
            dve.wait_ge(dve_step, step.n)
            step(nc.vector.tensor_tensor(r[2], r[0], r[1], ALU.add))
            step(nc.vector.tensor_scalar(r[2], r[2], 1.0, None, ALU.min))
            step(nc.vector.tensor_tensor(r[3], r[2], blk_lo[:, :], ALU.mult))
            step(nc.vector.tensor_tensor(r[4], r[2], blk_hi[:, :], ALU.mult))
            step(nc.vector.tensor_reduce(r[5][:, 0:1], r[3], AX.X, ALU.min))
            step(nc.vector.tensor_reduce(r[5][:, 1:2], r[4], AX.X, ALU.max))
            step(nc.vector.tensor_scalar(r[6][:, 0:1], r[5][:, 0:1], float(NBLK), float(NBLK - 1), ALU.add, ALU.min))
            step(nc.vector.tensor_tensor(r[6][:, 1:2], r[5][:, 1:2], r[6][:, 0:1], ALU.subtract))
            step(nc.vector.tensor_scalar(r[6][:, 1:2], r[6][:, 1:2], 1.0, None, ALU.max))
            nc.vector.tensor_copy(rng_i[:, :], r[6][:, 0:2]).then_inc(range_set, 1)
            dve.wait_ge(range_set, 1)
            first = dve.value_load(rng_i[0:1, 0:1], min_val=0, max_val=NBLK - 1)
            n_blocks = dve.value_load(rng_i[0:1, 1:2], min_val=1, max_val=NBLK)
            for k in range(4):
                dve.wait_ge(wsim_psum, k + 1)
                nc.vector.tensor_copy(w_sim[:, k // 2, (k % 2) * 512:(k % 2 + 1) * 512], bank[(0, 1, 6, 7)[k]][:, :]
                                      ).then_inc(wsim_ready, 1)
            mask_b = mask_w.bitcast(U8).rearrange("p (t k) -> p t k", t=TT)
            with dve.Fori(0, n_blocks) as i:
                base = dve.snap(i * XH)
                base8 = dve.snap(i * 8)
                at = within(dve, first + i) * BLK
                nc.vector.tensor_scalar(bias_h[:, :, :], mask_b[:, :, bass.ds(at, BLK)], -1.0, -MASKED,
                                        ALU.add, ALU.mult).then_inc(bias_ready, 1)
                for j in range(8):
                    dve.wait_ge(v_psum, base8 + (j + 1))
                    nc.vector.tensor_copy(v_blk[:, j // 2, (j % 2) * 512:(j % 2 + 1) * 512],
                                          bank[j % 4][:, :]).then_inc(v_ready, 1)

                def maxima(h):
                    dve.wait_ge(s_ready, base + (h + 1))
                    for t in range(TT):
                        ins = nc.vector.tensor_reduce(nm_blk[:, h, t:t + 1], bank[2 * (h % 2) + t][:, :], AX.X,
                                                      ALU.max, negate=True)
                    ins.then_inc(nm_blk_ready, 1)
                    dve.wait_ge(nm_blk_ready, base + (h + 1))
                    nc.vector.tensor_tensor(nm_new[:, h, :], nm_blk[:, h, :], nm_run[:, h, :],
                                            ALU.min).then_inc(nm_ready, 1)
                    dve.wait_ge(nm_ready, base + (h + 1))
                    nc.vector.tensor_tensor(m_diff[:, h, :], nm_new[:, h, :], nm_run[:, h, :],
                                            ALU.subtract).then_inc(diff_ready, 1)

                def copy_pT(h):
                    dve.wait_ge(pT_psum, 2 * base + (2 * h + 1))
                    if h >= 2:
                        dve.wait_ge(o_psum, base + (h - 1))
                    nc.vector.tensor_copy(probT[:, h % 2, 0, :], bank[4][:, :]).then_inc(pT_ready0, 1)

                def add_values(h):
                    dve.wait_ge(o_psum, base + (h + 1))
                    dve.wait_ge(alpha_ready, base + (h + 1))
                    for t in range(TT):
                        o = o_acc[:, t, h * XD:(h + 1) * XD]
                        ins = nc.vector.scalar_tensor_tensor(o, o, alpha[:, h, t:t + 1],
                                                             bank[6 + h % 2][:, t * XD:(t + 1) * XD],
                                                             ALU.mult, ALU.add)
                    ins.then_inc(o_added, 1)

                for h in range(XH + 2):
                    if h < XH:
                        maxima(h)
                    if 1 <= h <= XH:
                        copy_pT(h - 1)
                    if h >= 2:
                        add_values(h - 2)
                nc.vector.tensor_tensor(l_run[:, :, :], l_run[:, :, :], alpha[:, :, :], ALU.mult).then_inc(l_scaled, 1)
                dve.wait_ge(l_scaled, i + 1)
                nc.vector.tensor_tensor(l_run[:, :, :], l_run[:, :, :], l_blk[:, :, :], ALU.add)
                nc.vector.tensor_copy(nm_run[:, :, :], nm_new[:, :, :]).then_inc(run_kept, 1)
                dve.wait_ge(run_kept, i + 1)
            step(nc.vector.reciprocal(is_row[:, :], any_q[:, :]))
            step(nc.vector.tensor_tensor(is_row[:, :], is_row[:, :], any_q[:, :], ALU.mult))
            step(nc.vector.reciprocal(l_run[:, :, :], l_run[:, :, :]))
            for t in range(TT):
                ins = nc.vector.tensor_scalar(l_blk[:, :, t], l_run[:, :, t], is_row[:, t:t + 1], None, ALU.mult)
            step(ins)
            for t in range(TT):
                o = o_acc[:, t, :].rearrange("p (h d) -> p h d", h=XH)
                ins = nc.vector.tensor_tensor(o, o, l_blk[:, :, t].unsqueeze(2).to_broadcast([P, XH, XD]), ALU.mult)
            ins.then_inc(o_normed, 1)
            for j in range(1, 4, 2):
                dve.wait_ge(oT_psum, j + 1)
                nc.vector.tensor_copy(oT[:, 2 * j:2 * j + 2, :],
                                      bank[j][:, :].rearrange("p (m q) -> p m q", m=2)).then_inc(oT_ready, 1)
            dve.wait_ge(y_psum, 1)
            nc.vector.tensor_tensor(x_res[:, :, :], x_res[:, :, :],
                                    bank[4][:, :].rearrange("p (t d) -> p t d", t=TT), ALU.add).then_inc(x_ready, 1)
            dve.wait_ge(x_ready, 1)

            layer_norm(dve, step, x_res, xn, after=xn_ready)
            nc.vector.memset(v2[:, :, :, 16:17], 1.0)
            nc.vector.memset(part(region_a, 4096, 2048), 0.0)
            dve.wait_ge(lin_in, 128)
            step(nc.vector.tensor_scalar(qk_bias[:, :], qk_bias[:, :], 0.5, None, ALU.mult))
            dve.wait_ge(xnT_psum, 2)
            nc.vector.tensor_copy(xnT[:, 1, :], bank[1][:, 0:T]).then_inc(xnT_ready, 1)
            for m in range(4):
                dve.wait_ge(qk2_psum, 1 + m // 2)
                nc.vector.tensor_scalar(q2T[:, m, :], bank[2 + m // 2][:, (m % 2) * T:(m % 2 + 1) * T], 0.5,
                                        qk_bias[:, m:m + 1], ALU.mult, ALU.add).then_inc(q2_ready, 1)
            dve.wait_ge(q2_ready, 4)
            nc.vector.tensor_tensor(q2sq, q2T, q2T, ALU.mult).then_inc(q2_ready, 1)
            dve.wait_ge(v2_psum, 1)
            nc.vector.tensor_copy(v2[:, :, :, 0:16], bank[6][:, :].rearrange("p (t h d) -> p t h d", t=TT, h=LH)
                                  ).then_inc(v2_ready, 1)

            def features(b):
                return bank[b][:, :].rearrange("p (h m) -> p h m", h=LH)[:, :, 0:LM]

            for t in range(TT):
                dve.wait_ge(fq_psum, t + 1)
                step(nc.vector.tensor_reduce(q_ls[:, t, :], features(t), AX.X, ALU.max))
                nc.vector.tensor_tensor(fq[:, t, :, 0:LM], features(t),
                                        q_ls[:, t, :].unsqueeze(2).to_broadcast([P, LH, LM]), ALU.subtract
                                        ).then_inc(fq_arg, 1)
            for t in range(TT):
                dve.wait_ge(fk_psum, t + 1)
                ins = nc.vector.tensor_reduce(k_ls[:, t, :], features(2 + t), AX.X, ALU.max)
            step(ins)
            nc.vector.tensor_tensor(k_max[:, :], k_ls[:, 0, :], k_ls[:, 1, :], ALU.max).then_inc(k_maxed, 1)
            dve.wait_ge(k_stab_ready, 1)
            for t in range(TT):
                nc.vector.tensor_tensor(fk[:, t, :, 0:LM], features(2 + t),
                                        k_stab[:, :].unsqueeze(2).to_broadcast([P, LH, LM]), ALU.subtract
                                        ).then_inc(fk_arg, 1)
            for n in range(LH):
                h = 4 * (n % 4) + n // 4
                dve.wait_ge(s2_psum, n + 1)
                if n >= 2:
                    dve.wait_ge(p2_ready, 2 * n - 2)
                for t in range(TT):
                    ins = nc.vector.tensor_tensor_reduce(s2[:, n % 2, t, :], bank[4 + n % 2][:, t * T:(t + 1) * T],
                                                         band[:, t, :], -1.0, 3e38, ALU.add, ALU.min,
                                                         accum_out=nm2[:, t, h:h + 1])
                ins.then_inc(s2_ready, 1)
            for k in range(2):
                dve.wait_ge(fT_psum, 1 + k)
                nc.vector.tensor_scalar(fqT[:, 2 * k:2 * k + 2, :], bank[k][:, :].rearrange("p (c n) -> p c n", c=2),
                                        1e-4, None, ALU.add).then_inc(fqT_ready, 1)
            step(nc.vector.tensor_tensor(stat[:, 0], nm2[:, :, :], q_ls[:, :, :], ALU.add))
            for t in range(TT):
                ins = nc.vector.tensor_tensor(stat[:, 0, t], stat[:, 0, t], k_stab[:, :], ALU.add)
            ins.then_inc(gap_ready, 1)
            for g in range(4):
                own = (5, 6, 7) if g % 2 == 0 else (0, 1, 2)
                for k in range(2):
                    dve.wait_ge(mix_psum, 3 * g + k + 1)
                    nc.vector.tensor_tensor(mixed0[:, 4 * g + 2 * k:4 * g + 2 * k + 2, :],
                                            bank[own[k]][:, :].rearrange("p (h i) -> p h i", h=2),
                                            mixT[:, 0:T].unsqueeze(1).to_broadcast([P, 2, T]), ALU.mult
                                            ).then_inc(mix_ready, 1)
                dve.wait_ge(mix_psum, 3 * g + 3)
                nc.vector.tensor_tensor(mixed1[:, 4 * g:4 * g + 4, :],
                                        bank[own[2]][:, :].rearrange("p (h i) -> p h i", h=4),
                                        mixT[:, T:T + P].unsqueeze(1).to_broadcast([P, 4, P]), ALU.mult
                                        ).then_inc(mix_ready, 1)
            dve.wait_ge(gap_exp, 1)
            dve.wait_ge(p2_ready, 2 * LH)
            step(nc.vector.tensor_tensor(stat[:, 1], stat[:, 1], sum2[:, :, :], ALU.mult))
            nc.vector.reciprocal(stat[:, 3], sum2[:, :, :])
            dve.wait_ge(pv2_psum, LH)
            dve.wait_ge(hv_psum, 1)
            for t in range(TT):
                ins = nc.vector.tensor_copy(lin[:, t], bank[4 + t][:, 0:LH * 17].rearrange("p (h d) -> p h d", h=LH))
            step(ins)
            step(nc.vector.tensor_scalar(stat[:, 2], lin[:, :, :, 16], 1e-24, None, ALU.max))
            step(nc.vector.tensor_tensor(stat[:, 2], stat[:, 2], stat[:, 1], ALU.add))
            step(nc.vector.reciprocal(stat[:, 2], stat[:, 2]))

            def per_head(k, t):
                return stat[:, k, t].unsqueeze(2).to_broadcast([P, LH, 16])

            for t in range(TT):
                nc.vector.tensor_tensor(att[:, t], bank[3][:, t * D:(t + 1) * D].rearrange("p (h d) -> p h d", h=LH),
                                        per_head(3, t), ALU.mult)
                ins = nc.vector.tensor_tensor(lin[:, t, :, 0:16], lin[:, t, :, 0:16], per_head(2, t), ALU.mult)
            step(ins)
            for t in range(TT):
                ins = nc.vector.tensor_tensor(att[:, t], att[:, t], lin[:, t, :, 0:16], ALU.add)
            ins.then_inc(att_ready, 1)
            dve.wait_ge(attT_psum, 2)
            nc.vector.tensor_copy(attT[:, 1, :], bank[1][:, 0:T]).then_inc(attT_ready, 1)
            dve.wait_ge(y_psum, 2)
            nc.vector.tensor_tensor(x_res[:, :, :], x_res[:, :, :],
                                    bank[2][:, :].rearrange("p (t d) -> p t d", t=TT), ALU.add).then_inc(x_ready, 1)
            dve.wait_ge(x_ready, 2)

            layer_norm(dve, step, x_res, xn)
            for t in range(TT):
                ins = nc.vector.tensor_tensor_reduce(squares[:, t], xn[:, t], xn[:, t], 1.0, 0.0, ALU.mult, ALU.add,
                                                     accum_out=mv[:, t, 1:2])
            step(ins)
            nc.vector.tensor_scalar(var[:, :], mv[:, :, 1], 1.0 / D, EPS_OF_NORM[norms[0]], ALU.mult, ALU.add
                                    ).then_inc(var_ready, 1)
            norms[0] += 1
            dve.wait_ge(rstd_ready, norms[0])
            refine_rstd(dve, step)
            for t in range(TT):
                nc.vector.tensor_scalar(xn[:, t], xn[:, t], rstd[:, t:t + 1], None, ALU.mult).then_inc(xn_ready, 1)
            dve.wait_ge(xnT_psum, 3)
            nc.vector.tensor_scalar(xnT[:, 1, :], bank[1][:, 0:T], column("L0_ffn_norm_w", 1), None, ALU.mult
                                    ).then_inc(xnT_ready, 1)
            dve.wait_ge(iota_in, 16)
            nc.vector.tensor_copy(iota_h, iota.unsqueeze(2).to_broadcast([P, P, GS]))
            for t in range(TT):
                for half in range(2):
                    dve.wait_ge(sim_psum, 2 * t + half + 1)
                    sims = [bank[2 + 2 * t + half][:, k * NK:(k + 1) * NK] for k in range(EH)]
                    for k in range(EH):
                        ins = nc.vector.max(top[:, t, half * EH + k, :], sims[k])
                    step(ins)
                    for k in range(EH):
                        ins = nc.vector.max_index(top_i[:, t, half * EH + k, :], top[:, t, half * EH + k, :], sims[k])
            step(ins)
            nc.vector.tensor_copy(top_f, top_i)
            sided = top.rearrange("p t (h s) k -> p t h s k", s=2)
            for t in range(TT):
                ins = nc.vector.tensor_tensor(pairs[:, t].rearrange("p h (a b) -> p h a b", a=8),
                                              sided[:, t, :, 0, :].unsqueeze(3).to_broadcast([P, EH, 8, 8]),
                                              sided[:, t, :, 1, :].unsqueeze(2).to_broadcast([P, EH, 8, 8]), ALU.add)
            step(ins)
            for t in range(TT):
                for h in range(EH):
                    ins = nc.vector.max(best[:, t, h * 8:(h + 1) * 8], pairs[:, t, h, :])
            step(ins)
            for t in range(TT):
                for h in range(EH):
                    ins = nc.vector.max_index(best_i[:, t, h * 8:(h + 1) * 8], best[:, t, h * 8:(h + 1) * 8],
                                              pairs[:, t, h, :])
            step(ins)
            nc.vector.tensor_scalar(chosen[:, 2, :], best.rearrange("p t k -> p (t k)"), 0.0, None, ALU.max
                                    ).then_inc(chosen_ready, 1)
            nc.vector.tensor_scalar(rank_i[:, 0], best_i, 3, None, ALU.logical_shift_right)
            step(nc.vector.tensor_scalar(rank_i[:, 1], best_i, 7, None, ALU.bitwise_and))
            step(nc.vector.tensor_copy(rank, rank_i))
            for k in range(2):
                for t in range(TT):
                    step(nc.vector.tensor_tensor(pick, rank[:, k, t, :].unsqueeze(2).to_broadcast([P, 64, 8]),
                                                 iota[:, 0:8].unsqueeze(1).to_broadcast([P, 64, 8]), ALU.is_equal))
                    keys = top_f[:, t].rearrange("p (h s) k -> p h s k", s=2)[:, :, k, :]
                    picked = pick.rearrange("p (h k) j -> p h k j", h=EH)
                    step(nc.vector.tensor_tensor(picked, picked, keys.unsqueeze(2).to_broadcast([P, EH, 8, 8]),
                                                 ALU.mult))
                    step(nc.vector.tensor_reduce(side[:, k, t, :], pick, AX.X, ALU.add))
            step(nc.vector.scalar_tensor_tensor(expert, side[:, 0], float(NK), side[:, 1], ALU.mult, ALU.add))
            step(nc.vector.tensor_copy(expert_i, expert))
            nc.vector.tensor_scalar(split_i[:, 0], expert_i, P - 1, None, ALU.bitwise_and)
            step(nc.vector.tensor_scalar(split_i[:, 1], expert_i, 7, None, ALU.logical_shift_right))
            for k in range(2):
                nc.vector.tensor_copy(chosen[:, k, :], split_i[:, k].rearrange("p t k -> p (t k)")
                                      ).then_inc(chosen_ready, 1)
            dve.wait_ge(chosenT_psum, 1)
            step(nc.vector.tensor_copy(chosenT, bank[2][:, 0:3 * P].rearrange("p (s n) -> p s n", s=3)))
            for k in range(2):
                nc.vector.memset(stat[:, k, 0, 1:2], 0.0).then_inc(hidden_ready, 1)
            nc.vector.tensor_copy(chosen_h[:, 0:2], chosenT[:, 0:2])
            step(nc.vector.tensor_copy(chosen_h[:, 2], chosenT[:, 2]))
            step(nc.vector.tensor_tensor(rest_w, chosenT[:, 2], chosen_h[:, 2], ALU.subtract))
            step(nc.vector.tensor_copy(chosen_h[:, 3], rest_w))
            step(nc.vector.tensor_tensor(chosen_h[:, 4], rest_w, chosen_h[:, 3], ALU.subtract))

            def one_hots(g, n, at):
                def over(k, size):
                    return chosen_h[:, k, bass.ds(at, GS)].unsqueeze(1).to_broadcast([P, size, GS])

                nc.vector.tensor_tensor(hit_hi[:, g], iota_h[:, 0:ET], over(1, ET), ALU.is_equal).then_inc(hit_ready, 1)
                nc.vector.tensor_tensor(hot_lo[:, g], iota_h, over(0, P), ALU.is_equal)
                dve.wait_ge(hit_ready, n)
                for w in range(3):
                    ins = nc.vector.tensor_tensor(hot_hi[:, g, w], hit_hi[:, g], over(2 + w, ET), ALU.mult)
                ins.then_inc(hot_ready, 1)

            def weigh(g, n, at):
                dve.wait_ge(mixw_psum, n)
                for t in range(TT):
                    own = hidden[:, :, bass.ds(at + t * P, GS)]
                    ins = nc.vector.tensor_tensor(own, bank[2 + 2 * g + t][:, :].rearrange("p (h s) -> p h s", h=ET),
                                                  own, ALU.mult)
                ins.then_inc(hidden_ready, 1)

            one_hots(0, 1, 0)
            dve.wait_ge(gelu_ready, ET // 2)
            with dve.Fori(0, P // GS // 2 - 1) as i:
                two, at = dve.snap(i * 2), dve.snap(i * (2 * GS))
                one_hots(1, two + 2, at + GS)
                weigh(0, two + 1, at)
                one_hots(0, two + 3, at + 2 * GS)
                weigh(1, two + 2, at + GS)
            one_hots(1, P // GS, P - GS)
            weigh(0, P // GS - 1, P - 2 * GS)
            weigh(1, P // GS, P - GS)
            dve.wait_ge(y_psum, 3)
            nc.vector.tensor_tensor(x_res[:, :, :], x_res[:, :, :],
                                    bank[6][:, :].rearrange("p (t d) -> p t d", t=TT), ALU.add).then_inc(x_ready, 1)
            dve.wait_ge(x_ready, 3)

            layer_norm(dve, step, x_res, xn, after=xn_ready)
            dve.wait_ge(down_psum, ET // 2)
            nc.vector.memset(ctxT_b[CD - P:CD - P + 1], 1.0).then_inc(ones4_set, 1)
            nc.vector.memset(o4T_b[CD - P:CD - P + 1], 1.0).then_inc(ones4_set, 1)
            nc.vector.memset(nm4_run[:, :], 3e38)
            nc.vector.memset(l4[:, :], 0.0)
            step(nc.vector.memset(o4, 0.0))
            dve.wait_ge(xnT_psum, 4)
            nc.vector.tensor_copy(xnT[:, 1, :], bank[1][:, 0:T]).then_inc(xnT_ready, 1)
            dve.wait_ge(q4_psum, 1)
            for m in range(DC):
                nc.vector.tensor_scalar(q4T[:, m, :], bank[2][:, m * T:(m + 1) * T], column("L1_xattn_bq", m), None,
                                        ALU.add).then_inc(q4_ready, 1)
            dve.wait_ge(qk4_psum, 2)
            nc.vector.tensor_copy(qk_b, bank[4][0:CD - P + 1, 0:T]).then_inc(qk4_ready, 1)

            def maxima4(u):
                t = u % TT
                dve.wait_ge(s4_psum, u + 1)
                for half in range(2):
                    ins = nc.vector.tensor_reduce(nm4_half[:, t, half:half + 1], bank[2 * (u % 2) + half][:, :], AX.X,
                                                  ALU.max, negate=True)
                step(ins)
                nc.vector.scalar_tensor_tensor(nm4_new[:, t:t + 1], nm4_half[:, t, 0:1], nm4_run[:, t:t + 1],
                                               nm4_half[:, t, 1:2], ALU.min, ALU.min).then_inc(nm4_ready, 1)
                dve.wait_ge(nm4_ready, u + 1)
                nc.vector.tensor_tensor(diff4[:, u:u + 1], nm4_new[:, t:t + 1], nm4_run[:, t:t + 1], ALU.subtract
                                        ).then_inc(diff4_ready, 1)
                dve.wait_ge(diff4_ready, u + 1)
                step(nc.vector.tensor_copy(nm4_run[:, t:t + 1], nm4_new[:, t:t + 1]))

            def copy_p4T(u):
                dve.wait_ge(p4T_psum, 2 * u + 2)
                if u >= 2:
                    dve.wait_ge(o4_psum, u - 1)
                nc.vector.tensor_copy(p4T[:, u % 2, 512:1024], bank[5][:, :]).then_inc(p4T_ready1, 1)

            def add_values4(u):
                t = u % TT
                dve.wait_ge(o4_psum, u + 1)
                dve.wait_ge(alpha4_ready, u + 1)
                nc.vector.scalar_tensor_tensor(o4[:, t, :], o4[:, t, :], alpha4[:, u:u + 1], bank[6 + u % 2][:, 0:CD],
                                               ALU.mult, ALU.add).then_inc(o4_added, 1)

            def add_sums4(u):
                t = u % TT
                dve.wait_ge(alpha4_ready, u + 1)
                step(nc.vector.scalar_tensor_tensor(l4[:, t:t + 1], l4[:, t:t + 1], alpha4[:, u:u + 1],
                                                    sum4[:, u, 0:1], ALU.mult, ALU.add))
                step(nc.vector.tensor_tensor(l4[:, t:t + 1], l4[:, t:t + 1], sum4[:, u, 1:2], ALU.add))

            for u in range(UNITS + 2):
                if u < UNITS:
                    maxima4(u)
                if 1 <= u <= UNITS:
                    copy_p4T(u - 1)
                if u >= 2:
                    add_values4(u - 2)
                if 1 <= u <= UNITS:
                    add_sums4(u - 1)
            step(nc.vector.reciprocal(l4[:, :], l4[:, :]))
            dve.wait_ge(o4_added, UNITS)
            for t in range(TT):
                nc.vector.tensor_scalar(o4[:, t, :], o4[:, t, :], l4[:, t:t + 1], None, ALU.mult).then_inc(o4_normed, 1)
            dve.wait_ge(o4T_psum, 2)
            nc.vector.tensor_copy(o4T_b[0:CD - P], bank[1][0:CD - P, 0:T]).then_inc(o4T_ready, 1)
            dve.wait_ge(y_psum, 4)
            nc.vector.tensor_tensor(x_res[:, :, :], x_res[:, :, :],
                                    bank[2][:, :].rearrange("p (t d) -> p t d", t=TT), ALU.add).then_inc(x_ready, 1)
            dve.wait_ge(x_ready, 4)
            layer_norm(dve, step, x_res, xn, after=xn_ready)
            dve.wait_ge(xnT_psum, 5)
            nc.vector.tensor_copy(xnT[:, 1, :], bank[1][:, 0:T]).then_inc(xnT_ready, 1)
            dve.wait_ge(qkv5_psum, 1)
            for m in range(DC):
                nc.vector.tensor_scalar(q5T[:, m, :], bank[3][:, m * T:(m + 1) * T], column("L1_attn_bq", m),
                                        D ** -0.5, ALU.add, ALU.mult).then_inc(qkv5_ready, 1)
            dve.wait_ge(qkv5_psum, 3)
            nc.vector.tensor_copy(v5, bank[5][:, :].rearrange("p (t n) -> p t n", t=TT)).then_inc(v5_ready, 1)
            dve.wait_ge(masks5_in, 32)
            for t in range(TT):
                dve.wait_ge(s5_psum, t + 1)
                step(nc.vector.tensor_tensor(s5[:, t], bank[6 + t][:, 0:T], keep5[:, t], ALU.mult))
                nc.vector.tensor_tensor_reduce(s5[:, t], s5[:, t], fill5[:, t], -1.0, 3e38, ALU.add, ALU.min,
                                               accum_out=nm4_new[:, t:t + 1]).then_inc(s5_ready, 1)
            dve.wait_ge(p5T_psum, 1)
            nc.vector.tensor_copy(p5T, bank[0][:, :]).then_inc(p5T_ready, 1)
            step(nc.vector.reciprocal(l4[:, :], l4[:, :]))
            dve.wait_ge(o5_psum, 1)
            for t in range(TT):
                ins = nc.vector.tensor_scalar(att_flat[:, t], bank[1][:, t * D:(t + 1) * D], l4[:, t:t + 1], None, ALU.mult)
            ins.then_inc(att_ready, 1)
            dve.wait_ge(attT_psum, 4)
            nc.vector.tensor_copy(attT[:, 1, :], bank[3][:, 0:T]).then_inc(attT_ready, 1)
            dve.wait_ge(y_psum, 5)
            nc.vector.tensor_tensor(x_res[:, :, :], x_res[:, :, :],
                                    bank[4][:, :].rearrange("p (t d) -> p t d", t=TT), ALU.add).then_inc(x_ready, 1)
            dve.wait_ge(x_ready, 5)
            layer_norm(dve, step, x_res, xn, after=xn_ready)
            nc.vector.memset(r6[:, 5, :, MOE:MOE + 1], 1.0)
            dve.wait_ge(moe_small_in, 64)
            dve.wait_ge(xnT_psum, 6)
            nc.vector.tensor_copy(xnT[:, 1, :], bank[1][:, 0:T]).then_inc(xnT_ready, 1)
            dve.wait_ge(router_exp, 1)
            score, biased, best2, chosen1, weight = (r6[:, k, :, 0:MOE] for k in (0, 1, 2, 3, 5))
            step(nc.vector.tensor_scalar(score, score, 1.0, None, ALU.add))
            step(nc.vector.reciprocal(score, score))
            step(nc.vector.tensor_tensor(biased, score, ebias6.unsqueeze(1).to_broadcast([P, TT, MOE]), ALU.add))
            for t in range(TT):
                ins = nc.vector.max(best2[:, t], biased[:, t])
            step(ins)
            for t in range(TT):
                ins = nc.vector.max_index(r6_i[:, t], best2[:, t], biased[:, t])
            step(ins)
            step(nc.vector.tensor_copy(best2, r6_i[:, :, :]))
            for t in range(TT):
                ins = nc.vector.tensor_scalar(chosen1[:, t], iota6, best2[:, t, 0:1], None, ALU.is_equal)
            step(ins)
            for t in range(TT):
                ins = nc.vector.scalar_tensor_tensor(chosen1[:, t], iota6, best2[:, t, 1:2], chosen1[:, t],
                                                     ALU.is_equal, ALU.add)
            step(ins)
            step(nc.vector.tensor_tensor(chosen1, chosen1, score, ALU.mult))
            step(nc.vector.tensor_reduce(r6_s[:, :], chosen1, AX.X, ALU.add))
            step(nc.vector.tensor_scalar(r6_s[:, :], r6_s[:, :], 1e-20, None, ALU.add))
            step(nc.vector.reciprocal(r6_s[:, :], r6_s[:, :]))
            for t in range(TT):
                ins = nc.vector.tensor_scalar(weight[:, t], chosen1[:, t], r6_s[:, t:t + 1], None, ALU.mult)
            ins.then_inc(w6_ready, 1)
            dve.wait_ge(w6T_psum, 1)
            nc.vector.tensor_copy(w6T, bank[2][0:MOE + 1, 0:T]).then_inc(w6T_ready, 1)
            for m in range(FT):
                n = min(P, FALL - m * P)
                dve.wait_ge(up6_psum, m + 1)
                dve.wait_ge(silu_ready, m + 1)
                step(nc.vector.tensor_tensor(h6[0:n, m, :], bank[5 + m % 2][0:n, 0:T], silu6[0:n, m % 2, :], ALU.mult))
                nc.vector.tensor_tensor(h6[0:n, m, :], bank[5 + m % 2][0:n, T:2 * T], h6[0:n, m, :], ALU.mult
                                        ).then_inc(h6_ready, 1)
            dve.wait_ge(y_psum, 6)
            for t in range(TT):
                ins = nc.vector.tensor_tensor(x_res[:, t], x_res[:, t], bank[(7, 0)[t]][:, 0:D], ALU.add)
            ins.then_inc(x_ready, 1)

        @block.gpsimd
        def _(pool):
            pool.wait_ge(k_maxed, 1)
            nc.gpsimd.partition_all_reduce(k_stab[:, :], k_max[:, :], P, bass.bass_isa.ReduceOp.max
                                           ).then_inc(k_stab_ready, 1)


def by_tile(m):
    return m.astype(np.float32).reshape(TT, P, T).transpose(1, 0, 2).reshape(P, -1)


def laid_out(i):
    f = {k: np.asarray(v) for k, v in i.items()}
    f["L0_attn_v_b"] = f["L0_attn_Wqkv_b"][2 * D:]
    wqk = np.zeros((D, 2 * LH, 32), np.float32)
    wqk[:, :, :16] = f["L0_attn_Wqkv_w"][:2 * D].T.reshape(D, 2 * LH, 16)
    bqk = np.zeros((2 * LH, 32), np.float32)
    bqk[:, :16] = f["L0_attn_Wqkv_b"][:2 * D].reshape(2 * LH, 16)
    proj, minus_half = np.zeros((4, 32, 4, 32), np.float32), np.zeros((4, 32, 4, 32), np.float32)
    for g in range(4):
        proj[g, :16, g, :LM] = f["L0_attn_proj"].T
        minus_half[g, :16, g, :LM] = -0.5
    query, key = np.arange(T)[:, None], np.arange(T)[None, :]
    window = (key <= query) & (key >= query - 128)
    mixT = ((key <= query) - 0.25 * window).T.astype(np.float32)
    a = {
        "x": f["x"].reshape(T, D),
        "ctxT": np.ascontiguousarray(f["ctx_768"][0].T),
        "mask": np.ascontiguousarray(f["mask_1x1xSxS2_bk0"].reshape(T, S2)).view(np.uint32),
        "columns": np.concatenate([f[n].reshape(-1, P).T for n in COLUMNS], axis=1),
        "rows": np.concatenate([f[n] for n in ROWS])[None],
        "Wq": f["L0_xattn_Wq"], "Wkv": f["L0_xattn_Wkv"], "Wo": f["L0_xattn_Wo"],
        "wqk2": wqk.reshape(D, -1), "wv2": np.ascontiguousarray(f["L0_attn_Wqkv_w"][2 * D:].T),
        "wo2": np.ascontiguousarray(f["L0_attn_out_w"].T), "qk_bias": np.ascontiguousarray(bqk.reshape(8, P).T),
        "proj": proj.reshape(P, P),
        "w_q": f["L0_ffn_w_q"], "keysT": np.ascontiguousarray(f["L0_ffn_keys"].transpose(3, 0, 2, 1).reshape(P, -1)),
        "downT": np.ascontiguousarray(f["L0_ffn_expert_down"].T), "up": f["L0_ffn_expert_up"],
        "ctx": f["ctx_768"][0], "wq4": f["L1_xattn_Wq"],
        "wk4T": np.concatenate([f["L1_xattn_Wk"].T, f["L1_xattn_bk"][:, None]], axis=1),
        "wv4": np.concatenate([f["L1_xattn_Wv"], f["L1_xattn_bv"][None]], axis=0),
        "wq5": f["L1_attn_wq"], "wk5": f["L1_attn_wk"], "wv5": f["L1_attn_wv"], "wo5": f["L1_attn_wo"],
        "wr6": f["L1_ffn_W_gate_router"], "ebias6": f["L1_ffn_expert_bias"],
        "wg6": np.concatenate([f["L1_ffn_Wg"].transpose(1, 0, 2).reshape(D, -1), f["L1_ffn_Wg_s"]], axis=1),
        "wu6": np.concatenate([f["L1_ffn_Wu"].transpose(1, 0, 2).reshape(D, -1), f["L1_ffn_Wu_s"]], axis=1),
        "wd6": np.concatenate([f["L1_ffn_Wd"].reshape(-1, D), f["L1_ffn_Wd_s"]], axis=0),
        "keep5": by_tile(key > query + 1), "fill5": by_tile(np.where(key > query + 1, 0, -1e9)),
        "owner6": (np.arange(FALL)[None] // FF == np.arange(MOE + 1)[:, None]).astype(np.float32),
        "iota": np.tile(np.arange(P, dtype=np.float32), (P, 1)),
        "minus_half": minus_half.reshape(P, P),
        "band": by_tile(np.where(window, 0, -10000.0)),
        "mixT": np.concatenate([mixT[:P], mixT[P:, P:]], axis=1),
        "ident": np.eye(P, dtype=np.float32),
        "block_numbers": np.stack([np.arange(NBLK) - NBLK, np.arange(NBLK) + 1]).astype(np.float32),
    }
    return a


def kernel(**inputs):
    import concourse.bacc as bacc
    from concourse.bass_utils import run_bass_kernel_spmd

    nc = bacc.Bacc("TRN2", target_bir_lowering=False, num_devices=1)
    arrays, aps = {}, {}
    for name, v in laid_out(inputs).items():
        arrays[f"in_{name}"] = v
        aps[name] = nc.dram_tensor(f"in_{name}", v.shape, mybir.dt.from_np(v.dtype), kind="ExternalInput").ap()
    out = nc.dram_tensor("out_0_dram", (T, D), F32, kind="ExternalOutput").ap()
    build(nc, aps, out)
    r = run_bass_kernel_spmd(nc, [arrays], core_ids=[0])
    return r.results[0]["out_0_dram"].reshape(1, T, D)
```

```python
from contextlib import ExitStack

import numpy as np

import concourse.bass as bass
from concourse import mybir

ACT = mybir.ActivationFunctionType
ALU = mybir.AluOpType
AX = mybir.AxisListType
F32 = mybir.dt.float32
F32R = mybir.dt.float32r
BF16 = mybir.dt.bfloat16
U32 = mybir.dt.uint32
I32 = mybir.dt.int32
U8 = mybir.dt.uint8

P = 128
T = 256
TT = T // P
D = 256
DC = D // P
CD = 192
S2 = 4096
BLK = 512
NBLK = S2 // BLK
KT_PER = BLK // P
XH, XD = 16, 64
MASKED = -1e30
LH, LM = 16, 24
EXPERTS = 4096
ET = EXPERTS // P
EH, NK = 8, 64
GS = 16
FF, MOE = 192, 8
FALL = (MOE + 1) * FF
FT = (FALL + P - 1) // P
OWNERS = 32 + MOE + 1
UNITS = 2 * S2 // 1024


COLUMNS = ["L0_xattn_ln_gamma", "L0_xattn_ln_beta", "L0_ffn_norm_w", "L1_xattn_bq", "L1_attn_bq", "L1_attn_bk"]
EPS_OF_NORM = [1e-5] * 4 + [1e-6] + [1e-5] * 3
ROWS = ["L0_xattn_bo", "L0_attn_v_b", "L0_attn_out_b", "L1_attn_bv", "L1_attn_bo"]


class Chain:

    def __init__(self, eng, sem):
        self.eng, self.sem, self.n = eng, sem, 0

    def __call__(self, ins):
        self.n += 1
        ins.then_inc(self.sem, 1)
        self.eng.wait_ge(self.sem, self.n)


def build(nc, a, out):
    with ExitStack() as ctx:
        def sb(name, shape, dt=F32):
            return ctx.enter_context(nc.sbuf_tensor(name, shape, dt))

        def at_end(name, shape, back):
            return nc.alloc_sbuf_tensor_at(name, shape, F32R, offset=nc.sbuf_base - 4 * back)

        def sem(name):
            return ctx.enter_context(nc.semaphore(name))

        bank = [ctx.enter_context(nc.psum_tensor(f"bank{i}", [P, 512], F32)) for i in range(8)]

        ident = sb("ident", [P, P])
        turns = sb("turns", [P, XH])
        ones = sb("ones", [P, P])
        x_res = sb("x_res", [P, TT, D])
        xn = sb("xn", [P, TT, D])
        xnT = sb("xnT", [P, DC, T])
        bn = sb("bn", [P, TT, 6])
        mv = sb("mv", [P, TT, 2])
        rstd = sb("rstd", [P, TT])
        var = sb("var", [P, TT])
        root = sb("root", [P, TT])
        newton = sb("newton", [P, TT])
        columns = sb("columns", [P, len(COLUMNS) * DC])
        rows = sb("rows", [1, len(ROWS) * D])

        def column(name, c):
            k = COLUMNS.index(name) * DC + c
            return columns[:, k:k + 1]

        def row(name):
            k = ROWS.index(name) * D
            return rows[0:1, k:k + D]

        region_a = sb("region_a", [P, 14336])
        keys_in_a = at_end("keys_in_a", [P, 8 * BLK], 14336)
        owner6_r = at_end("owner6_r", [P, FALL], 14336 - FT * D)
        wkv_parts = at_end("wkv_parts", [P, 2048], 14336 - 8192 - 2048)
        region_g = sb("region_g", [P, 8192])
        wkv_upper = at_end("wkv_upper", [P, 2048], 8192 - 2048)[64:128]
        w6T = at_end("w6T", [P, T], 8192 - 512 - FT * T)
        def keys_of(h):
            if h < 8:
                return keys_in_a[:, h * BLK:(h + 1) * BLK]
            return keys_in_u[:, (h - 8) * BLK:(h - 7) * BLK] if h < XH - 1 else keys_in_qT[:, :]

        v_blk = region_a[:, 4096:8192].rearrange("p (t n) -> p t n", t=KT_PER)
        wkv = region_a[:, 8192:12288].rearrange("p (c n) -> p c n", c=2)
        wq = region_a[:, 12288:14336].rearrange("p (c n) -> p c n", c=2)
        o_acc = region_g[:, 0:2048].rearrange("p (t n) -> p t n", t=TT)
        prob = region_g[:, 2048:4096].rearrange("p (b t k) -> p b t k", b=2, t=TT)
        probT = region_g[:, 4096:6144].rearrange("p (b t k) -> p b t k", b=2, t=TT)
        mask_w = region_g[:, 6144:8192]
        oT = region_g[:, 2048:4096].rearrange("p (c n) -> p c n", c=8)
        wo = sb("wo", [P, 8, D])
        qT = sb("qT", [P, 8, T])
        keys_in_qT = at_end("keys_in_qT", [P, BLK], 8 * T)
        qT_flat = qT[:, :, :].rearrange("p m q -> p (m q)")
        region_u = sb("region_u", [P, 8192])
        keys_in_u = at_end("keys_in_u", [P, 7 * BLK], 8192 - 4224)
        region_d = sb("region_d", [P, 8192])
        q_parts = at_end("q_parts", [P, 2, 8, 2, T], 8192)
        q_upper, q_rest = q_parts[:, 0], q_parts[:, 1]
        wqk2 = region_u[:, 0:2048].rearrange("p (c n) -> p c n", c=DC)
        wv2 = region_u[:, 2048:2560].rearrange("p (c n) -> p c n", c=DC)
        wo2 = region_u[:, 2560:3072].rearrange("p (c n) -> p c n", c=DC)
        proj = region_u[:, 3072:3200]
        minus_half = region_u[:, 3200:3328]
        band = region_u[:, 3328:3840].rearrange("p (t k) -> p t k", t=TT)
        mixT = region_u[:, 3840:4224]

        def part(region, at, size):
            return region[:, at:at + size]

        q2T = part(region_a, 0, 1024).rearrange("p (c n) -> p c n", c=4)
        k2T = part(region_a, 1024, 1024).rearrange("p (c n) -> p c n", c=4)
        q2sq = part(region_a, 2048, 1024).rearrange("p (c n) -> p c n", c=4)
        k2sq = part(region_a, 3072, 1024).rearrange("p (c n) -> p c n", c=4)
        fq = part(region_a, 4096, 1024).rearrange("p (t h m) -> p t h m", t=TT, h=LH)
        fk = part(region_a, 5120, 1024).rearrange("p (t h m) -> p t h m", t=TT, h=LH)
        fqT = part(region_a, 6144, 1024).rearrange("p (c n) -> p c n", c=4)
        fkT = part(region_a, 7168, 1024).rearrange("p (c n) -> p c n", c=4)
        mixed0 = part(region_a, 8192, 4096).rearrange("p (h i) -> p h i", h=LH)
        mixed1 = part(region_a, 12288, 2048).rearrange("p (h i) -> p h i", h=LH)
        s2 = part(region_g, 0, 1024).rearrange("p (b t k) -> p b t k", b=2, t=TT)
        p2 = part(region_g, 1024, 1024).rearrange("p (b t k) -> p b t k", b=2, t=TT)
        p2T = part(region_g, 2048, 1024).rearrange("p (b k) -> p b k", b=2)
        v2 = part(region_g, 3072, TT * LH * 32).rearrange("p (t h d) -> p t h d", t=TT, h=LH)
        lin = part(region_g, 4672, TT * D).rearrange("p (t h d) -> p t h d", t=TT, h=LH)
        pvT = part(region_g, 5184, 1024).rearrange("p (c n) -> p c n", c=4)
        hvT = part(region_g, 6208, 1024).rearrange("p (c n) -> p c n", c=4)
        k2_diag = part(region_a, 8192, 4096).rearrange("p (c g n) -> p c g n", c=4, g=4)
        fq_diag = part(region_d, 0, 4096).rearrange("p (c g n) -> p c g n", c=4, g=4)
        att = part(region_g, 4160, TT * D).rearrange("p (t h d) -> p t h d", t=TT, h=LH)
        att_flat = part(region_g, 4160, TT * D).rearrange("p (t n) -> p t n", t=TT)
        attT = sb("attT", [P, DC, T])
        ctx_b_upper = at_end("ctx_b_upper", [P, BLK], DC * T)
        w_q3 = part(region_d, 0, 4096).rearrange("p (g d) -> p g d", g=2 * EH)
        keysT = part(region_d, 4096, 1024)
        downT = region_d[:, :].rearrange("p (c e) -> p c e", c=DC)
        up = region_u[:, :].rearrange("p (h d) -> p h d", h=ET)
        w_sim = sb("w_sim", [P, DC, 2 * EH * NK])
        hidden = region_g[:, :].rearrange("p (h t) -> p h t", h=ET)
        hot_lo = part(region_a, 0, GS * P).bitcast(BF16).rearrange("p (b l s) -> p b l s", b=2, s=GS)
        hot_hi = part(region_a, 2048, 3 * GS * ET).bitcast(BF16).rearrange("p (b w h s) -> p b w h s", b=2, w=3, s=GS)
        hit_hi = part(region_a, 4096, GS * ET).bitcast(BF16).rearrange("p (b h s) -> p b h s", b=2, s=GS)
        iota_h = part(region_a, 6400, GS * P // 2).bitcast(BF16).rearrange("p (l s) -> p l s", s=GS)
        chosen_h = part(region_a, 7424, 5 * P // 2).bitcast(BF16).rearrange("p (k n) -> p k n", k=5)
        rest_w = part(region_a, 7744, P)
        iota = part(region_a, 5120, P)
        chosenT = part(region_a, 5248, 3 * P).rearrange("p (s n) -> p s n", s=3)
        top = part(region_a, 5632, TT * 2 * EH * 8).rearrange("p (t g k) -> p t g k", t=TT, g=2 * EH)
        top_i = part(region_a, 5888, TT * 2 * EH * 8).bitcast(U32).rearrange("p (t g k) -> p t g k", t=TT, g=2 * EH)
        top_f = part(region_a, 6144, TT * 2 * EH * 8).rearrange("p (t g k) -> p t g k", t=TT, g=2 * EH)
        pairs = part(region_a, 0, TT * EH * 64).rearrange("p (t h k) -> p t h k", t=TT, h=EH)
        pick = part(region_a, 1024, 512).rearrange("p (k j) -> p k j", j=8)
        squares = part(region_a, 1536, TT * D).rearrange("p (t d) -> p t d", t=TT)
        best = part(region_a, 2048, P).rearrange("p (t k) -> p t k", t=TT)
        best_i = part(region_a, 2176, P).bitcast(U32).rearrange("p (t k) -> p t k", t=TT)
        rank_i = part(region_a, 2304, 2 * P).bitcast(U32).rearrange("p (s t k) -> p s t k", s=2, t=TT)
        rank = part(region_a, 2560, 2 * P).rearrange("p (s t k) -> p s t k", s=2, t=TT)
        side = part(region_a, 2816, 2 * P).rearrange("p (s t k) -> p s t k", s=2, t=TT)
        expert = part(region_a, 3072, P).rearrange("p (t k) -> p t k", t=TT)
        expert_i = part(region_a, 3200, P).bitcast(U32).rearrange("p (t k) -> p t k", t=TT)
        split_i = part(region_a, 3328, 2 * P).bitcast(U32).rearrange("p (s t k) -> p s t k", s=2, t=TT)
        chosen = part(region_a, 3584, 3 * P).rearrange("p (s n) -> p s n", s=3)
        wq4 = part(qT_flat, 0, 512).rearrange("p (c n) -> p c n", c=DC)
        wk4T = part(qT_flat, 512, 2 * (CD + 1)).rearrange("p (c n) -> p c n", c=DC)
        wv4a = part(qT_flat, 898, D)
        wv4b = part(qT_flat, 1154, D)[0:CD - P + 1]
        ctxT_a = region_d[:, 0:S2]
        ctxT_b = region_d[0:CD - P + 1, S2:2 * S2]
        ctx_rows = part(region_a, 8192, S2 // P * CD).rearrange("p (k d) -> p k d", k=S2 // P)
        q4T = part(region_g, 0, 512).rearrange("p (c n) -> p c n", c=DC)
        qk_a = part(region_g, 512, T)
        qk_b = part(region_g, 768, T)[0:CD - P + 1]
        p4 = part(region_g, 1024, 2048).rearrange("p (b k) -> p b k", b=2)
        p4T = part(region_g, 3072, 2048).rearrange("p (b k) -> p b k", b=2)
        o4 = part(region_g, 5120, TT * CD).rearrange("p (t d) -> p t d", t=TT)
        o4T_a = part(region_g, 5504, T)
        o4T_b = part(region_g, 5760, T)[0:CD - P + 1]
        nm4_half = sb("nm4_half", [P, TT, 2])
        nm4_run = sb("nm4_run", [P, TT])
        nm4_new = sb("nm4_new", [P, TT])
        diff4 = sb("diff4", [P, UNITS])
        alpha4 = sb("alpha4", [P, UNITS])
        sum4 = sb("sum4", [P, UNITS, 2])
        l4 = sb("l4", [P, TT])
        w5 = wo[:, :, :].rearrange("p c n -> p (c n)").rearrange("p (w c n) -> p w c n", w=4, c=DC)
        q5T = part(region_g, 0, 512).rearrange("p (c n) -> p c n", c=DC)
        k5T = part(region_g, 512, 512).rearrange("p (c n) -> p c n", c=DC)
        v5 = part(region_g, 1024, 512).rearrange("p (t n) -> p t n", t=TT)
        s5 = part(region_g, 1536, 512).rearrange("p (t n) -> p t n", t=TT)
        p5 = part(region_g, 2048, 512).rearrange("p (t n) -> p t n", t=TT)
        p5T = part(region_g, 2560, 512)
        keep5 = part(region_g, 6016, 512).rearrange("p (t n) -> p t n", t=TT)
        fill5 = part(region_g, 6528, 512).rearrange("p (t n) -> p t n", t=TT)
        wg6 = part(region_u, 0, DC * FALL).rearrange("p (c n) -> p c n", c=DC)
        wu6 = part(region_u, DC * FALL, DC * FALL).rearrange("p (c n) -> p c n", c=DC)
        wd6 = part(region_a, 0, FT * D).rearrange("p (m n) -> p m n", m=FT)
        owner6 = part(region_a, FT * D, FALL)[0:OWNERS]
        wr6 = part(region_a, FT * D + FALL, DC * MOE).rearrange("p (c n) -> p c n", c=DC)
        ebias6 = part(region_a, FT * D + FALL + 16, MOE)
        iota6 = part(region_a, FT * D + FALL + 24, MOE)
        silu6 = part(region_g, 0, 2 * T).rearrange("p (b n) -> p b n", b=2)
        h6 = part(region_g, 512, FT * T).rearrange("p (m n) -> p m n", m=FT)
        r6 = sb("r6", [P, 6, TT, MOE + 1])
        r6_i = sb("r6_i", [P, TT, 8], U32)
        r6_s = sb("r6_s", [P, TT])
        qk_bias = sb("qk_bias", [P, 8])
        q_ls = sb("q_ls", [P, TT, LH])
        k_ls = sb("k_ls", [P, TT, LH])
        k_max = sb("k_max", [P, LH])
        k_stab = sb("k_stab", [P, LH])
        nm2 = sb("nm2", [P, TT, LH])
        sum2 = sb("sum2", [P, TT, LH])
        stat = sb("stat", [P, 4, TT, LH])
        ctx_a = sb("ctx_a", [P, BLK])
        ctx_b = sb("ctx_b", [P, BLK])
        ctx_b_rest = at_end("ctx_b_rest", [P, BLK], BLK)
        bias_h = sb("bias_h", [P, TT, BLK], BF16)
        seen = sb("seen", [P, TT, NBLK])
        is_row = sb("is_row", [P, TT])
        any_q = sb("any_q", [P, TT])
        rng = sb("rng", [1, 8 * NBLK])
        rng_i = sb("rng_i", [1, 2], I32)
        blk_lo = sb("blk_lo", [1, NBLK])
        blk_hi = sb("blk_hi", [1, NBLK])
        nm_run = sb("nm_run", [P, XH, TT])
        nm_blk = sb("nm_blk", [P, XH, TT])
        nm_new = sb("nm_new", [P, XH, TT])
        m_diff = sb("m_diff", [P, XH, TT])
        alpha = sb("alpha", [P, XH, TT])
        l_blk = sb("l_blk", [P, XH, TT])
        l_run = sb("l_run", [P, XH, TT])

        x_in, weights_in, mask_in, small_in, wkv_in, wo_in = (
            sem(n) for n in ("x_in", "weights_in", "mask_in", "small_in", "wkv_in", "wo_in"))
        ctx_landed, ctx_free = sem("ctx_landed"), sem("ctx_free")
        dve_step = sem("dve_step")
        consts_set = sem("consts_set")
        blocks_seen, blocks_counted, range_set = sem("blocks_seen"), sem("blocks_counted"), sem("range_set")
        xn_ready, xnT_psum, xnT_ready = sem("xn_ready"), sem("xnT_psum"), sem("xnT_ready")
        q_psum, q_ready = sem("q_psum"), sem("q_ready")
        wkv_upper_set, wkv_split, ctx_split, q_split, q_twice, k_upper_set, k_split, ctx_upper_set = (
            sem(n) for n in ("wkv_upper_set", "wkv_split", "ctx_split", "q_split", "q_twice", "k_upper_set", "k_split",
                             "ctx_upper_set"))
        bias_ready, k_psum, v_psum, v_ready = (
            sem(n) for n in ("bias_ready", "k_psum", "v_psum", "v_ready"))
        s_ready, nm_blk_ready, nm_ready, diff_ready, prob_ready, alpha_ready = (
            sem(n) for n in ("s_ready", "nm_blk_ready", "nm_ready", "diff_ready", "prob_ready", "alpha_ready"))
        pT_psum, pT_ready0, pT_ready1, o_psum, o_added = (
            sem(n) for n in ("pT_psum", "pT_ready0", "pT_ready1", "o_psum", "o_added"))
        l_scaled, run_kept = sem("l_scaled"), sem("run_kept")
        o_normed, oT_psum, oT_ready, y_psum, x_ready = (
            sem(n) for n in ("o_normed", "oT_psum", "oT_ready", "y_psum", "x_ready"))
        var_ready, root_ready = sem("var_ready"), sem("root_ready")
        stored = sem("stored")
        late_w_in, ctxT_in, ctx_rows_in, masks5_in, moe_in, moe_small_in = (
            sem(n) for n in ("late_w_in", "ctxT_in", "ctx_rows_in", "masks5_in", "moe_in", "moe_small_in"))
        q4_psum, q4_ready, qk4_psum, qk4_ready = (
            sem(n) for n in ("q4_psum", "q4_ready", "qk4_psum", "qk4_ready"))
        s4_psum, nm4_ready, diff4_ready, p4_ready, alpha4_ready, p4T_psum, p4T_ready0, p4T_ready1, o4_psum, o4_added = (
            sem(n) for n in ("s4_psum", "nm4_ready", "diff4_ready", "p4_ready", "alpha4_ready", "p4T_psum",
                             "p4T_ready0", "p4T_ready1", "o4_psum", "o4_added"))
        v5_ready = sem("v5_ready")
        o4_normed, o4T_psum, o4T_ready, ones4_set = (
            sem(n) for n in ("o4_normed", "o4T_psum", "o4T_ready", "ones4_set"))
        qkv5_psum, qkv5_ready, s5_psum, s5_ready, p5_ready, p5T_psum, p5T_ready, o5_psum = (
            sem(n) for n in ("qkv5_psum", "qkv5_ready", "s5_psum", "s5_ready", "p5_ready", "p5T_psum", "p5T_ready",
                             "o5_psum"))
        owner6_ready = sem("owner6_ready")
        router_psum, router_exp, w6_ready, w6T_psum, w6T_ready, gate_psum, up6_psum, silu_ready, h6_ready = (
            sem(n) for n in ("router_psum", "router_exp", "w6_ready", "w6T_psum", "w6T_ready", "gate_psum", "up6_psum",
                             "silu_ready", "h6_ready"))
        up_in = sem("up_in")
        sim_in, experts_in, wsim_psum, wsim_ready, iota_in = (
            sem(n) for n in ("sim_in", "experts_in", "wsim_psum", "wsim_ready", "iota_in"))
        sim_psum, down_psum, gelu_ready, chosen_ready, chosenT_psum = (
            sem(n) for n in ("sim_psum", "down_psum", "gelu_ready", "chosen_ready", "chosenT_psum"))
        hit_ready, hot_ready, mixw_psum, hidden_ready = (
            sem(n) for n in ("hit_ready", "hot_ready", "mixw_psum", "hidden_ready"))
        lin_in, norm_done = sem("lin_in"), sem("norm_done")
        qk2_psum, q2_ready, k2_ready, v2_psum, v2_ready = (
            sem(n) for n in ("qk2_psum", "q2_ready", "k2_ready", "v2_psum", "v2_ready"))
        fq_psum, fk_psum, k_maxed, k_stab_ready, fq_arg, fk_arg, fq_ready, fk_ready = (
            sem(n) for n in ("fq_psum", "fk_psum", "k_maxed", "k_stab_ready", "fq_arg", "fk_arg", "fq_ready", "fk_ready"))
        k2_diag_zero, k2_diag_in, fq_diag_zero, fq_diag_in, pvT_ready, hvT_ready, turned_psum = (
            sem(n) for n in ("k2_diag_zero", "k2_diag_in", "fq_diag_zero", "fq_diag_in", "pvT_ready", "hvT_ready",
                             "turned_psum"))
        s2_psum, s2_ready, p2_ready, p2T_psum, p2T_ready, pv2_psum = (
            sem(n) for n in ("s2_psum", "s2_ready", "p2_ready", "p2T_psum", "p2T_ready", "pv2_psum"))
        fT_psum, fqT_ready, fkT_ready, mix_psum, mix_ready, hv_psum = (
            sem(n) for n in ("fT_psum", "fqT_ready", "fkT_ready", "mix_psum", "mix_ready", "hv_psum"))
        gap_ready, gap_exp, att_ready, attT_psum, attT_ready = (
            sem(n) for n in ("gap_ready", "gap_exp", "att_ready", "attT_psum", "attT_ready"))

        norms = [0]

        def refine_rstd(dve, step):
            step(nc.vector.reciprocal(rstd[:, :], root[:, :]))
            step(nc.vector.tensor_tensor(newton[:, :], var[:, :], rstd[:, :], ALU.mult))
            step(nc.vector.tensor_tensor(newton[:, :], newton[:, :], rstd[:, :], ALU.mult))
            step(nc.vector.tensor_scalar(newton[:, :], newton[:, :], -0.5, 1.5, ALU.mult, ALU.add))
            step(nc.vector.tensor_tensor(rstd[:, :], rstd[:, :], newton[:, :], ALU.mult))

        def take_root(act, nth):
            act.wait_ge(var_ready, nth)
            nc.scalar.activation(root[:, :], var[:, :], ACT.Sqrt).then_inc(root_ready, 1)

        def layer_norm(dve, step, src, dst, after=None):
            for t in range(TT):
                ins = nc.vector.bn_stats(bn[:, t], src[:, t])
            step(ins)
            for t in range(TT):
                ins = nc.vector.bn_aggr(mv[:, t], bn[:, t])
            step(ins)
            nc.vector.tensor_scalar(var[:, :], mv[:, :, 1], EPS_OF_NORM[norms[0]], None, ALU.add).then_inc(var_ready, 1)
            norms[0] += 1
            dve.wait_ge(root_ready, norms[0])
            refine_rstd(dve, step)
            for t in range(TT):
                ins = nc.vector.tensor_scalar(dst[:, t], src[:, t], mv[:, t, 0:1], rstd[:, t:t + 1],
                                              ALU.subtract, ALU.mult)
                if after is not None:
                    ins.then_inc(after, 1)
            if after is None:
                step(ins)

        def within(eng, b):
            return nc.s_assert_within(b, 0, NBLK - 1)

        def turn_xn(pe, nth, into):
            pe.wait_ge(xn_ready, TT * nth)
            for c in range(DC):
                for t in range(TT):
                    mm = nc.tensor.transpose(into[c][:, t * P:(t + 1) * P],
                                             xn[:, t, c * P:(c + 1) * P], ident[:, :])
            mm.then_inc(xnT_psum, 1)

        def turn_and_project(pe, nth, src, banks, w, bias, dst):
            pe.wait_ge(att_ready, nth)
            for c in range(DC):
                for t in range(TT):
                    mm = nc.tensor.transpose(banks[c][:, t * P:(t + 1) * P], src[:, t, c * P:(c + 1) * P], ident[:, :])
                mm.then_inc(attT_psum, 1)
            pe.wait_ge(attT_ready, 2 * nth)
            for t in range(TT):
                into = dst[:, t * D:(t + 1) * D]
                nc.tensor.matmul(into, lhsT=ones[0:1, :], rhs=bias, start=True, stop=False)
                for c in range(DC):
                    mm = nc.tensor.matmul(into, lhsT=attT[:, c, t * P:(t + 1) * P], rhs=w[:, c, :],
                                          start=False, stop=c == DC - 1)
            mm.then_inc(y_psum, 1)

        block = ctx.enter_context(nc.Block())

        @block.sync
        def _(sp):
            sp.dma_start(x_res[:, :, :], a["x"].rearrange("(t p) d -> p t d", p=P)).then_inc(x_in, 16)
            sp.dma_start(mask_w.bitcast(U32).rearrange("p (t w) -> p t w", t=TT),
                         a["mask"].rearrange("(t p) w -> p t w", p=P)).then_inc(mask_in, 16)
            sp.dma_start(ident[:, :], a["ident"]).then_inc(small_in, 16)
            sp.dma_start(columns[:, :], a["columns"]).then_inc(small_in, 16)
            sp.dma_start(blk_lo[:, :], a["block_numbers"][0:1]).then_inc(small_in, 16)
            sp.dma_start(blk_hi[:, :], a["block_numbers"][1:2]).then_inc(small_in, 16)
            sp.dma_start(rows[:, :], a["rows"]).then_inc(small_in, 16)
            sp.dma_start(wq, a["Wq"].rearrange("(c p) n -> p c n", p=P)).then_inc(weights_in, 16)
            sp.dma_start(wkv[:, 0, :], a["Wkv"][0:P]).then_inc(wkv_in, 16)
            for k in range(2):
                sp.dma_start(wkv[64 * k:64 * k + 64, 1, :], a["Wkv"][P:CD]).then_inc(wkv_in, 16)
            sp.wait_ge(range_set, 1)
            first = sp.value_load(rng_i[0:1, 0:1], min_val=0, max_val=NBLK - 1)
            n_blocks = sp.value_load(rng_i[0:1, 1:2], min_val=1, max_val=NBLK)

            def load_block(b):
                sp.dma_start(ctx_a[:, :], a["ctxT"][0:P, bass.ds(b * BLK, BLK)]).then_inc(ctx_landed, 16)
                for k in range(2):
                    sp.dma_start(ctx_b[64 * k:64 * k + 64, :], a["ctxT"][P:CD, bass.ds(b * BLK, BLK)]
                                 ).then_inc(ctx_landed, 16)

            with sp.Fori(0, n_blocks) as i:
                sp.wait_ge(ctx_free, i + 1)
                load_block(within(sp, first + i))
            sp.dma_start(wo[:, :, :], a["Wo"].rearrange("(c p) n -> p c n", p=P)).then_inc(wo_in, 16)
            for dst, name in ((wqk2, "wqk2"), (wv2, "wv2"), (wo2, "wo2")):
                sp.dma_start(dst, a[name].rearrange("(c p) n -> p c n", p=P)).then_inc(lin_in, 16)
            for dst, name in ((proj, "proj"), (minus_half, "minus_half"), (mixT, "mixT"), (qk_bias[:, :], "qk_bias")):
                sp.dma_start(dst, a[name]).then_inc(lin_in, 16)
            sp.dma_start(band, a["band"].rearrange("p (t k) -> p t k", t=TT)).then_inc(lin_in, 16)
            sp.wait_ge(o_normed, 1)
            sp.dma_start(w_q3, a["w_q"].rearrange("(g p) d -> p g d", p=P)).then_inc(sim_in, 16)
            sp.dma_start(keysT, a["keysT"]).then_inc(sim_in, 16)
            sp.wait_ge(k2_diag_zero, 1)
            sp.wait_ge(k2_ready, 4)
            for g in range(4):
                own = slice(32 * g, 32 * g + 32)
                sp.dma_start(k2_diag[own, :, g, :], k2T[own, :, :]).then_inc(k2_diag_in, 16)
            sp.wait_ge(fq_diag_zero, 1)
            sp.wait_ge(fqT_ready, 2)
            for g in range(4):
                own = slice(32 * g, 32 * g + LM)
                sp.dma_start(fq_diag[own, :, g, :], fqT[own, :, :]).then_inc(fq_diag_in, 16)
            sp.wait_ge(mix_psum, 12)
            for c in range(DC):
                sp.dma_start(downT[:, c], a["downT"][c * P:(c + 1) * P]).then_inc(experts_in, 16)
            sp.wait_ge(x_ready, 2)
            sp.dma_start(iota, a["iota"]).then_inc(iota_in, 16)
            for c in range(2):
                sp.dma_start(up[:, c * 16:(c + 1) * 16], a["up"].rearrange("(h l) d -> l h d", l=P)[:, c * 16:(c + 1) * 16]
                             ).then_inc(up_in, 16)
            sp.dma_start(wq4, a["wq4"].rearrange("(c p) n -> p c n", p=P)).then_inc(late_w_in, 16)
            sp.dma_start(wk4T, a["wk4T"].rearrange("(c p) n -> p c n", p=P)).then_inc(late_w_in, 16)
            sp.dma_start(wv4a, a["wv4"][0:P]).then_inc(late_w_in, 16)
            sp.dma_start(wv4b, a["wv4"][P:CD + 1]).then_inc(late_w_in, 16)
            sp.dma_start(ctx_rows, a["ctx"].rearrange("(k p) d -> p k d", p=P)).then_inc(ctx_rows_in, 16)
            sp.wait_ge(down_psum, ET // 2)
            sp.dma_start(ctxT_a, a["ctxT"][0:P]).then_inc(ctxT_in, 16)
            sp.dma_start(ctxT_b[0:CD - P], a["ctxT"][P:CD]).then_inc(ctxT_in, 16)
            for w, name in enumerate(("wq5", "wk5", "wv5", "wo5")):
                sp.dma_start(w5[:, w], a[name].rearrange("(c p) n -> p c n", p=P)).then_inc(late_w_in, 16)
            sp.wait_ge(x_ready, 3)
            sp.dma_start(keep5, a["keep5"].rearrange("p (t n) -> p t n", t=TT)).then_inc(masks5_in, 16)
            sp.dma_start(fill5, a["fill5"].rearrange("p (t n) -> p t n", t=TT)).then_inc(masks5_in, 16)
            sp.dma_start(wr6, a["wr6"].rearrange("(c p) n -> p c n", p=P)).then_inc(moe_small_in, 16)
            sp.dma_start(ebias6, a["ebias6"].partition_broadcast(P)).then_inc(moe_small_in, 16)
            sp.dma_start(iota6, a["iota"][:, 0:MOE]).then_inc(moe_small_in, 16)
            sp.dma_start(owner6, a["owner6"]).then_inc(moe_small_in, 16)
            sp.dma_start(wg6, a["wg6"].rearrange("(c p) n -> p c n", p=P)).then_inc(moe_in, 16)
            sp.dma_start(wu6, a["wu6"].rearrange("(c p) n -> p c n", p=P)).then_inc(moe_in, 16)
            full = FALL // P
            sp.dma_start(wd6[:, 0:full], a["wd6"][0:full * P].rearrange("(m p) n -> p m n", p=P)).then_inc(moe_in, 16)
            sp.dma_start(wd6[0:FALL - full * P, full], a["wd6"][full * P:FALL]).then_inc(moe_in, 16)
            sp.wait_ge(x_ready, 6)
            sp.dma_start(out.rearrange("(t p) d -> p t d", p=P), x_res[:, :, :]).then_inc(stored, 16)
            sp.wait_ge(stored, 16)

        @block.tensor
        def _(pe):
            pe.wait_ge(small_in, 80)
            pe.wait_ge(consts_set, 2)
            turn_xn(pe, 1, (bank[1], bank[7]))
            pe.wait_ge(weights_in, 16)
            pe.wait_ge(xnT_ready, 2)
            for m in range(8):
                dst = bank[2 + m // 2][:, (m % 2) * T:(m % 2 + 1) * T]
                for c in range(DC):
                    mm = nc.tensor.matmul(dst, lhsT=wq[:, c, m * P:(m + 1) * P], rhs=xnT[:, c, :],
                                          start=c == 0, stop=c == DC - 1)
                if m % 2:
                    mm.then_inc(q_psum, 1)
                if m == 1:
                    pe.wait_ge(blocks_seen, 1)
                    nc.tensor.matmul(bank[0][0:1, 0:TT * NBLK], lhsT=ones[:, 0:1],
                                     rhs=seen[:, :, :].rearrange("p t b -> p (t b)"),
                                     start=True, stop=True).then_inc(blocks_counted, 1)
            pe.wait_ge(wkv_in, 48)
            pe.wait_ge(wkv_split, 2)
            pe.wait_ge(range_set, 1)
            n_blocks = pe.value_load(rng_i[0:1, 1:2], min_val=1, max_val=NBLK)
            pe.wait_ge(q_ready, 4)
            with pe.Fori(0, n_blocks) as i:
                base = pe.snap(i * XH)
                base8 = pe.snap(i * 8)
                pe.wait_ge(ctx_landed, i * 48 + 48)
                for j in range(8):
                    for keys in (True, False):
                        if j >= 2:
                            pe.wait_ge(k_split if keys else v_ready, base8 + (j - 1))
                        dst = bank[2 * (j % 2) + (not keys)][:, :]
                        own = slice(j * P, (j + 1) * P)
                        tile = slice(j // 2 * P, (j // 2 + 1) * P)
                        cols = slice(1024 + j % 2 * 512, 1024 + (j % 2 + 1) * 512)
                        if keys:
                            nc.tensor.matmul(dst, lhsT=wkv[:, 0, own], rhs=ctx_a[:, :], start=True, stop=False)
                        else:
                            nc.tensor.matmul(dst, lhsT=ctx_a[:, tile], rhs=wkv[:, 0, cols], start=True, stop=False)
                        if j == 0 and keys:
                            pe.wait_ge(ctx_split, i + 1)
                        for src in (ctx_b_upper, ctx_b_rest):
                            lhsT, rhs = (wkv_parts[:, own], src[:, :]) if keys else (src[:, tile], wkv_parts[:, cols])
                            mm = nc.tensor.matmul(dst, lhsT=lhsT, rhs=rhs, start=False, stop=src is ctx_b_rest)
                        mm.then_inc(k_psum if keys else v_psum, 1)
                pe.wait_ge(k_split, base8 + 8)
                pe.wait_ge(v_ready, base8 + 8)
                pe.wait_ge(q_split, 8)
                pe.wait_ge(q_twice, 12)

                def scores(h):
                    if h >= 2:
                        pe.wait_ge(prob_ready, 2 * base + 2 * (h - 1))
                    for t in range(TT):
                        dst = bank[2 * (h % 2) + t][:, :]
                        for q in (q_upper, q_rest):
                            mm = nc.tensor.matmul(dst, lhsT=q[:, h // 2, h % 2, t * P:(t + 1) * P],
                                                  rhs=keys_of(h), start=q is q_upper, stop=q is q_rest)
                            if h == 0 and t == 0 and q is q_upper:
                                mm.then_inc(ctx_free, 1)
                    mm.then_inc(s_ready, 1)

                def turn(h):
                    for t in range(TT):
                        pe.wait_ge(prob_ready, 2 * base + (2 * h + t + 1))
                        if h >= 1:
                            pe.wait_ge((pT_ready0, pT_ready1)[t], base + h)
                        for k in range(KT_PER):
                            mm = nc.tensor.transpose(bank[4 + t][:, k * P:(k + 1) * P],
                                                     prob[:, h % 2, t, k * P:(k + 1) * P], ident[:, :])
                        mm.then_inc(pT_psum, 1)

                def values(h):
                    if h >= 2:
                        pe.wait_ge(o_added, base + (h - 1))
                    for t in range(TT):
                        pe.wait_ge((pT_ready0, pT_ready1)[t], base + (h + 1))
                        for k in range(KT_PER):
                            mm = nc.tensor.matmul(bank[6 + h % 2][:, t * XD:(t + 1) * XD],
                                                  lhsT=probT[:, h % 2, t, k * P:(k + 1) * P],
                                                  rhs=v_blk[:, k, h * XD:(h + 1) * XD],
                                                  start=k == 0, stop=k == KT_PER - 1)
                    mm.then_inc(o_psum, 1)

                for h in range(XH + 2):
                    if h < XH:
                        scores(h)
                    if 1 <= h <= XH:
                        turn(h - 1)
                    if h >= 2:
                        values(h - 2)
            pe.wait_ge(o_normed, 1)
            for c in range(8):
                for t in range(TT):
                    mm = nc.tensor.transpose(bank[c // 2][:, (c % 2) * T + t * P:(c % 2) * T + (t + 1) * P],
                                             o_acc[:, t, c * P:(c + 1) * P], ident[:, :])
                if c % 2:
                    mm.then_inc(oT_psum, 1)
            pe.wait_ge(wo_in, 16)
            pe.wait_ge(oT_ready, 4)
            for t in range(TT):
                dst = bank[4][:, t * D:(t + 1) * D]
                nc.tensor.matmul(dst, lhsT=ones[0:1, :], rhs=row("L0_xattn_bo"), start=True, stop=False)
                for c in range(8):
                    mm = nc.tensor.matmul(dst, lhsT=oT[:, c, t * P:(t + 1) * P], rhs=wo[:, c, :],
                                          start=False, stop=c == 7)
            mm.then_inc(y_psum, 1)

            pe.wait_ge(sim_in, 32)
            for c in range(DC):
                for g in range(2 * EH):
                    mm = nc.tensor.matmul(bank[(3, 5, 6, 7)[2 * c + g // EH]][:, (g % EH) * NK:(g % EH + 1) * NK],
                                          lhsT=w_q3[:, g, c * P:(c + 1) * P], rhs=keysT[:, g * NK:(g + 1) * NK],
                                          start=True, stop=True)
                    if g % EH == EH - 1:
                        mm.then_inc(wsim_psum, 1)
            turn_xn(pe, 2, (bank[0], bank[1]))
            pe.wait_ge(lin_in, 128)
            pe.wait_ge(xnT_ready, 4)
            pe.wait_ge(wsim_ready, 4)
            for m in range(8):
                for c in range(DC):
                    mm = nc.tensor.matmul(bank[2 + m // 2][:, (m % 2) * T:(m % 2 + 1) * T],
                                          lhsT=wqk2[:, c, m * P:(m + 1) * P], rhs=xnT[:, c, :],
                                          start=c == 0, stop=c == DC - 1)
                if m % 2:
                    mm.then_inc(qk2_psum, 1)
            for t in range(TT):
                dst = bank[6][:, t * D:(t + 1) * D]
                nc.tensor.matmul(dst, lhsT=ones[0:1, :], rhs=row("L0_attn_v_b"), start=True, stop=False)
                for c in range(DC):
                    mm = nc.tensor.matmul(dst, lhsT=xnT[:, c, t * P:(t + 1) * P], rhs=wv2[:, c, :],
                                          start=False, stop=c == DC - 1)
            mm.then_inc(v2_psum, 1)
            for x2, sq, ready, psum, first in ((q2T, q2sq, q2_ready, fq_psum, 0), (k2T, k2sq, k2_ready, fk_psum, 2)):
                pe.wait_ge(ready, 5)
                if first:
                    pe.wait_ge(q2_ready, 5)
                for t in range(TT):
                    for c in range(4):
                        dst = bank[first + t][:, c * P:(c + 1) * P]
                        nc.tensor.matmul(dst, lhsT=x2[:, c, t * P:(t + 1) * P], rhs=proj, start=True, stop=False)
                        mm = nc.tensor.matmul(dst, lhsT=sq[:, c, t * P:(t + 1) * P], rhs=minus_half,
                                              start=False, stop=True)
                    mm.then_inc(psum, 1)

            def scores2(h):
                if h >= 2:
                    pe.wait_ge(s2_ready, h - 1)
                for t in range(TT):
                    mm = nc.tensor.matmul(bank[4 + h % 2][:, t * T:(t + 1) * T], lhsT=q2T[:, h // 4, t * P:(t + 1) * P],
                                          rhs=k2_diag[:, h // 4, h % 4, :], start=True, stop=True)
                mm.then_inc(s2_psum, 1)

            def turn2(h):
                pe.wait_ge(p2_ready, 2 * h + 2)
                if h >= 2:
                    pe.wait_ge(p2T_ready, h - 1)
                for j in range(TT):
                    for t in range(TT):
                        mm = nc.tensor.transpose(bank[6 + h % 2][:, (2 * j + t) * P:(2 * j + t + 1) * P],
                                                 p2[:, h % 2, t, j * P:(j + 1) * P], ident[:, :])
                mm.then_inc(p2T_psum, 1)

            def head_rows(banks, h):
                return banks[h // 8][32 * (h % 4):32 * (h % 4) + 32, (h // 4 % 2) * T:(h // 4 % 2 + 1) * T]

            def values2(h):
                pe.wait_ge(p2T_ready, h + 1)
                for j in range(TT):
                    mm = nc.tensor.matmul(head_rows((bank[2], bank[3]), h), lhsT=v2[:, j, h, :],
                                          rhs=p2T[:, h % 2, j * T:(j + 1) * T], start=j == 0, stop=j == TT - 1)
                mm.then_inc(pv2_psum, 1)

            def turn_features(f):
                for c in range(4):
                    for t in range(TT):
                        mm = nc.tensor.transpose(bank[c // 2][:, (c % 2) * T + t * P:(c % 2) * T + (t + 1) * P],
                                                 f[:, t, 4 * c:4 * c + 4, :].rearrange("p h m -> p (h m)"), ident[:, :])
                    if c % 2:
                        mm.then_inc(fT_psum, 1)

            pe.wait_ge(fq_ready, 2)
            turn_features(fq)
            pe.wait_ge(v2_ready, 1)
            pe.wait_ge(k2_diag_in, 64)
            for h in range(LH + 2):
                if h < LH:
                    scores2(h)
                if 1 <= h <= LH:
                    turn2(h - 1)
                if h == 2:
                    pe.wait_ge(fk_arg, 2)
                if h == 3:
                    pe.wait_ge(fk_ready, 2)
                    pe.wait_ge(fqT_ready, 2)
                    turn_features(fk)
                if h >= 2:
                    values2(h - 2)
            pe.wait_ge(fq_diag_in, 64)
            pe.wait_ge(fkT_ready, 2)
            pe.wait_ge(pvT_ready, 1)

            def products(c):
                own = (6, 7, 2) if c % 2 == 0 else (0, 1, 4)
                if c >= 2:
                    pe.wait_ge(mix_ready, 3 * (c - 1))
                for k in range(2):
                    nc.tensor.matmul(bank[own[k]][:, :], lhsT=fkT[:, c, 0:P],
                                     rhs=fq_diag[:, c, 2 * k:2 * k + 2, :].rearrange("p g n -> p (g n)"),
                                     start=True, stop=True).then_inc(mix_psum, 1)
                nc.tensor.matmul(bank[own[2]][:, :], lhsT=fkT[:, c, P:T], rhs=fq_diag[:, c, :, P:T],
                                 start=True, stop=True).then_inc(mix_psum, 1)

            def mixed_values(c):
                pe.wait_ge(mix_ready, 3 * (c + 1))
                for h in range(4 * c, 4 * c + 4):
                    dst = head_rows((bank[3], bank[5]), h)
                    nc.tensor.matmul(dst, lhsT=v2[:, 0, h, :], rhs=mixed0[:, h, :], start=True, stop=False)
                    mm = nc.tensor.matmul(dst[:, P:T], lhsT=v2[:, 1, h, :], rhs=mixed1[:, h, :], start=False, stop=True)
                mm.then_inc(hv_psum, 1)

            def turn_back(src, first):
                for t in range(TT):
                    for c in range(4):
                        mm = nc.tensor.transpose(bank[first + t][:, c * P:(c + 1) * P], src[:, c, t * P:(t + 1) * P],
                                                 ident[:, :])
                mm.then_inc(turned_psum, 1)

            products(0)
            products(1)
            pe.wait_ge(pvT_ready, 2)
            mixed_values(0)
            products(2)
            mixed_values(1)
            products(3)
            mixed_values(2)
            turn_back(pvT, 6)
            mixed_values(3)
            pe.wait_ge(hvT_ready, 2)
            turn_back(hvT, 0)
            turn_and_project(pe, 1, att_flat, (bank[0], bank[1]), wo2, row("L0_attn_out_b"), bank[2])

            turn_xn(pe, 3, (bank[0], bank[1]))
            pe.wait_ge(xnT_ready, 6)
            for t in range(TT):
                for half in range(2):
                    for c in range(DC):
                        mm = nc.tensor.matmul(bank[2 + 2 * t + half][:, :], lhsT=xnT[:, c, t * P:(t + 1) * P],
                                              rhs=w_sim[:, c, half * 512:(half + 1) * 512],
                                              start=c == 0, stop=c == DC - 1)
                    mm.then_inc(sim_psum, 1)
            pe.wait_ge(experts_in, 32)
            for e in range(ET):
                b = e // 2
                if e % 2 == 0 and b >= 4:
                    pe.wait_ge(gelu_ready, b - 3)
                for c in range(DC):
                    mm = nc.tensor.matmul(bank[(6, 7, 0, 1)[b % 4]][:, (e % 2) * T:(e % 2 + 1) * T],
                                          lhsT=downT[:, c, e * P:(e + 1) * P], rhs=xnT[:, c, :],
                                          start=c == 0, stop=c == DC - 1)
                if e % 2:
                    mm.then_inc(down_psum, 1)
                if e == ET - 7:
                    pe.wait_ge(chosen_ready, 3)
                    for k in range(3):
                        mm = nc.tensor.transpose(bank[2][:, k * P:(k + 1) * P], chosen[:, k, :], ident[:, :])
                    mm.then_inc(chosenT_psum, 1)
            with pe.Fori(0, P // GS // 2) as i:
                two = pe.snap(i * 2)
                for g in range(2):
                    pe.wait_ge(hot_ready, two + (g + 1))
                    pe.wait_ge(hidden_ready, two + (g + 1))
                    for t in range(TT):
                        own = slice(64 * t, 64 * t + 64)
                        for s in range(GS):
                            for w in range(3):
                                mm = nc.tensor.matmul(
                                    bank[2 + 2 * g + t][:, :].rearrange("p (h s) -> p h s", h=ET)[:, :, s],
                                    lhsT=hot_lo[own, g, :, s], rhs=hot_hi[own, g, w, :, s], start=w == 0, stop=w == 2)
                    mm.then_inc(mixw_psum, 1)
            pe.wait_ge(gelu_ready, ET // 2)
            pe.wait_ge(hidden_ready, 2 + P // GS)
            pe.wait_ge(up_in, 32)
            for t in range(TT):
                for e in range(ET):
                    mm = nc.tensor.matmul(bank[6][:, t * D:(t + 1) * D], lhsT=hidden[:, e, t * P:(t + 1) * P],
                                          rhs=up[:, e, :], start=e == 0, stop=e == ET - 1)
            mm.then_inc(y_psum, 1)

            turn_xn(pe, 4, (bank[0], bank[1]))
            pe.wait_ge(late_w_in, 128)
            pe.wait_ge(xnT_ready, 8)
            for m in range(DC):
                for c in range(DC):
                    mm = nc.tensor.matmul(bank[2][:, m * T:(m + 1) * T], lhsT=wq4[:, c, m * P:(m + 1) * P],
                                          rhs=xnT[:, c, :], start=c == 0, stop=c == DC - 1)
            mm.then_inc(q4_psum, 1)
            pe.wait_ge(q4_ready, 2)
            for m, rows_m in ((0, P), (1, CD - P + 1)):
                for c in range(DC):
                    mm = nc.tensor.matmul(bank[3 + m][0:rows_m, 0:T], lhsT=wk4T[:, c, m * P:m * P + rows_m],
                                          rhs=q4T[:, c, :], start=c == 0, stop=c == DC - 1)
                mm.then_inc(qk4_psum, 1)
            pe.wait_ge(ctxT_in, 32)
            pe.wait_ge(ctx_rows_in, 16)
            pe.wait_ge(ones4_set, 2)
            pe.wait_ge(qk4_ready, 2)

            def scores4(u):
                i, t = u // TT, u % TT
                if u >= 2:
                    pe.wait_ge(p4_ready, 2 * (u - 1))
                for half in range(2):
                    dst = bank[2 * (u % 2) + half][:, :]
                    keys = slice(i * 1024 + half * 512, i * 1024 + half * 512 + 512)
                    nc.tensor.matmul(dst, lhsT=qk_a[:, t * P:(t + 1) * P], rhs=ctxT_a[:, keys], start=True, stop=False)
                    mm = nc.tensor.matmul(dst, lhsT=qk_b[:, t * P:(t + 1) * P], rhs=ctxT_b[:, keys],
                                          start=False, stop=True)
                mm.then_inc(s4_psum, 1)

            def turn4(u):
                for half in range(2):
                    pe.wait_ge(p4_ready, 2 * u + half + 1)
                    if u >= 1:
                        pe.wait_ge((p4T_ready0, p4T_ready1)[half], u)
                    for k in range(4):
                        mm = nc.tensor.transpose(bank[4 + half][:, k * P:(k + 1) * P],
                                                 p4[:, u % 2, half * 512 + k * P:half * 512 + (k + 1) * P], ident[:, :])
                    mm.then_inc(p4T_psum, 1)

            def values4(u):
                i = u // TT
                if u >= 2:
                    pe.wait_ge(o4_added, u - 1)
                for k in range(8):
                    if k % 4 == 0:
                        pe.wait_ge((p4T_ready0, p4T_ready1)[k // 4], u + 1)
                    mm = nc.tensor.matmul(bank[6 + u % 2][:, 0:CD], lhsT=p4T[:, u % 2, k * P:(k + 1) * P],
                                          rhs=ctx_rows[:, i * 8 + k, :], start=k == 0, stop=k == 7)
                mm.then_inc(o4_psum, 1)

            for u in range(UNITS + 2):
                if u < UNITS:
                    scores4(u)
                if 1 <= u <= UNITS:
                    turn4(u - 1)
                if u >= 2:
                    values4(u - 2)
            pe.wait_ge(o4_normed, 2)
            for t in range(TT):
                mm = nc.tensor.transpose(bank[0][:, t * P:(t + 1) * P], o4[:, t, 0:P], ident[:, :])
            mm.then_inc(o4T_psum, 1)
            for t in range(TT):
                mm = nc.tensor.transpose(bank[1][0:CD - P, t * P:(t + 1) * P], o4[:, t, P:CD], ident[:, :])
            mm.then_inc(o4T_psum, 1)
            pe.wait_ge(o4T_ready, 2)
            for t in range(TT):
                nc.tensor.matmul(bank[2][:, t * D:(t + 1) * D], lhsT=o4T_a[:, t * P:(t + 1) * P], rhs=wv4a,
                                 start=True, stop=False)
                mm = nc.tensor.matmul(bank[2][:, t * D:(t + 1) * D], lhsT=o4T_b[:, t * P:(t + 1) * P], rhs=wv4b,
                                      start=False, stop=True)
            mm.then_inc(y_psum, 1)
            turn_xn(pe, 5, (bank[0], bank[1]))
            pe.wait_ge(xnT_ready, 10)
            for w in range(2):
                for m in range(DC):
                    for c in range(DC):
                        mm = nc.tensor.matmul(bank[3 + w][:, m * T:(m + 1) * T], lhsT=w5[:, w, c, m * P:(m + 1) * P],
                                              rhs=xnT[:, c, :], start=c == 0, stop=c == DC - 1)
                mm.then_inc(qkv5_psum, 1)
            for t in range(TT):
                dst = bank[5][:, t * D:(t + 1) * D]
                nc.tensor.matmul(dst, lhsT=ones[0:1, :], rhs=row("L1_attn_bv"), start=True, stop=False)
                for c in range(DC):
                    mm = nc.tensor.matmul(dst, lhsT=xnT[:, c, t * P:(t + 1) * P], rhs=w5[:, 2, c, :],
                                          start=False, stop=c == DC - 1)
            mm.then_inc(qkv5_psum, 1)
            pe.wait_ge(qkv5_ready, 4)
            for t in range(TT):
                for c in range(DC):
                    mm = nc.tensor.matmul(bank[6 + t][:, 0:T], lhsT=q5T[:, c, t * P:(t + 1) * P], rhs=k5T[:, c, :],
                                          start=c == 0, stop=c == DC - 1)
                mm.then_inc(s5_psum, 1)
            for t in range(TT):
                pe.wait_ge(p5_ready, t + 1)
                for j in range(TT):
                    mm = nc.tensor.transpose(bank[0][:, (2 * t + j) * P:(2 * t + j + 1) * P], p5[:, t, j * P:(j + 1) * P],
                                             ident[:, :])
            mm.then_inc(p5T_psum, 1)
            pe.wait_ge(p5T_ready, 1)
            pe.wait_ge(v5_ready, 1)
            for t in range(TT):
                for j in range(TT):
                    mm = nc.tensor.matmul(bank[1][:, t * D:(t + 1) * D],
                                          lhsT=p5T[:, (2 * t + j) * P:(2 * t + j + 1) * P], rhs=v5[:, j, :],
                                          start=j == 0, stop=j == TT - 1)
            mm.then_inc(o5_psum, 1)
            turn_and_project(pe, 2, att_flat, (bank[2], bank[3]), w5[:, 3], row("L1_attn_bo"), bank[4])
            turn_xn(pe, 6, (bank[0], bank[1]))
            pe.wait_ge(xnT_ready, 12)
            pe.wait_ge(moe_small_in, 64)
            for t in range(TT):
                for c in range(DC):
                    mm = nc.tensor.matmul(bank[2][:, t * MOE:(t + 1) * MOE], lhsT=xnT[:, c, t * P:(t + 1) * P],
                                          rhs=wr6[:, c, :], start=c == 0, stop=c == DC - 1)
            mm.then_inc(router_psum, 1)
            pe.wait_ge(moe_in, 64)

            def rows_of(m):
                return min(P, FALL - m * P)

            def gate_and_up(m):
                n = rows_of(m)
                if m >= 2:
                    pe.wait_ge(silu_ready, m - 1)
                    pe.wait_ge(h6_ready, m - 1)
                for w, b, psum in ((wg6, 3, gate_psum), (wu6, 5, None)):
                    for c in range(DC):
                        mm = nc.tensor.matmul(bank[b + m % 2][0:n, 0:T], lhsT=w[:, c, m * P:m * P + n],
                                              rhs=xnT[:, c, :], start=c == 0, stop=c == DC - 1)
                    if psum:
                        mm.then_inc(psum, 1)
                if m == 0:
                    pe.wait_ge(w6_ready, 1)
                    for t in range(TT):
                        mm = nc.tensor.transpose(bank[2][0:MOE + 1, t * P:(t + 1) * P], r6[:, 5, t, :], ident[:, :])
                    mm.then_inc(w6T_psum, 1)
                    pe.wait_ge(w6T_ready, 2)
                    pe.wait_ge(owner6_ready, 1)
                mm = nc.tensor.matmul(bank[5 + m % 2][0:n, T:2 * T], lhsT=owner6_r[0:OWNERS, m * P:m * P + n],
                                      rhs=w6T[0:OWNERS, :],
                                      start=True, stop=True)
                mm.then_inc(up6_psum, 1)

            def down(m):
                n = rows_of(m)
                pe.wait_ge(h6_ready, m + 1)
                for t in range(TT):
                    mm = nc.tensor.matmul(bank[(7, 0)[t]][:, 0:D], lhsT=h6[0:n, m, t * P:(t + 1) * P],
                                          rhs=wd6[0:n, m, :], start=m == 0, stop=m == FT - 1)
                if m == FT - 1:
                    mm.then_inc(y_psum, 1)

            for m in range(FT + 1):
                if m < FT:
                    gate_and_up(m)
                if m >= 1:
                    down(m - 1)

        @block.scalar
        def _(act):
            take_root(act, 1)
            take_root(act, 2)
            act.wait_ge(small_in, 80)
            act.wait_ge(xnT_psum, 1)
            nc.scalar.activation(xnT[:, 0, :], bank[1][:, 0:T], ACT.Identity, bias=column("L0_xattn_ln_beta", 0),
                                 scale=column("L0_xattn_ln_gamma", 0)).then_inc(xnT_ready, 1)
            for j in range(4):
                two = slice(2 * j, 2 * j + 2)
                act.wait_ge(q_psum, j + 1)
                nc.scalar.activation(qT[:, two, :], bank[2 + j][:, :].rearrange("p (m q) -> p m q", m=2),
                                     ACT.Copy, scale=XD ** -0.5).then_inc(q_ready, 1)
                act.wait_ge(q_ready, j + 1)
                for s in range(2):
                    own, other = slice(64 * s, 64 * s + 64), slice(64 * (1 - s), 64 * (1 - s) + 64)
                    nc.scalar.copy(q_upper[other, two, s, :], qT[own, two, :]).then_inc(q_twice, 1)
            act.wait_ge(range_set, 1)
            n_blocks = act.value_load(rng_i[0:1, 1:2], min_val=1, max_val=NBLK)
            with act.Fori(0, n_blocks) as i:
                base = act.snap(i * XH)
                base8 = act.snap(i * 8)
                for j in range(8):
                    act.wait_ge(k_psum, base8 + (j + 1))
                    if j == 7:
                        act.wait_ge(q_twice, 12)
                    nc.scalar.copy(keys_of(2 * j)[0:64], bank[2 * (j % 2)][0:64, :])
                    nc.scalar.copy(keys_of(2 * j + 1)[64:128], bank[2 * (j % 2)][64:128, :]).then_inc(k_upper_set, 1)
                    act.wait_ge(v_psum, base8 + (j + 1))
                    nc.scalar.copy(v_blk[:, j // 2, (j % 2) * 512:(j % 2 + 1) * 512], bank[2 * (j % 2) + 1][:, :]
                                   ).then_inc(v_ready, 1)

                def exps(h):
                    act.wait_ge(nm_ready, base + (h + 1))
                    if h >= 2:
                        act.wait_ge(pT_psum, 2 * base + 2 * (h - 1))
                    for t in range(TT):
                        nc.scalar.activation(prob[:, h % 2, t, :], bank[2 * (h % 2) + t][:, :], ACT.Exp,
                                             scale=-1.0, bias=nm_new[:, h, t:t + 1],
                                             accum_out=l_blk[:, h, t:t + 1]).then_inc(prob_ready, 1)
                    act.wait_ge(diff_ready, base + (h + 1))
                    nc.scalar.activation(alpha[:, h, :], m_diff[:, h, :], ACT.Exp).then_inc(alpha_ready, 1)

                def copy_pT(h):
                    act.wait_ge(pT_psum, 2 * base + (2 * h + 2))
                    if h >= 2:
                        act.wait_ge(o_psum, base + (h - 1))
                    nc.scalar.copy(probT[:, h % 2, 1, :], bank[5][:, :]).then_inc(pT_ready1, 1)

                for h in range(XH + 1):
                    if h < XH:
                        exps(h)
                    if h >= 1:
                        copy_pT(h - 1)
            for j in range(0, 4, 2):
                act.wait_ge(oT_psum, j + 1)
                nc.scalar.copy(oT[:, 2 * j:2 * j + 2, :],
                               bank[j][:, :].rearrange("p (m q) -> p m q", m=2)).then_inc(oT_ready, 1)

            take_root(act, 3)
            for k in range(4):
                act.wait_ge(wsim_psum, k + 1)
                nc.scalar.copy(w_sim[:, k // 2, (k % 2) * 512:(k % 2 + 1) * 512], bank[(3, 5, 6, 7)[k]][:, :]
                               ).then_inc(wsim_ready, 1)
            act.wait_ge(xnT_psum, 2)
            nc.scalar.copy(xnT[:, 0, :], bank[0][:, 0:T]).then_inc(xnT_ready, 1)
            for m in range(4):
                act.wait_ge(qk2_psum, 3 + m // 2)
                ins = nc.scalar.activation(k2T[:, m, :], bank[4 + m // 2][:, (m % 2) * T:(m % 2 + 1) * T], ACT.Identity,
                                           bias=qk_bias[:, 4 + m:5 + m], scale=0.5).then_inc(k2_ready, 1)
            act.wait_ge(k2_ready, 4)
            nc.scalar.activation(k2sq, k2T, ACT.Square).then_inc(k2_ready, 1)

            def exp_features(arg, ready, f):
                for t in range(TT):
                    act.wait_ge(arg, t + 1)
                    nc.scalar.activation(f[:, t, :, 0:LM], f[:, t, :, 0:LM], ACT.Exp).then_inc(ready, 1)

            def copy_features(first, fT, ready):
                for k in range(2):
                    act.wait_ge(fT_psum, first + k)
                    nc.scalar.activation(fT[:, 2 * k:2 * k + 2, :], bank[k][:, :].rearrange("p (c n) -> p c n", c=2),
                                         ACT.Copy, bias=1e-4).then_inc(ready, 1)

            exp_features(fq_arg, fq_ready, fq)
            copy_features(1, fqT, fqT_ready)
            exp_features(fk_arg, fk_ready, fk)

            def exps2(h):
                act.wait_ge(s2_ready, h + 1)
                if h >= 2:
                    act.wait_ge(p2T_psum, h - 1)
                for t in range(TT):
                    nc.scalar.activation(p2[:, h % 2, t, :], s2[:, h % 2, t, :], ACT.Exp, scale=-1.0,
                                         bias=nm2[:, t, h:h + 1], accum_out=sum2[:, t, h:h + 1]).then_inc(p2_ready, 1)

            def copy_p2T(h):
                act.wait_ge(p2T_psum, h + 1)
                if h >= 2:
                    act.wait_ge(pv2_psum, h - 1)
                nc.scalar.copy(p2T[:, h % 2, :], bank[6 + h % 2][:, :]).then_inc(p2T_ready, 1)

            def two_chunks(b):
                return bank[b][:, :].rearrange("p (c n) -> p c n", c=2)

            for h in range(LH + 1):
                if h < LH:
                    exps2(h)
                if h >= 1:
                    copy_p2T(h - 1)
                if h == 4:
                    copy_features(3, fkT, fkT_ready)
                if h == LH // 2 + 2:
                    act.wait_ge(pv2_psum, LH // 2)
                    nc.scalar.copy(pvT[:, 0:2, :], two_chunks(2)).then_inc(pvT_ready, 1)
            act.wait_ge(pv2_psum, LH)
            nc.scalar.copy(pvT[:, 2:4, :], two_chunks(3)).then_inc(pvT_ready, 1)
            act.wait_ge(gap_ready, 1)
            nc.scalar.activation(stat[:, 1], stat[:, 0], ACT.Exp, scale=-1.0).then_inc(gap_exp, 1)
            for k in range(2):
                act.wait_ge(hv_psum, 2 * k + 2)
                nc.scalar.copy(hvT[:, 2 * k:2 * k + 2, :], two_chunks((3, 5)[k])).then_inc(hvT_ready, 1)
            act.wait_ge(attT_psum, 1)
            nc.scalar.copy(attT[:, 0, :], bank[0][:, 0:T]).then_inc(attT_ready, 1)

            take_root(act, 4)
            take_root(act, 5)
            act.wait_ge(xnT_psum, 3)
            nc.scalar.activation(xnT[:, 0, :], bank[0][:, 0:T], ACT.Copy, scale=column("L0_ffn_norm_w", 0)
                                 ).then_inc(xnT_ready, 1)
            for b in range(ET // 2):
                act.wait_ge(down_psum, b + 1)
                nc.scalar.activation(hidden[:, 2 * b:2 * b + 2, :],
                                     bank[(6, 7, 0, 1)[b % 4]][:, :].rearrange("p (e t) -> p e t", e=2), ACT.Gelu
                                     ).then_inc(gelu_ready, 1)

            take_root(act, 6)
            act.wait_ge(xnT_psum, 4)
            nc.scalar.copy(xnT[:, 0, :], bank[0][:, 0:T]).then_inc(xnT_ready, 1)
            act.wait_ge(qk4_psum, 1)
            nc.scalar.copy(qk_a, bank[3][:, 0:T]).then_inc(qk4_ready, 1)

            def exps4(u):
                t = u % TT
                act.wait_ge(nm4_ready, u + 1)
                if u >= 2:
                    act.wait_ge(p4T_psum, 2 * (u - 1))
                for half in range(2):
                    nc.scalar.activation(p4[:, u % 2, half * 512:(half + 1) * 512], bank[2 * (u % 2) + half][:, :],
                                         ACT.Exp, bias=nm4_new[:, t:t + 1], accum_out=sum4[:, u, half:half + 1]
                                         ).then_inc(p4_ready, 1)
                act.wait_ge(diff4_ready, u + 1)
                nc.scalar.activation(alpha4[:, u:u + 1], diff4[:, u:u + 1], ACT.Exp).then_inc(alpha4_ready, 1)

            def copy_p4T(u):
                act.wait_ge(p4T_psum, 2 * u + 1)
                if u >= 2:
                    act.wait_ge(o4_psum, u - 1)
                nc.scalar.copy(p4T[:, u % 2, 0:512], bank[4][:, :]).then_inc(p4T_ready0, 1)

            for u in range(UNITS + 1):
                if u < UNITS:
                    exps4(u)
                if u >= 1:
                    copy_p4T(u - 1)
            act.wait_ge(o4T_psum, 1)
            nc.scalar.copy(o4T_a, bank[0][:, 0:T]).then_inc(o4T_ready, 1)
            take_root(act, 7)
            act.wait_ge(xnT_psum, 5)
            nc.scalar.copy(xnT[:, 0, :], bank[0][:, 0:T]).then_inc(xnT_ready, 1)
            act.wait_ge(qkv5_psum, 2)
            for m in range(DC):
                nc.scalar.activation(k5T[:, m, :], bank[4][:, m * T:(m + 1) * T], ACT.Identity,
                                     bias=column("L1_attn_bk", m)).then_inc(qkv5_ready, 1)
            for t in range(TT):
                act.wait_ge(s5_ready, t + 1)
                nc.scalar.activation(p5[:, t, :], s5[:, t, :], ACT.Exp, scale=-1.0, bias=nm4_new[:, t:t + 1],
                                     accum_out=l4[:, t:t + 1]).then_inc(p5_ready, 1)
            act.wait_ge(attT_psum, 3)
            nc.scalar.copy(attT[:, 0, :], bank[2][:, 0:T]).then_inc(attT_ready, 1)
            take_root(act, 8)
            act.wait_ge(xnT_psum, 6)
            nc.scalar.copy(xnT[:, 0, :], bank[0][:, 0:T]).then_inc(xnT_ready, 1)
            act.wait_ge(router_psum, 1)
            nc.scalar.activation(r6[:, 0, :, 0:MOE], bank[2][:, 0:TT * MOE].rearrange("p (t e) -> p t e", t=TT),
                                 ACT.Exp, scale=-1.0).then_inc(router_exp, 1)
            for m in range(FT):
                n = min(P, FALL - m * P)
                act.wait_ge(gate_psum, m + 1)
                if m >= 2:
                    act.wait_ge(h6_ready, m - 1)
                nc.scalar.activation(silu6[0:n, m % 2, :], bank[3 + m % 2][0:n, 0:T], ACT.Silu).then_inc(silu_ready, 1)

        @block.vector
        def _(dve):
            step = Chain(dve, dve_step)
            nc.vector.memset(ones[:, :], 1.0).then_inc(consts_set, 1)
            nc.vector.memset(nm_run[:, :, :], -2 * MASKED).then_inc(consts_set, 1)
            nc.vector.memset(l_run[:, :, :], 0.0).then_inc(ctx_free, 1)
            step(nc.vector.memset(o_acc, 0.0))
            dve.wait_ge(small_in, 80)
            dve.wait_ge(x_in, 16)
            def find_blocks():
                dve.wait_ge(mask_in, 16)
                step(nc.vector.tensor_reduce(seen[:, :, :],
                                             mask_w.bitcast(U32).rearrange("p (t b w) -> p t b w", t=TT, b=NBLK),
                                             AX.X, ALU.max))
                step(nc.vector.tensor_scalar(seen[:, :, :], seen[:, :, :], 1.0, None, ALU.min))
                nc.vector.tensor_reduce(any_q[:, :], seen[:, :, :], AX.X, ALU.max).then_inc(blocks_seen, 1)

            def find_range():
                dve.wait_ge(blocks_counted, 1)
                r = [rng[:, k * NBLK:(k + 1) * NBLK] for k in range(8)]
                nc.vector.tensor_copy(rng[:, 0:2 * NBLK], bank[0][0:1, 0:2 * NBLK]).then_inc(dve_step, 1)
                step.n += 1
                dve.wait_ge(dve_step, step.n)
                step(nc.vector.tensor_tensor(r[2], r[0], r[1], ALU.add))
                step(nc.vector.tensor_scalar(r[2], r[2], 1.0, None, ALU.min))
                step(nc.vector.tensor_tensor(r[3], r[2], blk_lo[:, :], ALU.mult))
                step(nc.vector.tensor_tensor(r[4], r[2], blk_hi[:, :], ALU.mult))
                step(nc.vector.tensor_reduce(r[5][:, 0:1], r[3], AX.X, ALU.min))
                step(nc.vector.tensor_reduce(r[5][:, 1:2], r[4], AX.X, ALU.max))
                step(nc.vector.tensor_scalar(r[6][:, 0:1], r[5][:, 0:1], float(NBLK), float(NBLK - 1), ALU.add, ALU.min))
                step(nc.vector.tensor_tensor(r[6][:, 1:2], r[5][:, 1:2], r[6][:, 0:1], ALU.subtract))
                step(nc.vector.tensor_scalar(r[6][:, 1:2], r[6][:, 1:2], 1.0, None, ALU.max))
                nc.vector.tensor_copy(rng_i[:, :], r[6][:, 0:2]).then_inc(range_set, 1)

            layer_norm(dve, step, x_res, xn)
            layer_norm(dve, step, xn, xn, after=xn_ready)
            dve.wait_ge(xnT_psum, 1)
            nc.vector.tensor_scalar(xnT[:, 1, :], bank[7][:, 0:T], column("L0_xattn_ln_gamma", 1), column("L0_xattn_ln_beta", 1),
                                    ALU.mult, ALU.add).then_inc(xnT_ready, 1)
            find_blocks()
            dve.wait_ge(wkv_in, 48)
            nc.vector.tensor_copy(wkv_upper, wkv[64:128, 1, :]).then_inc(wkv_upper_set, 1)
            nc.vector.tensor_copy(wkv_parts[0:64], wkv[0:64, 1, :]).then_inc(wkv_split, 1)
            find_range()
            dve.wait_ge(wkv_upper_set, 1)
            nc.vector.tensor_tensor(wkv_parts[64:128], wkv[64:128, 1, :], wkv_upper.bitcast(F32),
                                    ALU.subtract).then_inc(wkv_split, 1)
            for j in range(4):
                two = slice(2 * j, 2 * j + 2)
                dve.wait_ge(q_ready, j + 1)
                for s in range(2):
                    own = slice(64 * s, 64 * s + 64)
                    nc.vector.tensor_copy(q_upper[own, two, s, :], qT[own, two, :]).then_inc(q_split, 1)
            dve.wait_ge(range_set, 1)
            first = dve.value_load(rng_i[0:1, 0:1], min_val=0, max_val=NBLK - 1)
            n_blocks = dve.value_load(rng_i[0:1, 1:2], min_val=1, max_val=NBLK)
            mask_b = mask_w.bitcast(U8).rearrange("p (t k) -> p t k", t=TT)
            with dve.Fori(0, n_blocks) as i:
                base = dve.snap(i * XH)
                base8 = dve.snap(i * 8)
                at = within(dve, first + i) * BLK
                dve.wait_ge(ctx_landed, i * 48 + 48)
                nc.vector.tensor_copy(ctx_b_upper[:, :], ctx_b[:, :]).then_inc(ctx_upper_set, 1)
                dve.wait_ge(ctx_upper_set, i + 1)
                nc.vector.tensor_tensor(ctx_b_rest[:, :], ctx_b[:, :], ctx_b_upper[:, :].bitcast(F32), ALU.subtract
                                        ).then_inc(ctx_split, 1)
                nc.vector.tensor_scalar(bias_h[:, :, :], mask_b[:, :, bass.ds(at, BLK)], -1.0, -MASKED,
                                        ALU.add, ALU.mult).then_inc(bias_ready, 1)
                dve.wait_ge(bias_ready, i + 1)
                for j in range(8):
                    dve.wait_ge(k_upper_set, base8 + (j + 1))
                    whole, even, odd = bank[2 * (j % 2)], keys_of(2 * j), keys_of(2 * j + 1)
                    nc.vector.tensor_tensor(even[64:128], whole[0:64, :], even[0:64].bitcast(F32), ALU.subtract)
                    nc.vector.tensor_tensor(odd[0:64], whole[64:128, :], odd[64:128].bitcast(F32), ALU.subtract
                                            ).then_inc(k_split, 1)

                def maxima(h):
                    dve.wait_ge(s_ready, base + (h + 1))
                    nc.vector.memset(turns[:, h:h + 1], 0.0)
                    for t in range(TT):
                        ins = nc.vector.tensor_tensor_reduce(bank[2 * (h % 2) + t][:, :], bank[2 * (h % 2) + t][:, :],
                                                             bias_h[:, t, :], -1.0, 3e38, ALU.add, ALU.min,
                                                             accum_out=nm_blk[:, h, t:t + 1])
                    ins.then_inc(nm_blk_ready, 1)
                    dve.wait_ge(nm_blk_ready, base + (h + 1))
                    nc.vector.tensor_tensor(nm_new[:, h, :], nm_blk[:, h, :], nm_run[:, h, :],
                                            ALU.min).then_inc(nm_ready, 1)
                    dve.wait_ge(nm_ready, base + (h + 1))
                    nc.vector.tensor_tensor(m_diff[:, h, :], nm_new[:, h, :], nm_run[:, h, :],
                                            ALU.subtract).then_inc(diff_ready, 1)

                def copy_pT(h):
                    dve.wait_ge(pT_psum, 2 * base + (2 * h + 1))
                    if h >= 2:
                        dve.wait_ge(o_psum, base + (h - 1))
                    nc.vector.tensor_copy(probT[:, h % 2, 0, :], bank[4][:, :]).then_inc(pT_ready0, 1)

                def add_values(h):
                    dve.wait_ge(o_psum, base + (h + 1))
                    dve.wait_ge(alpha_ready, base + (h + 1))
                    for t in range(TT):
                        o = o_acc[:, t, h * XD:(h + 1) * XD]
                        ins = nc.vector.scalar_tensor_tensor(o, o, alpha[:, h, t:t + 1],
                                                             bank[6 + h % 2][:, t * XD:(t + 1) * XD],
                                                             ALU.mult, ALU.add)
                    ins.then_inc(o_added, 1)

                for h in range(XH + 2):
                    if h < XH:
                        maxima(h)
                    if 1 <= h <= XH:
                        copy_pT(h - 1)
                    if h >= 2:
                        add_values(h - 2)
                nc.vector.tensor_tensor(l_run[:, :, :], l_run[:, :, :], alpha[:, :, :], ALU.mult).then_inc(l_scaled, 1)
                dve.wait_ge(l_scaled, i + 1)
                nc.vector.tensor_tensor(l_run[:, :, :], l_run[:, :, :], l_blk[:, :, :], ALU.add)
                nc.vector.tensor_copy(nm_run[:, :, :], nm_new[:, :, :]).then_inc(run_kept, 1)
                dve.wait_ge(run_kept, i + 1)
            step(nc.vector.reciprocal(is_row[:, :], any_q[:, :]))
            step(nc.vector.tensor_tensor(is_row[:, :], is_row[:, :], any_q[:, :], ALU.mult))
            step(nc.vector.reciprocal(l_run[:, :, :], l_run[:, :, :]))
            for t in range(TT):
                ins = nc.vector.tensor_scalar(l_blk[:, :, t], l_run[:, :, t], is_row[:, t:t + 1], None, ALU.mult)
            step(ins)
            for t in range(TT):
                o = o_acc[:, t, :].rearrange("p (h d) -> p h d", h=XH)
                ins = nc.vector.tensor_tensor(o, o, l_blk[:, :, t].unsqueeze(2).to_broadcast([P, XH, XD]), ALU.mult)
            ins.then_inc(o_normed, 1)
            for j in range(1, 4, 2):
                dve.wait_ge(oT_psum, j + 1)
                nc.vector.tensor_copy(oT[:, 2 * j:2 * j + 2, :],
                                      bank[j][:, :].rearrange("p (m q) -> p m q", m=2)).then_inc(oT_ready, 1)
            dve.wait_ge(y_psum, 1)
            nc.vector.tensor_tensor(x_res[:, :, :], x_res[:, :, :],
                                    bank[4][:, :].rearrange("p (t d) -> p t d", t=TT), ALU.add).then_inc(x_ready, 1)
            dve.wait_ge(x_ready, 1)

            layer_norm(dve, step, x_res, xn, after=xn_ready)
            nc.vector.memset(v2[:, :, :, 16:17], 1.0)
            nc.vector.memset(v2[:, :, :, 17:32], 0.0)
            nc.vector.memset(part(region_a, 4096, 2048), 0.0)
            dve.wait_ge(lin_in, 128)
            step(nc.vector.tensor_scalar(qk_bias[:, :], qk_bias[:, :], 0.5, None, ALU.mult))
            dve.wait_ge(xnT_psum, 2)
            nc.vector.tensor_copy(xnT[:, 1, :], bank[1][:, 0:T]).then_inc(xnT_ready, 1)
            for m in range(4):
                dve.wait_ge(qk2_psum, 1 + m // 2)
                nc.vector.tensor_scalar(q2T[:, m, :], bank[2 + m // 2][:, (m % 2) * T:(m % 2 + 1) * T], 0.5,
                                        qk_bias[:, m:m + 1], ALU.mult, ALU.add).then_inc(q2_ready, 1)
            dve.wait_ge(q2_ready, 4)
            nc.vector.tensor_tensor(q2sq, q2T, q2T, ALU.mult).then_inc(q2_ready, 1)
            dve.wait_ge(v2_psum, 1)
            nc.vector.tensor_copy(v2[:, :, :, 0:16], bank[6][:, :].rearrange("p (t h d) -> p t h d", t=TT, h=LH)
                                  ).then_inc(v2_ready, 1)

            def features(b):
                return bank[b][:, :].rearrange("p (h m) -> p h m", h=LH)[:, :, 0:LM]

            for t in range(TT):
                dve.wait_ge(fq_psum, t + 1)
                step(nc.vector.tensor_reduce(q_ls[:, t, :], features(t), AX.X, ALU.max))
                nc.vector.tensor_tensor(fq[:, t, :, 0:LM], features(t),
                                        q_ls[:, t, :].unsqueeze(2).to_broadcast([P, LH, LM]), ALU.subtract
                                        ).then_inc(fq_arg, 1)
            for t in range(TT):
                dve.wait_ge(fk_psum, t + 1)
                ins = nc.vector.tensor_reduce(k_ls[:, t, :], features(2 + t), AX.X, ALU.max)
            step(ins)
            nc.vector.tensor_tensor(k_max[:, :], k_ls[:, 0, :], k_ls[:, 1, :], ALU.max).then_inc(k_maxed, 1)
            dve.wait_ge(k_stab_ready, 1)
            for t in range(TT):
                nc.vector.tensor_tensor(fk[:, t, :, 0:LM], features(2 + t),
                                        k_stab[:, :].unsqueeze(2).to_broadcast([P, LH, LM]), ALU.subtract
                                        ).then_inc(fk_arg, 1)
            for h in range(LH):
                dve.wait_ge(s2_psum, h + 1)
                if h >= 2:
                    dve.wait_ge(p2_ready, 2 * h - 2)
                for t in range(TT):
                    ins = nc.vector.tensor_tensor_reduce(s2[:, h % 2, t, :], bank[4 + h % 2][:, t * T:(t + 1) * T],
                                                         band[:, t, :], -1.0, 3e38, ALU.add, ALU.min,
                                                         accum_out=nm2[:, t, h:h + 1])
                ins.then_inc(s2_ready, 1)
            dve.wait_ge(s2_ready, LH)
            step(nc.vector.tensor_tensor(stat[:, 0], nm2[:, :, :], q_ls[:, :, :], ALU.add))
            for t in range(TT):
                ins = nc.vector.tensor_tensor(stat[:, 0, t], stat[:, 0, t], k_stab[:, :], ALU.add)
            ins.then_inc(gap_ready, 1)
            for c in range(4):
                own = (6, 7, 2) if c % 2 == 0 else (0, 1, 4)
                for k in range(2):
                    dve.wait_ge(mix_psum, 3 * c + k + 1)
                    nc.vector.tensor_tensor(mixed0[:, 4 * c + 2 * k:4 * c + 2 * k + 2, :],
                                            bank[own[k]][:, :].rearrange("p (h i) -> p h i", h=2),
                                            mixT[:, 0:T].unsqueeze(1).to_broadcast([P, 2, T]), ALU.mult
                                            ).then_inc(mix_ready, 1)
                dve.wait_ge(mix_psum, 3 * c + 3)
                nc.vector.tensor_tensor(mixed1[:, 4 * c:4 * c + 4, :],
                                        bank[own[2]][:, :].rearrange("p (h i) -> p h i", h=4),
                                        mixT[:, T:T + P].unsqueeze(1).to_broadcast([P, 4, P]), ALU.mult
                                        ).then_inc(mix_ready, 1)
            dve.wait_ge(gap_exp, 1)
            dve.wait_ge(p2_ready, 2 * LH)
            nc.vector.tensor_tensor(stat[:, 1], stat[:, 1], sum2[:, :, :], ALU.mult)
            step(nc.vector.reciprocal(stat[:, 3], sum2[:, :, :]))

            def per_head(k, t):
                return stat[:, k, t].unsqueeze(2).to_broadcast([P, LH, 16])

            def by_head(b):
                return bank[b][:, :].rearrange("p (h d) -> p h d", h=LH)

            dve.wait_ge(turned_psum, 1)
            for t in range(TT):
                nc.vector.tensor_tensor(att[:, t], by_head(6 + t)[:, :, 0:16], per_head(3, t), ALU.mult)
            dve.wait_ge(turned_psum, 2)
            for t in range(TT):
                ins = nc.vector.tensor_scalar(stat[:, 2, t], by_head(t)[:, :, 16], 1e-24, None, ALU.max)
            step(ins)
            step(nc.vector.tensor_tensor(stat[:, 2], stat[:, 2], stat[:, 1], ALU.add))
            step(nc.vector.reciprocal(stat[:, 2], stat[:, 2]))
            for t in range(TT):
                ins = nc.vector.tensor_tensor(lin[:, t], by_head(t)[:, :, 0:16], per_head(2, t), ALU.mult)
            step(ins)
            for t in range(TT):
                ins = nc.vector.tensor_tensor(att[:, t], att[:, t], lin[:, t], ALU.add)
            ins.then_inc(att_ready, 1)
            dve.wait_ge(attT_psum, 2)
            nc.vector.tensor_copy(attT[:, 1, :], bank[1][:, 0:T]).then_inc(attT_ready, 1)
            dve.wait_ge(y_psum, 2)
            nc.vector.tensor_tensor(x_res[:, :, :], x_res[:, :, :],
                                    bank[2][:, :].rearrange("p (t d) -> p t d", t=TT), ALU.add).then_inc(x_ready, 1)
            dve.wait_ge(x_ready, 2)

            layer_norm(dve, step, x_res, xn)
            for t in range(TT):
                ins = nc.vector.tensor_tensor_reduce(squares[:, t], xn[:, t], xn[:, t], 1.0, 0.0, ALU.mult, ALU.add,
                                                     accum_out=mv[:, t, 1:2])
            step(ins)
            nc.vector.tensor_scalar(var[:, :], mv[:, :, 1], 1.0 / D, EPS_OF_NORM[norms[0]], ALU.mult, ALU.add
                                    ).then_inc(var_ready, 1)
            norms[0] += 1
            dve.wait_ge(root_ready, norms[0])
            refine_rstd(dve, step)
            for t in range(TT):
                nc.vector.tensor_scalar(xn[:, t], xn[:, t], rstd[:, t:t + 1], None, ALU.mult).then_inc(xn_ready, 1)
            dve.wait_ge(xnT_psum, 3)
            nc.vector.tensor_scalar(xnT[:, 1, :], bank[1][:, 0:T], column("L0_ffn_norm_w", 1), None, ALU.mult
                                    ).then_inc(xnT_ready, 1)
            dve.wait_ge(iota_in, 16)
            nc.vector.tensor_copy(iota_h, iota.unsqueeze(2).to_broadcast([P, P, GS]))
            for t in range(TT):
                for half in range(2):
                    dve.wait_ge(sim_psum, 2 * t + half + 1)
                    sims = [bank[2 + 2 * t + half][:, k * NK:(k + 1) * NK] for k in range(EH)]
                    for k in range(EH):
                        ins = nc.vector.max(top[:, t, half * EH + k, :], sims[k])
                    step(ins)
                    for k in range(EH):
                        ins = nc.vector.max_index(top_i[:, t, half * EH + k, :], top[:, t, half * EH + k, :], sims[k])
            step(ins)
            nc.vector.tensor_copy(top_f, top_i)
            sided = top.rearrange("p t (h s) k -> p t h s k", s=2)
            for t in range(TT):
                ins = nc.vector.tensor_tensor(pairs[:, t].rearrange("p h (a b) -> p h a b", a=8),
                                              sided[:, t, :, 0, :].unsqueeze(3).to_broadcast([P, EH, 8, 8]),
                                              sided[:, t, :, 1, :].unsqueeze(2).to_broadcast([P, EH, 8, 8]), ALU.add)
            step(ins)
            for t in range(TT):
                for h in range(EH):
                    ins = nc.vector.max(best[:, t, h * 8:(h + 1) * 8], pairs[:, t, h, :])
            step(ins)
            for t in range(TT):
                for h in range(EH):
                    ins = nc.vector.max_index(best_i[:, t, h * 8:(h + 1) * 8], best[:, t, h * 8:(h + 1) * 8],
                                              pairs[:, t, h, :])
            step(ins)
            nc.vector.tensor_scalar(chosen[:, 2, :], best.rearrange("p t k -> p (t k)"), 0.0, None, ALU.max
                                    ).then_inc(chosen_ready, 1)
            nc.vector.tensor_scalar(rank_i[:, 0], best_i, 3, None, ALU.logical_shift_right)
            step(nc.vector.tensor_scalar(rank_i[:, 1], best_i, 7, None, ALU.bitwise_and))
            step(nc.vector.tensor_copy(rank, rank_i))
            for k in range(2):
                for t in range(TT):
                    step(nc.vector.tensor_tensor(pick, rank[:, k, t, :].unsqueeze(2).to_broadcast([P, 64, 8]),
                                                 iota[:, 0:8].unsqueeze(1).to_broadcast([P, 64, 8]), ALU.is_equal))
                    keys = top_f[:, t].rearrange("p (h s) k -> p h s k", s=2)[:, :, k, :]
                    picked = pick.rearrange("p (h k) j -> p h k j", h=EH)
                    step(nc.vector.tensor_tensor(picked, picked, keys.unsqueeze(2).to_broadcast([P, EH, 8, 8]),
                                                 ALU.mult))
                    step(nc.vector.tensor_reduce(side[:, k, t, :], pick, AX.X, ALU.add))
            step(nc.vector.scalar_tensor_tensor(expert, side[:, 0], float(NK), side[:, 1], ALU.mult, ALU.add))
            step(nc.vector.tensor_copy(expert_i, expert))
            nc.vector.tensor_scalar(split_i[:, 0], expert_i, P - 1, None, ALU.bitwise_and)
            step(nc.vector.tensor_scalar(split_i[:, 1], expert_i, 7, None, ALU.logical_shift_right))
            for k in range(2):
                nc.vector.tensor_copy(chosen[:, k, :], split_i[:, k].rearrange("p t k -> p (t k)")
                                      ).then_inc(chosen_ready, 1)
            dve.wait_ge(chosenT_psum, 1)
            step(nc.vector.tensor_copy(chosenT, bank[2][:, 0:3 * P].rearrange("p (s n) -> p s n", s=3)))
            for k in range(2):
                nc.vector.memset(stat[:, k, 0, 1:2], 0.0).then_inc(hidden_ready, 1)
            nc.vector.tensor_copy(chosen_h[:, 0:2], chosenT[:, 0:2])
            step(nc.vector.tensor_copy(chosen_h[:, 2], chosenT[:, 2]))
            step(nc.vector.tensor_tensor(rest_w, chosenT[:, 2], chosen_h[:, 2], ALU.subtract))
            step(nc.vector.tensor_copy(chosen_h[:, 3], rest_w))
            step(nc.vector.tensor_tensor(chosen_h[:, 4], rest_w, chosen_h[:, 3], ALU.subtract))

            def one_hots(g, n, at):
                def over(k, size):
                    return chosen_h[:, k, bass.ds(at, GS)].unsqueeze(1).to_broadcast([P, size, GS])

                nc.vector.tensor_tensor(hit_hi[:, g], iota_h[:, 0:ET], over(1, ET), ALU.is_equal).then_inc(hit_ready, 1)
                nc.vector.tensor_tensor(hot_lo[:, g], iota_h, over(0, P), ALU.is_equal)
                dve.wait_ge(hit_ready, n)
                for w in range(3):
                    ins = nc.vector.tensor_tensor(hot_hi[:, g, w], hit_hi[:, g], over(2 + w, ET), ALU.mult)
                ins.then_inc(hot_ready, 1)

            def weigh(g, n, at):
                dve.wait_ge(mixw_psum, n)
                for t in range(TT):
                    own = hidden[:, :, bass.ds(at + t * P, GS)]
                    ins = nc.vector.tensor_tensor(own, bank[2 + 2 * g + t][:, :].rearrange("p (h s) -> p h s", h=ET),
                                                  own, ALU.mult)
                ins.then_inc(hidden_ready, 1)

            one_hots(0, 1, 0)
            dve.wait_ge(gelu_ready, ET // 2)
            with dve.Fori(0, P // GS // 2 - 1) as i:
                two, at = dve.snap(i * 2), dve.snap(i * (2 * GS))
                one_hots(1, two + 2, at + GS)
                weigh(0, two + 1, at)
                one_hots(0, two + 3, at + 2 * GS)
                weigh(1, two + 2, at + GS)
            one_hots(1, P // GS, P - GS)
            weigh(0, P // GS - 1, P - 2 * GS)
            weigh(1, P // GS, P - GS)
            dve.wait_ge(y_psum, 3)
            nc.vector.tensor_tensor(x_res[:, :, :], x_res[:, :, :],
                                    bank[6][:, :].rearrange("p (t d) -> p t d", t=TT), ALU.add).then_inc(x_ready, 1)
            dve.wait_ge(x_ready, 3)

            layer_norm(dve, step, x_res, xn, after=xn_ready)
            nc.vector.memset(o4T_b[CD - P:CD - P + 1], 1.0).then_inc(ones4_set, 1)
            nc.vector.memset(nm4_run[:, :], 3e38)
            nc.vector.memset(l4[:, :], 0.0)
            step(nc.vector.memset(o4, 0.0))
            dve.wait_ge(xnT_psum, 4)
            nc.vector.tensor_copy(xnT[:, 1, :], bank[1][:, 0:T]).then_inc(xnT_ready, 1)
            dve.wait_ge(q4_psum, 1)
            for m in range(DC):
                nc.vector.tensor_scalar(q4T[:, m, :], bank[2][:, m * T:(m + 1) * T], column("L1_xattn_bq", m), None,
                                        ALU.add).then_inc(q4_ready, 1)
            dve.wait_ge(qk4_psum, 2)
            nc.vector.tensor_copy(qk_b, bank[4][0:CD - P + 1, 0:T]).then_inc(qk4_ready, 1)

            def maxima4(u):
                t = u % TT
                dve.wait_ge(s4_psum, u + 1)
                for half in range(2):
                    ins = nc.vector.tensor_reduce(nm4_half[:, t, half:half + 1], bank[2 * (u % 2) + half][:, :], AX.X,
                                                  ALU.max, negate=True)
                step(ins)
                nc.vector.scalar_tensor_tensor(nm4_new[:, t:t + 1], nm4_half[:, t, 0:1], nm4_run[:, t:t + 1],
                                               nm4_half[:, t, 1:2], ALU.min, ALU.min).then_inc(nm4_ready, 1)
                dve.wait_ge(nm4_ready, u + 1)
                nc.vector.tensor_tensor(diff4[:, u:u + 1], nm4_new[:, t:t + 1], nm4_run[:, t:t + 1], ALU.subtract
                                        ).then_inc(diff4_ready, 1)
                dve.wait_ge(diff4_ready, u + 1)
                step(nc.vector.tensor_copy(nm4_run[:, t:t + 1], nm4_new[:, t:t + 1]))

            def copy_p4T(u):
                dve.wait_ge(p4T_psum, 2 * u + 2)
                if u >= 2:
                    dve.wait_ge(o4_psum, u - 1)
                nc.vector.tensor_copy(p4T[:, u % 2, 512:1024], bank[5][:, :]).then_inc(p4T_ready1, 1)

            def add_values4(u):
                t = u % TT
                dve.wait_ge(o4_psum, u + 1)
                dve.wait_ge(alpha4_ready, u + 1)
                nc.vector.scalar_tensor_tensor(o4[:, t, :], o4[:, t, :], alpha4[:, u:u + 1], bank[6 + u % 2][:, 0:CD],
                                               ALU.mult, ALU.add).then_inc(o4_added, 1)

            def add_sums4(u):
                t = u % TT
                dve.wait_ge(alpha4_ready, u + 1)
                step(nc.vector.scalar_tensor_tensor(l4[:, t:t + 1], l4[:, t:t + 1], alpha4[:, u:u + 1],
                                                    sum4[:, u, 0:1], ALU.mult, ALU.add))
                step(nc.vector.tensor_tensor(l4[:, t:t + 1], l4[:, t:t + 1], sum4[:, u, 1:2], ALU.add))

            for u in range(UNITS + 2):
                if u < UNITS:
                    maxima4(u)
                if 1 <= u <= UNITS:
                    copy_p4T(u - 1)
                if u >= 2:
                    add_values4(u - 2)
                if 1 <= u <= UNITS:
                    add_sums4(u - 1)
            step(nc.vector.reciprocal(l4[:, :], l4[:, :]))
            dve.wait_ge(o4_added, UNITS)
            for t in range(TT):
                nc.vector.tensor_scalar(o4[:, t, :], o4[:, t, :], l4[:, t:t + 1], None, ALU.mult).then_inc(o4_normed, 1)
            dve.wait_ge(o4T_psum, 2)
            nc.vector.tensor_copy(o4T_b[0:CD - P], bank[1][0:CD - P, 0:T]).then_inc(o4T_ready, 1)
            dve.wait_ge(y_psum, 4)
            nc.vector.tensor_tensor(x_res[:, :, :], x_res[:, :, :],
                                    bank[2][:, :].rearrange("p (t d) -> p t d", t=TT), ALU.add).then_inc(x_ready, 1)
            dve.wait_ge(x_ready, 4)
            layer_norm(dve, step, x_res, xn, after=xn_ready)
            dve.wait_ge(xnT_psum, 5)
            nc.vector.tensor_copy(xnT[:, 1, :], bank[1][:, 0:T]).then_inc(xnT_ready, 1)
            dve.wait_ge(qkv5_psum, 1)
            for m in range(DC):
                nc.vector.tensor_scalar(q5T[:, m, :], bank[3][:, m * T:(m + 1) * T], column("L1_attn_bq", m),
                                        D ** -0.5, ALU.add, ALU.mult).then_inc(qkv5_ready, 1)
            dve.wait_ge(qkv5_psum, 3)
            nc.vector.tensor_copy(v5, bank[5][:, :].rearrange("p (t n) -> p t n", t=TT)).then_inc(v5_ready, 1)
            dve.wait_ge(masks5_in, 32)
            for t in range(TT):
                dve.wait_ge(s5_psum, t + 1)
                step(nc.vector.tensor_tensor(s5[:, t], bank[6 + t][:, 0:T], keep5[:, t], ALU.mult))
                nc.vector.tensor_tensor_reduce(s5[:, t], s5[:, t], fill5[:, t], -1.0, 3e38, ALU.add, ALU.min,
                                               accum_out=nm4_new[:, t:t + 1]).then_inc(s5_ready, 1)
            dve.wait_ge(p5T_psum, 1)
            nc.vector.tensor_copy(p5T, bank[0][:, :]).then_inc(p5T_ready, 1)
            step(nc.vector.reciprocal(l4[:, :], l4[:, :]))
            dve.wait_ge(o5_psum, 1)
            for t in range(TT):
                ins = nc.vector.tensor_scalar(att_flat[:, t], bank[1][:, t * D:(t + 1) * D], l4[:, t:t + 1], None, ALU.mult)
            ins.then_inc(att_ready, 1)
            dve.wait_ge(attT_psum, 4)
            nc.vector.tensor_copy(attT[:, 1, :], bank[3][:, 0:T]).then_inc(attT_ready, 1)
            dve.wait_ge(y_psum, 5)
            nc.vector.tensor_tensor(x_res[:, :, :], x_res[:, :, :],
                                    bank[4][:, :].rearrange("p (t d) -> p t d", t=TT), ALU.add).then_inc(x_ready, 1)
            dve.wait_ge(x_ready, 5)
            layer_norm(dve, step, x_res, xn, after=xn_ready)
            nc.vector.memset(r6[:, 5, :, MOE:MOE + 1], 1.0)
            step(nc.vector.tensor_scalar(w6T[0:OWNERS, :], ones[0:OWNERS, 0:1].to_broadcast([OWNERS, T]), 0.0, None,
                                         ALU.mult))
            dve.wait_ge(moe_small_in, 64)
            dve.wait_ge(xnT_psum, 6)
            nc.vector.tensor_copy(xnT[:, 1, :], bank[1][:, 0:T]).then_inc(xnT_ready, 1)
            dve.wait_ge(router_exp, 1)
            score, biased, best2, chosen1, weight = (r6[:, k, :, 0:MOE] for k in (0, 1, 2, 3, 5))
            step(nc.vector.tensor_scalar(score, score, 1.0, None, ALU.add))
            step(nc.vector.reciprocal(score, score))
            step(nc.vector.tensor_tensor(biased, score, ebias6.unsqueeze(1).to_broadcast([P, TT, MOE]), ALU.add))
            for t in range(TT):
                ins = nc.vector.max(best2[:, t], biased[:, t])
            step(ins)
            for t in range(TT):
                ins = nc.vector.max_index(r6_i[:, t], best2[:, t], biased[:, t])
            step(ins)
            step(nc.vector.tensor_copy(best2, r6_i[:, :, :]))
            for t in range(TT):
                ins = nc.vector.tensor_scalar(chosen1[:, t], iota6, best2[:, t, 0:1], None, ALU.is_equal)
            step(ins)
            for t in range(TT):
                ins = nc.vector.scalar_tensor_tensor(chosen1[:, t], iota6, best2[:, t, 1:2], chosen1[:, t],
                                                     ALU.is_equal, ALU.add)
            step(ins)
            step(nc.vector.tensor_tensor(chosen1, chosen1, score, ALU.mult))
            step(nc.vector.tensor_reduce(r6_s[:, :], chosen1, AX.X, ALU.add))
            step(nc.vector.tensor_scalar(r6_s[:, :], r6_s[:, :], 1e-20, None, ALU.add))
            step(nc.vector.reciprocal(r6_s[:, :], r6_s[:, :]))
            for t in range(TT):
                ins = nc.vector.tensor_scalar(weight[:, t], chosen1[:, t], r6_s[:, t:t + 1], None, ALU.mult)
            ins.then_inc(w6_ready, 1)
            dve.wait_ge(w6T_psum, 1)
            nc.vector.tensor_copy(w6T[0:MOE + 1, :], bank[2][0:MOE + 1, 0:T]).then_inc(w6T_ready, 1)
            dve.wait_ge(w6T_ready, 1)
            nc.vector.tensor_tensor(w6T[32:OWNERS, :], bank[2][0:MOE + 1, 0:T], w6T[0:MOE + 1, :].bitcast(F32),
                                    ALU.subtract).then_inc(w6T_ready, 1)
            for m in range(FT):
                n = min(P, FALL - m * P)
                dve.wait_ge(up6_psum, m + 1)
                dve.wait_ge(silu_ready, m + 1)
                step(nc.vector.tensor_tensor(h6[0:n, m, :], bank[5 + m % 2][0:n, 0:T], silu6[0:n, m % 2, :], ALU.mult))
                nc.vector.tensor_tensor(h6[0:n, m, :], bank[5 + m % 2][0:n, T:2 * T], h6[0:n, m, :], ALU.mult
                                        ).then_inc(h6_ready, 1)
            dve.wait_ge(y_psum, 6)
            for t in range(TT):
                ins = nc.vector.tensor_tensor(x_res[:, t], x_res[:, t], bank[(7, 0)[t]][:, 0:D], ALU.add)
            ins.then_inc(x_ready, 1)

        @block.gpsimd
        def _(pool):
            pool.wait_ge(q_split, 8)
            for s in range(2):
                own, other = slice(64 * s, 64 * s + 64), slice(64 * (1 - s), 64 * (1 - s) + 64)
                for half in (own, other):
                    nc.gpsimd.tensor_tensor(q_rest[half, :, s, :], qT[own, :, :], q_upper[own, :, s, :].bitcast(F32),
                                            ALU.subtract).then_inc(q_twice, 1)
            pool.wait_ge(x_ready, 1)
            nc.gpsimd.memset(part(region_a, 8192, 4096), 0.0).then_inc(k2_diag_zero, 1)
            pool.wait_ge(wsim_psum, 4)
            nc.gpsimd.memset(part(region_d, 0, 4096), 0.0).then_inc(fq_diag_zero, 1)
            pool.wait_ge(k_maxed, 1)
            nc.gpsimd.partition_all_reduce(k_stab[:, :], k_max[:, :], P, bass.bass_isa.ReduceOp.max
                                           ).then_inc(k_stab_ready, 1)
            pool.wait_ge(down_psum, ET // 2)
            nc.gpsimd.memset(ctxT_b[CD - P:CD - P + 1], 1.0).then_inc(ones4_set, 1)
            pool.wait_ge(moe_small_in, 64)
            nc.gpsimd.tensor_copy(owner6_r[0:OWNERS, :], owner6).then_inc(owner6_ready, 1)



def by_tile(m):
    return m.astype(np.float32).reshape(TT, P, T).transpose(1, 0, 2).reshape(P, -1)


def laid_out(i):
    f = {k: np.asarray(v) for k, v in i.items()}
    f["L0_attn_v_b"] = f["L0_attn_Wqkv_b"][2 * D:]
    wqk = np.zeros((D, 2 * LH, 32), np.float32)
    wqk[:, :, :16] = f["L0_attn_Wqkv_w"][:2 * D].T.reshape(D, 2 * LH, 16)
    bqk = np.zeros((2 * LH, 32), np.float32)
    bqk[:, :16] = f["L0_attn_Wqkv_b"][:2 * D].reshape(2 * LH, 16)
    proj, minus_half = np.zeros((4, 32, 4, 32), np.float32), np.zeros((4, 32, 4, 32), np.float32)
    for g in range(4):
        proj[g, :16, g, :LM] = f["L0_attn_proj"].T
        minus_half[g, :16, g, :LM] = -0.5
    query, key = np.arange(T)[:, None], np.arange(T)[None, :]
    window = (key <= query) & (key >= query - 128)
    mixT = ((key <= query) - 0.25 * window).T.astype(np.float32)
    a = {
        "x": f["x"].reshape(T, D),
        "ctxT": np.ascontiguousarray(f["ctx_768"][0].T),
        "mask": np.ascontiguousarray(f["mask_1x1xSxS2_bk0"].reshape(T, S2)).view(np.uint32),
        "columns": np.concatenate([f[n].reshape(-1, P).T for n in COLUMNS], axis=1),
        "rows": np.concatenate([f[n] for n in ROWS])[None],
        "Wq": f["L0_xattn_Wq"], "Wkv": f["L0_xattn_Wkv"], "Wo": f["L0_xattn_Wo"],
        "wqk2": wqk.reshape(D, -1), "wv2": np.ascontiguousarray(f["L0_attn_Wqkv_w"][2 * D:].T),
        "wo2": np.ascontiguousarray(f["L0_attn_out_w"].T), "qk_bias": np.ascontiguousarray(bqk.reshape(8, P).T),
        "proj": proj.reshape(P, P),
        "w_q": f["L0_ffn_w_q"], "keysT": np.ascontiguousarray(f["L0_ffn_keys"].transpose(3, 0, 2, 1).reshape(P, -1)),
        "downT": np.ascontiguousarray(f["L0_ffn_expert_down"].T), "up": f["L0_ffn_expert_up"],
        "ctx": f["ctx_768"][0], "wq4": f["L1_xattn_Wq"],
        "wk4T": np.concatenate([f["L1_xattn_Wk"].T, f["L1_xattn_bk"][:, None]], axis=1),
        "wv4": np.concatenate([f["L1_xattn_Wv"], f["L1_xattn_bv"][None]], axis=0),
        "wq5": f["L1_attn_wq"], "wk5": f["L1_attn_wk"], "wv5": f["L1_attn_wv"], "wo5": f["L1_attn_wo"],
        "wr6": f["L1_ffn_W_gate_router"], "ebias6": f["L1_ffn_expert_bias"],
        "wg6": np.concatenate([f["L1_ffn_Wg"].transpose(1, 0, 2).reshape(D, -1), f["L1_ffn_Wg_s"]], axis=1),
        "wu6": np.concatenate([f["L1_ffn_Wu"].transpose(1, 0, 2).reshape(D, -1), f["L1_ffn_Wu_s"]], axis=1),
        "wd6": np.concatenate([f["L1_ffn_Wd"].reshape(-1, D), f["L1_ffn_Wd_s"]], axis=0),
        "keep5": by_tile(key > query + 1), "fill5": by_tile(np.where(key > query + 1, 0, -1e9)),
        "owner6": np.where(np.arange(OWNERS)[:, None] < 32, np.arange(FALL)[None] // FF == np.arange(OWNERS)[:, None],
                           np.arange(FALL)[None] // FF == np.arange(OWNERS)[:, None] - 32).astype(np.float32),
        "iota": np.tile(np.arange(P, dtype=np.float32), (P, 1)),
        "minus_half": minus_half.reshape(P, P),
        "band": by_tile(np.where(window, 0, -10000.0)),
        "mixT": np.concatenate([mixT[:P], mixT[P:, P:]], axis=1),
        "ident": np.eye(P, dtype=np.float32),
        "block_numbers": np.stack([np.arange(NBLK) - NBLK, np.arange(NBLK) + 1]).astype(np.float32),
    }
    return a


def kernel(**inputs):
    import concourse.bacc as bacc
    from concourse.bass_utils import run_bass_kernel_spmd

    nc = bacc.Bacc("TRN2", target_bir_lowering=False, num_devices=1)
    arrays, aps = {}, {}
    for name, v in laid_out(inputs).items():
        arrays[f"in_{name}"] = v
        aps[name] = nc.dram_tensor(f"in_{name}", v.shape, mybir.dt.from_np(v.dtype), kind="ExternalInput").ap()
    out = nc.dram_tensor("out_0_dram", (T, D), F32, kind="ExternalOutput").ap()
    build(nc, aps, out)
    r = run_bass_kernel_spmd(nc, [arrays], core_ids=[0])
    return r.results[0]["out_0_dram"].reshape(1, T, D)
```
